# Optimizing a Trainium2 kernel written in Bass

```python
import numpy as np
import jax
import jax.numpy as jnp

def _softmax(x, axis=-1):
    return jax.nn.softmax(x, axis=axis)

def _gelu(x):
    return jax.nn.gelu(x, approximate=True)

def _silu(x):
    return jax.nn.silu(x)

def _sigmoid(x):
    return jax.nn.sigmoid(x)

def _layernorm(x, axis=-1, eps=1e-05):
    m = jnp.mean(x, axis=axis, keepdims=True)
    v = jnp.var(x, axis=axis, keepdims=True)
    return (x - m) / jnp.sqrt(v + eps)

def _scatter_add(tgt, idx, src, axis=0):
    return tgt.at[idx].add(src)

def _segment_sum(src, seg, n):
    return jax.ops.segment_sum(src, seg, n)
kernel_name = 'mk_early_fusion_d4_tok_img512_r4_d6ba3a'

def setup_inputs(seed: int=0):
    np.random.seed(seed)
    _w = jnp.asarray

    def _rec_inputs():
        import jax
        import jax.numpy as jnp
        _rk = jax.random.key(seed)
        x = -0.000392918 + 0.999932 * jax.random.normal(jax.random.fold_in(_rk, 1), (32, 1, 128, 128), jnp.float32)
        txt = 0.229487 + 0.681011 * jax.random.normal(jax.random.fold_in(_rk, 2), (32, 77, 128), jnp.float32)
        return (x, txt)
    x, txt = _rec_inputs()

    def _L0_tok_setup():
        import math
        import jax, jax.numpy as jnp
        import numpy as np
        PW = PH = 16
        EMB = 128
        HID = 128
        B, H, W = (64, 128, 128)
        L = H // PW * (W // PH)
        SIGMA_ZERO = 0.1

        def _f_noise(x):
            return jnp.sign(x) * jnp.sqrt(jnp.abs(x))

        def _noisy_linear(x, w, b, sw, sb, eps_in, eps_out):
            ei = _f_noise(eps_in)
            eo = _f_noise(eps_out)
            w_n = w + sw * (eo[:, None] * ei[None, :])
            b_n = b + sb * eo
            return x @ w_n.T + b_n

        def _unfold_patches(x):
            b = x.shape[0]
            p = x.reshape(b, H // PW, PW, W // PH, PH)
            p = p.transpose(0, 1, 3, 2, 4)
            return p.reshape(b, L, PW * PH)

        def _pos_encoding(x):
            pos = jnp.arange(L, dtype=jnp.float32)[:, None]
            div = jnp.exp(jnp.arange(0, EMB, 2, dtype=jnp.float32) * (-math.log(10000.0) / EMB))
            ang = pos * div
            pe = jnp.stack([jnp.sin(ang), jnp.cos(ang)], axis=-1).reshape(L, EMB)
            return x + pe[None, :, :]
        key = jax.random.key(seed)
        ks = jax.random.split(key, 12)
        in_f = PW * PH
        sig = SIGMA_ZERO / math.sqrt(in_f)
        bnd1 = 1.0 / math.sqrt(in_f)
        bnd3 = 1.0 / math.sqrt(HID)
        u = lambda k, shape, bnd: jax.random.uniform(k, shape, jnp.float32, -bnd, bnd)
        return {'inputs': jax.random.normal(ks[0], (B, 1, H, W), jnp.float32), 'W1_w': u(ks[1], (HID, in_f), bnd1), 'W1_b': u(ks[2], (HID,), bnd1), 'W1_sw': jnp.full((HID, in_f), sig, jnp.float32), 'W1_sb': jnp.full((HID,), sig, jnp.float32), 'W2_w': u(ks[3], (HID, in_f), bnd1), 'W2_b': u(ks[4], (HID,), bnd1), 'W2_sw': jnp.full((HID, in_f), sig, jnp.float32), 'W2_sb': jnp.full((HID,), sig, jnp.float32), 'W3_w': u(ks[5], (EMB, HID), bnd3), 'W3_b': u(ks[6], (EMB,), bnd3), 'eps_in1': jax.random.normal(ks[7], (in_f,), jnp.float32), 'eps_out1': jax.random.normal(ks[8], (HID,), jnp.float32), 'eps_in2': jax.random.normal(ks[9], (in_f,), jnp.float32), 'eps_out2': jax.random.normal(ks[10], (HID,), jnp.float32)}
    _L0_tok_all = _L0_tok_setup()
    _L0_tok_in = {k: v for k, v in _L0_tok_all.items() if k in ('W1_w', 'W1_b', 'W1_sw', 'W1_sb', 'W2_w', 'W2_b', 'W2_sw', 'W2_sb', 'W3_w', 'W3_b', 'eps_in1', 'eps_out1', 'eps_in2', 'eps_out2')}
    del _L0_tok_all

    def _L0_attn_setup():
        import jax, jax.numpy as jnp
        import numpy as np
        B, N, D, H = (2, 1024, 128, 8)
        HD = D // H
        key = jax.random.key(seed)
        k1, k2, k3, k4, k5 = jax.random.split(key, 5)
        s = D ** (-0.5)
        return {'x': jax.random.normal(k1, (B, N, D), dtype=jnp.float32), 'Wq': jax.random.normal(k2, (D, D), dtype=jnp.float32) * s, 'bq': jax.random.normal(k3, (D,), dtype=jnp.float32) * 0.01, 'Wk': jax.random.normal(k4, (D, D), dtype=jnp.float32) * s, 'bk': jax.random.normal(k5, (D,), dtype=jnp.float32) * 0.01}
    _L0_attn_all = _L0_attn_setup()
    _L0_attn_in = {k: v for k, v in _L0_attn_all.items() if k in ('Wq', 'bq', 'Wk', 'bk')}
    del _L0_attn_all

    def _L0_ffn_setup():
        import jax, jax.numpy as jnp
        import numpy as np
        NUM_EXPERTS = 8
        TOP_K = 2
        key = jax.random.key(seed)
        k0, k1, k2, k3, k4 = jax.random.split(key, 5)
        sl, bs, hs, ffn = (512, 2, 128, 512)
        T = sl * bs
        x = jax.random.normal(k0, (sl, bs, hs), jnp.float32)
        expert_weights = jax.random.uniform(k1, (T, TOP_K), jnp.float32)
        expert_indices = jax.random.randint(k2, (T, TOP_K), 0, NUM_EXPERTS)
        w1 = jax.random.normal(k3, (NUM_EXPERTS, hs, ffn), jnp.float32) * hs ** (-0.5)
        w2 = jax.random.normal(k4, (NUM_EXPERTS, ffn, hs), jnp.float32) * ffn ** (-0.5)
        return dict(x=x, expert_weights=expert_weights, expert_indices=expert_indices, w1=w1, w2=w2)
    _L0_ffn_all = _L0_ffn_setup()
    _L0_ffn_in = {k: v for k, v in _L0_ffn_all.items() if k in ('expert_weights', 'expert_indices', 'w1', 'w2')}
    del _L0_ffn_all

    def _L1_attn_setup():
        import jax, jax.numpy as jnp
        import numpy as np
        H = 8
        W = 64
        SHIFT = True
        DIM = 128
        SCALE = (DIM // H) ** (-0.5)
        key = jax.random.key(seed)
        k1, k2, k3, k4 = jax.random.split(key, 4)
        x = jax.random.normal(k1, (8, 1024, DIM), dtype=jnp.float32)
        w_qkv = jax.random.normal(k2, (3 * DIM, DIM), dtype=jnp.float32) * 0.02
        w_proj = jax.random.normal(k3, (DIM, DIM), dtype=jnp.float32) * 0.02
        b_proj = jax.random.normal(k4, (DIM,), dtype=jnp.float32) * 0.02
        return {'x': x, 'w_qkv': w_qkv, 'w_proj': w_proj, 'b_proj': b_proj}
    _L1_attn_all = _L1_attn_setup()
    _L1_attn_in = {k: v for k, v in _L1_attn_all.items() if k in ('w_qkv', 'w_proj', 'b_proj')}
    del _L1_attn_all

    def _L1_ffn_setup():
        import jax, jax.numpy as jnp
        import numpy as np
        LUT_SIZE = 1024
        TWO_PI = 2.0 * np.pi

        def _lut_tables():
            ang = jnp.arange(LUT_SIZE, dtype=jnp.float32) * (TWO_PI / LUT_SIZE)
            return (jnp.sin(ang), jnp.cos(ang))

        def _lookup_sin_cos(theta):
            sin_t, cos_t = _lut_tables()
            idx = jnp.mod(jnp.round(theta * (LUT_SIZE / TWO_PI)), LUT_SIZE).astype(jnp.int32)
            return (sin_t[idx], cos_t[idx])
        key = jax.random.key(seed)
        ks = jax.random.split(key, 5)
        B, S, D, N = (2, 128, 128, 64)
        x = jax.random.normal(ks[0], (B, S, D), dtype=jnp.float32)
        W = jax.random.normal(ks[1], (N, D), dtype=jnp.float32) * 0.02
        B_param = jnp.zeros((N, D), dtype=jnp.float32)
        attn_cos = jnp.ones((N, D), dtype=jnp.float32)
        attn_sin = jnp.ones((N, D), dtype=jnp.float32)
        bound = 0.5 * np.sqrt(6.0 / (N + D))
        proj_cos_w = jax.random.uniform(ks[2], (D, N), jnp.float32, -bound, bound)
        proj_sin_w = jax.random.uniform(ks[3], (D, N), jnp.float32, -bound, bound)
        return {'x': x, 'W': W, 'B_param': B_param, 'attn_cos': attn_cos, 'attn_sin': attn_sin, 'proj_cos_w': proj_cos_w, 'proj_sin_w': proj_sin_w}
    _L1_ffn_all = _L1_ffn_setup()
    _L1_ffn_in = {k: v for k, v in _L1_ffn_all.items() if k in ('W', 'B_param', 'attn_cos', 'attn_sin', 'proj_cos_w', 'proj_sin_w')}
    del _L1_ffn_all

    def _L2_attn_setup():
        import jax, jax.numpy as jnp
        import numpy as np
        EPS = 1e-12

        def _l2norm(x):
            n = jnp.sqrt(jnp.sum(x * x, axis=-1, keepdims=True))
            return x / jnp.maximum(n, EPS)
        key = jax.random.key(seed)
        ks = jax.random.split(key, 8)
        B, T, V = (4, 512, 128)
        C, H, NB = (128, 4, 64)
        return {'x': jax.random.normal(ks[0], (B, T, V), dtype=jnp.float32), 'basis': jax.random.normal(ks[1], (V, 2 * NB), dtype=jnp.float32), 'shared_q_w': jax.random.normal(ks[2], (V, C), dtype=jnp.float32) * 0.02, 'shared_k_w': jax.random.normal(ks[3], (V, C), dtype=jnp.float32) * 0.02, 'v_coeffs': jax.random.normal(ks[4], (C, 2 * NB), dtype=jnp.float32) * 0.02, 'o_coeffs': jax.random.normal(ks[5], (C, 2 * NB), dtype=jnp.float32) * 0.02, 'decay_logits': jnp.linspace(1.0, 5.0, H, dtype=jnp.float32), 'out_scale': jnp.float32(0.1)}
    _L2_attn_all = _L2_attn_setup()
    _L2_attn_in = {k: v for k, v in _L2_attn_all.items() if k in ('basis', 'shared_q_w', 'shared_k_w', 'v_coeffs', 'o_coeffs', 'decay_logits', 'out_scale')}
    del _L2_attn_all

    def _L2_ffn_setup():
        import jax, jax.numpy as jnp
        import numpy as np
        from jax import lax
        N, M, DIM, HEADS, TOPK = (4, 512, 128, 8, 16)

        def _split_heads(t, h):
            n, m, c = t.shape
            return t.reshape(n, m, h, c // h).transpose(0, 2, 1, 3).reshape(n * h, m, c // h)
        key = jax.random.key(seed)
        ks = jax.random.split(key, 7)
        f = lambda k, s, sc=1.0: jax.random.normal(k, s, dtype=jnp.float32) * sc
        return {'x': f(ks[0], (N, M, DIM)), 'pos_w': f(ks[1], (DIM, 1, 3), 0.1), 'pos_b': f(ks[2], (DIM,), 0.02), 'qkv_w': f(ks[3], (3 * DIM, DIM), 0.02), 'qkv_b': f(ks[4], (3 * DIM,), 0.02), 'wo_w': f(ks[5], (DIM, DIM), 0.02), 'wo_b': f(ks[6], (DIM,), 0.02)}
    _L2_ffn_all = _L2_ffn_setup()
    _L2_ffn_in = {k: v for k, v in _L2_ffn_all.items() if k in ('pos_w', 'pos_b', 'qkv_w', 'qkv_b', 'wo_w', 'wo_b')}
    del _L2_ffn_all

    def _L3_attn_setup():
        import jax, jax.numpy as jnp
        import numpy as np
        DIM = 128
        HEADS = 8
        DIM_HEAD = 64
        INNER = HEADS * DIM_HEAD
        key = jax.random.key(seed)
        kx, kq, kk, kv, ko = jax.random.split(key, 5)
        x = jax.random.normal(kx, (2, 1024, DIM), dtype=jnp.float32)
        lim = float(np.sqrt(6.0 / (DIM + INNER)))
        Wq = jax.random.uniform(kq, (INNER, DIM), minval=-lim, maxval=lim, dtype=jnp.float32)
        Wk = jax.random.uniform(kk, (INNER, DIM), minval=-lim, maxval=lim, dtype=jnp.float32)
        Wv = jax.random.uniform(kv, (INNER, DIM), minval=-lim, maxval=lim, dtype=jnp.float32) * 0.67
        lim_o = float(np.sqrt(6.0 / (INNER + DIM)))
        Wo = jax.random.uniform(ko, (DIM, INNER), minval=-lim_o, maxval=lim_o, dtype=jnp.float32) * 0.67
        return {'x': x, 'Wq': Wq, 'Wk': Wk, 'Wv': Wv, 'Wo': Wo}
    _L3_attn_all = _L3_attn_setup()
    _L3_attn_in = {k: v for k, v in _L3_attn_all.items() if k in ('Wq', 'Wk', 'Wv', 'Wo')}
    del _L3_attn_all

    def _L3_ffn_setup():
        import jax, jax.numpy as jnp
        import numpy as np
        B, S, D, E, O = (256, 64, 128, 16, 128)
        key = jax.random.key(seed)
        k_x, k_wg, k_bg, k_we, k_be = jax.random.split(key, 5)
        scale_g = 1.0 / np.sqrt(D)
        scale_e = 1.0 / np.sqrt(D)
        return {'x': jax.random.normal(k_x, (B, S, D), dtype=jnp.float32), 'Wg': jax.random.uniform(k_wg, (D, E), jnp.float32, -scale_g, scale_g), 'bg': jax.random.uniform(k_bg, (E,), jnp.float32, -scale_g, scale_g), 'We': jax.random.uniform(k_we, (E, D, O), jnp.float32, -scale_e, scale_e), 'be': jax.random.uniform(k_be, (E, O), jnp.float32, -scale_e, scale_e)}
    _L3_ffn_all = _L3_ffn_setup()
    _L3_ffn_in = {k: v for k, v in _L3_ffn_all.items() if k in ('Wg', 'bg', 'We', 'be')}
    del _L3_ffn_all
    return {'x': x, 'txt': txt, 'L0_tok_W1_w': _L0_tok_in['W1_w'], 'L0_tok_W1_b': _L0_tok_in['W1_b'], 'L0_tok_W1_sw': _L0_tok_in['W1_sw'], 'L0_tok_W1_sb': _L0_tok_in['W1_sb'], 'L0_tok_W2_w': _L0_tok_in['W2_w'], 'L0_tok_W2_b': _L0_tok_in['W2_b'], 'L0_tok_W2_sw': _L0_tok_in['W2_sw'], 'L0_tok_W2_sb': _L0_tok_in['W2_sb'], 'L0_tok_W3_w': _L0_tok_in['W3_w'], 'L0_tok_W3_b': _L0_tok_in['W3_b'], 'L0_tok_eps_in1': _L0_tok_in['eps_in1'], 'L0_tok_eps_out1': _L0_tok_in['eps_out1'], 'L0_tok_eps_in2': _L0_tok_in['eps_in2'], 'L0_tok_eps_out2': _L0_tok_in['eps_out2'], 'L0_attn_Wq': _L0_attn_in['Wq'], 'L0_attn_bq': _L0_attn_in['bq'], 'L0_attn_Wk': _L0_attn_in['Wk'], 'L0_attn_bk': _L0_attn_in['bk'], 'L0_ffn_expert_weights': _L0_ffn_in['expert_weights'], 'L0_ffn_expert_indices': _L0_ffn_in['expert_indices'], 'L0_ffn_w1': _L0_ffn_in['w1'], 'L0_ffn_w2': _L0_ffn_in['w2'], 'L1_attn_w_qkv': _L1_attn_in['w_qkv'], 'L1_attn_w_proj': _L1_attn_in['w_proj'], 'L1_attn_b_proj': _L1_attn_in['b_proj'], 'L1_ffn_W': _L1_ffn_in['W'], 'L1_ffn_B_param': _L1_ffn_in['B_param'], 'L1_ffn_attn_cos': _L1_ffn_in['attn_cos'], 'L1_ffn_attn_sin': _L1_ffn_in['attn_sin'], 'L1_ffn_proj_cos_w': _L1_ffn_in['proj_cos_w'], 'L1_ffn_proj_sin_w': _L1_ffn_in['proj_sin_w'], 'L2_attn_basis': _L2_attn_in['basis'], 'L2_attn_shared_q_w': _L2_attn_in['shared_q_w'], 'L2_attn_shared_k_w': _L2_attn_in['shared_k_w'], 'L2_attn_v_coeffs': _L2_attn_in['v_coeffs'], 'L2_attn_o_coeffs': _L2_attn_in['o_coeffs'], 'L2_attn_decay_logits': _L2_attn_in['decay_logits'], 'L2_attn_out_scale': _L2_attn_in['out_scale'], 'L2_ffn_pos_w': _L2_ffn_in['pos_w'], 'L2_ffn_pos_b': _L2_ffn_in['pos_b'], 'L2_ffn_qkv_w': _L2_ffn_in['qkv_w'], 'L2_ffn_qkv_b': _L2_ffn_in['qkv_b'], 'L2_ffn_wo_w': _L2_ffn_in['wo_w'], 'L2_ffn_wo_b': _L2_ffn_in['wo_b'], 'L3_attn_Wq': _L3_attn_in['Wq'], 'L3_attn_Wk': _L3_attn_in['Wk'], 'L3_attn_Wv': _L3_attn_in['Wv'], 'L3_attn_Wo': _L3_attn_in['Wo'], 'L3_ffn_Wg': _L3_ffn_in['Wg'], 'L3_ffn_bg': _L3_ffn_in['bg'], 'L3_ffn_We': _L3_ffn_in['We'], 'L3_ffn_be': _L3_ffn_in['be']}

def reference(x, txt, L0_tok_W1_w, L0_tok_W1_b, L0_tok_W1_sw, L0_tok_W1_sb, L0_tok_W2_w, L0_tok_W2_b, L0_tok_W2_sw, L0_tok_W2_sb, L0_tok_W3_w, L0_tok_W3_b, L0_tok_eps_in1, L0_tok_eps_out1, L0_tok_eps_in2, L0_tok_eps_out2, L0_attn_Wq, L0_attn_bq, L0_attn_Wk, L0_attn_bk, L0_ffn_expert_weights, L0_ffn_expert_indices, L0_ffn_w1, L0_ffn_w2, L1_attn_w_qkv, L1_attn_w_proj, L1_attn_b_proj, L1_ffn_W, L1_ffn_B_param, L1_ffn_attn_cos, L1_ffn_attn_sin, L1_ffn_proj_cos_w, L1_ffn_proj_sin_w, L2_attn_basis, L2_attn_shared_q_w, L2_attn_shared_k_w, L2_attn_v_coeffs, L2_attn_o_coeffs, L2_attn_decay_logits, L2_attn_out_scale, L2_ffn_pos_w, L2_ffn_pos_b, L2_ffn_qkv_w, L2_ffn_qkv_b, L2_ffn_wo_w, L2_ffn_wo_b, L3_attn_Wq, L3_attn_Wk, L3_attn_Wv, L3_attn_Wo, L3_ffn_Wg, L3_ffn_bg, L3_ffn_We, L3_ffn_be):
    import jax
    import jax.numpy as jnp

    def _L0_tok_ref(inputs, W1_w, W1_b, W1_sw, W1_sb, W2_w, W2_b, W2_sw, W2_sb, W3_w, W3_b, eps_in1, eps_out1, eps_in2, eps_out2):
        import math
        import jax, jax.numpy as jnp
        import numpy as np
        PW = PH = 16
        EMB = 128
        HID = 128
        B, H, W = (64, 128, 128)
        L = H // PW * (W // PH)
        SIGMA_ZERO = 0.1

        def _f_noise(x):
            return jnp.sign(x) * jnp.sqrt(jnp.abs(x))

        def _noisy_linear(x, w, b, sw, sb, eps_in, eps_out):
            ei = _f_noise(eps_in)
            eo = _f_noise(eps_out)
            w_n = w + sw * (eo[:, None] * ei[None, :])
            b_n = b + sb * eo
            return x @ w_n.T + b_n

        def _unfold_patches(x):
            b = x.shape[0]
            p = x.reshape(b, H // PW, PW, W // PH, PH)
            p = p.transpose(0, 1, 3, 2, 4)
            return p.reshape(b, L, PW * PH)

        def _pos_encoding(x):
            pos = jnp.arange(L, dtype=jnp.float32)[:, None]
            div = jnp.exp(jnp.arange(0, EMB, 2, dtype=jnp.float32) * (-math.log(10000.0) / EMB))
            ang = pos * div
            pe = jnp.stack([jnp.sin(ang), jnp.cos(ang)], axis=-1).reshape(L, EMB)
            return x + pe[None, :, :]
        x = _unfold_patches(inputs)
        g = _noisy_linear(x, W1_w, W1_b, W1_sw, W1_sb, eps_in1, eps_out1)
        x_gate = g * jnp.tanh(jax.nn.softplus(g))
        x_inner = _noisy_linear(x, W2_w, W2_b, W2_sw, W2_sb, eps_in2, eps_out2)
        x = x_gate * x_inner
        x = x @ W3_w.T + W3_b
        return _pos_encoding(x)

    def _L0_attn_ref(x, Wq, bq, Wk, bk):
        import jax, jax.numpy as jnp
        import numpy as np
        B, N, D, H = (2, 1024, 128, 8)
        HD = D // H
        b, n, d = x.shape
        q = (jnp.einsum('bnd,ed->bne', x, Wq) + bq).reshape(b, n, H, HD).transpose(0, 2, 1, 3)
        k = (jnp.einsum('bnd,ed->bne', x, Wk) + bk).reshape(b, n, H, HD).transpose(0, 2, 1, 3)
        v = k
        scale = d ** (-0.5)
        attn = jnp.einsum('bhqe,bhke->bhqk', q, k) * scale
        attn = jax.nn.softmax(attn, axis=-1)
        out = jnp.einsum('bhqk,bhke->bhqe', attn, v)
        return out.transpose(0, 2, 1, 3).reshape(b, n, d)

    def _L0_ffn_ref(x, expert_weights, expert_indices, w1, w2):
        import jax, jax.numpy as jnp
        import numpy as np
        NUM_EXPERTS = 8
        TOP_K = 2
        'Dropless MoE: sort assignments by expert, gather tokens, grouped MLP,\n            scatter-combine with top-k router weights (megablocks gather/scatter semantics).'
        in_shape = x.shape
        hs = in_shape[-1]
        x_flat = x.reshape(-1, hs)
        T = x_flat.shape[0]
        flat_ids = expert_indices.reshape(-1)
        order = jnp.argsort(flat_ids)
        bin_ids = flat_ids[order]
        token_ids = order // TOP_K
        xg = x_flat[token_ids]
        y = jnp.zeros_like(xg)
        for e in range(NUM_EXPERTS):
            h = jax.nn.gelu(xg @ w1[e], approximate=False)
            y = jnp.where((bin_ids == e)[:, None], h @ w2[e], y)
        w = expert_weights.reshape(-1)[order][:, None]
        out = jnp.zeros((T, hs), x.dtype).at[token_ids].add(w * y)
        return out.reshape(in_shape)

    def _L1_attn_ref(x, w_qkv, w_proj, b_proj):
        import jax, jax.numpy as jnp
        import numpy as np
        H = 8
        W = 64
        SHIFT = True
        DIM = 128
        SCALE = (DIM // H) ** (-0.5)
        B, N, C = x.shape
        if SHIFT:
            x = jnp.roll(x, -W // 2, axis=1)
        pad = (W - N % W) % W
        if pad:
            x = jnp.pad(x, ((0, 0), (0, pad), (0, 0)))
        nw = x.shape[1] // W
        xw = x.reshape(B * nw, W, C)
        qkv = xw @ w_qkv.T
        qkv = qkv.reshape(B * nw, W, 3, H, C // H)
        q, k, v = (qkv[:, :, 0], qkv[:, :, 1], qkv[:, :, 2])
        attn = jnp.einsum('bwhd,bwgd->bwhg', q, k) * SCALE
        attn = jax.nn.softmax(attn, axis=-1)
        out = jnp.einsum('bwhg,bwgd->bwhd', attn, v)
        out = out.transpose(0, 2, 1, 3).reshape(B * nw, W, C)
        out = out @ w_proj.T + b_proj
        out = out.reshape(B, nw * W, C)[:, :N]
        if SHIFT:
            out = jnp.roll(out, W // 2, axis=1)
        return out

    def _L1_ffn_ref(x, W, B_param, attn_cos, attn_sin, proj_cos_w, proj_sin_w):
        import jax, jax.numpy as jnp
        import numpy as np
        LUT_SIZE = 1024
        TWO_PI = 2.0 * np.pi

        def _lut_tables():
            ang = jnp.arange(LUT_SIZE, dtype=jnp.float32) * (TWO_PI / LUT_SIZE)
            return (jnp.sin(ang), jnp.cos(ang))

        def _lookup_sin_cos(theta):
            sin_t, cos_t = _lut_tables()
            idx = jnp.mod(jnp.round(theta * (LUT_SIZE / TWO_PI)), LUT_SIZE).astype(jnp.int32)
            return (sin_t[idx], cos_t[idx])
        wavelength = 1.0 + jnp.abs(W)
        theta = x[..., None, :] / wavelength + B_param
        sin_theta, cos_theta = _lookup_sin_cos(theta)
        cos_sum = jnp.sum(cos_theta * attn_cos, axis=-1)
        sin_sum = jnp.sum(sin_theta * attn_sin, axis=-1)
        out = jnp.einsum('bsn,dn->bsd', cos_sum, proj_cos_w) + jnp.einsum('bsn,dn->bsd', sin_sum, proj_sin_w)
        return jax.nn.silu(out)

    def _L2_attn_ref(x, basis, shared_q_w, shared_k_w, v_coeffs, o_coeffs, decay_logits, out_scale):
        import jax, jax.numpy as jnp
        import numpy as np
        EPS = 1e-12

        def _l2norm(x):
            n = jnp.sqrt(jnp.sum(x * x, axis=-1, keepdims=True))
            return x / jnp.maximum(n, EPS)
        B, T, V = x.shape
        H = decay_logits.shape[0]
        C = shared_q_w.shape[1]
        D = C // H
        v_w = basis @ v_coeffs.T
        o_w = basis @ o_coeffs.T
        q = _l2norm(x @ shared_q_w)
        k = _l2norm(x @ shared_k_w)
        v = x @ v_w
        q = q.reshape(B, T, H, D).transpose(0, 2, 1, 3)
        k = k.reshape(B, T, H, D).transpose(0, 2, 1, 3)
        v = v.reshape(B, T, H, D).transpose(0, 2, 1, 3)
        scores = jnp.einsum('bhqd,bhkd->bhqk', q, k)
        decay = jax.nn.sigmoid(decay_logits)
        pos = jnp.arange(T)
        diff = pos[None, :] - pos[:, None]
        mask = (diff > 0).astype(scores.dtype)
        expo = jnp.clip(diff.astype(jnp.float32) - 1.0, 0.0, None)
        decay_w = decay[:, None, None] ** expo[None] * mask[None]
        scores = scores * decay_w[None].astype(scores.dtype)
        retrieved = jnp.einsum('bhqk,bhkd->bhqd', scores, v)
        retrieved = retrieved.transpose(0, 2, 1, 3).reshape(B, T, C)
        return retrieved @ o_w.T * out_scale

    def _L2_ffn_ref(x, pos_w, pos_b, qkv_w, qkv_b, wo_w, wo_b):
        import jax, jax.numpy as jnp
        import numpy as np
        from jax import lax
        N, M, DIM, HEADS, TOPK = (4, 512, 128, 8, 16)

        def _split_heads(t, h):
            n, m, c = t.shape
            return t.reshape(n, m, h, c // h).transpose(0, 2, 1, 3).reshape(n * h, m, c // h)
        n, m, c = x.shape
        h = HEADS
        scale = c ** (-0.5)
        pos = lax.conv_general_dilated(x.transpose(0, 2, 1), pos_w, window_strides=(1,), padding=[(1, 1)], feature_group_count=c, dimension_numbers=('NCH', 'OIH', 'NCH'))
        x = x + (pos + pos_b[None, :, None]).transpose(0, 2, 1)
        qkv = x @ qkv_w.T + qkv_b
        q, k, v = jnp.split(qkv, [c, 2 * c], axis=-1)
        q = _split_heads(q, h)
        k = _split_heads(k, h)
        v = _split_heads(v, h)
        qd = lax.stop_gradient(q)
        kd = lax.stop_gradient(k)
        logits = jnp.einsum('bmd,bpd->bmp', qd * scale, kd)
        _, idx = lax.top_k(logits, TOPK)
        gather = jax.vmap(lambda t, i: t[i])
        k_sel = gather(k, idx)
        v_sel = gather(v, idx)
        attn = jax.nn.softmax(jnp.einsum('bmd,bmkd->bmk', q * scale, k_sel), axis=-1)
        out = jnp.einsum('bmk,bmkd->bmd', attn, v_sel)
        d = c // h
        out = out.reshape(n, h, m, d).transpose(0, 2, 1, 3).reshape(n, m, c)
        return out @ wo_w.T + wo_b

    def _L3_attn_ref(x, Wq, Wk, Wv, Wo):
        import jax, jax.numpy as jnp
        import numpy as np
        DIM = 128
        HEADS = 8
        DIM_HEAD = 64
        INNER = HEADS * DIM_HEAD
        scale = DIM_HEAD ** (-0.5)
        b, n, _ = x.shape

        def proj(W):
            t = jnp.einsum('bnc,ec->bne', x, W)
            return t.reshape(b, n, HEADS, DIM_HEAD).transpose(0, 2, 1, 3)
        q, k, v = (proj(Wq), proj(Wk), proj(Wv))
        dots = jnp.einsum('bhqd,bhkd->bhqk', q, k) * scale
        attn = jax.nn.softmax(dots, axis=-1)
        out = jnp.einsum('bhqk,bhkd->bhqd', attn, v)
        out = out.transpose(0, 2, 1, 3).reshape(b, n, INNER)
        out = jnp.einsum('bne,ce->bnc', out, Wo)
        return out + x

    def _L3_ffn_ref(x, Wg, bg, We, be):
        import jax, jax.numpy as jnp
        import numpy as np
        B, S, D, E, O = (256, 64, 128, 16, 128)
        scores = jax.nn.softmax(jnp.mean(x, axis=1) @ Wg + bg, axis=-1)
        idx = jnp.argmax(scores, axis=-1)
        gate = jnp.take_along_axis(scores, idx[:, None], axis=-1)
        W_sel = We[idx]
        b_sel = be[idx]
        y = jnp.einsum('bsd,bdo->bso', x, W_sel) + b_sel[:, None, :]
        return gate[:, :, None] * y
    h = _L0_tok_ref(x, L0_tok_W1_w, L0_tok_W1_b, L0_tok_W1_sw, L0_tok_W1_sb, L0_tok_W2_w, L0_tok_W2_b, L0_tok_W2_sw, L0_tok_W2_sb, L0_tok_W3_w, L0_tok_W3_b, L0_tok_eps_in1, L0_tok_eps_out1, L0_tok_eps_in2, L0_tok_eps_out2)
    h = jnp.concatenate([h, txt], axis=1)
    h = h + _L0_attn_ref(_layernorm(h, axis=-1), L0_attn_Wq, L0_attn_bq, L0_attn_Wk, L0_attn_bk)
    h = h + _L0_ffn_ref(_layernorm(h, axis=-1), L0_ffn_expert_weights, L0_ffn_expert_indices, L0_ffn_w1, L0_ffn_w2)
    h = h + _L1_attn_ref(_layernorm(h, axis=-1), L1_attn_w_qkv, L1_attn_w_proj, L1_attn_b_proj)
    h = h + _L1_ffn_ref(_layernorm(h, axis=-1), L1_ffn_W, L1_ffn_B_param, L1_ffn_attn_cos, L1_ffn_attn_sin, L1_ffn_proj_cos_w, L1_ffn_proj_sin_w)
    h = h + _L2_attn_ref(_layernorm(h, axis=-1), L2_attn_basis, L2_attn_shared_q_w, L2_attn_shared_k_w, L2_attn_v_coeffs, L2_attn_o_coeffs, L2_attn_decay_logits, L2_attn_out_scale)
    h = h + _L2_ffn_ref(_layernorm(h, axis=-1), L2_ffn_pos_w, L2_ffn_pos_b, L2_ffn_qkv_w, L2_ffn_qkv_b, L2_ffn_wo_w, L2_ffn_wo_b)
    h = h + _L3_attn_ref(_layernorm(h, axis=-1), L3_attn_Wq, L3_attn_Wk, L3_attn_Wv, L3_attn_Wo)
    h = h + _L3_ffn_ref(_layernorm(h, axis=-1), L3_ffn_Wg, L3_ffn_bg, L3_ffn_We, L3_ffn_be)
    return h

_drawn_inputs = setup_inputs


def setup_inputs(seed=0):
    import zlib

    import numpy as np

    out = dict(_drawn_inputs(seed))
    spreads = {'L0_tok_W1_sw': (0.0062500000931322575, 0.6),
     'L0_tok_W1_sb': (0.0062500000931322575, 0.6),
     'L0_tok_W2_sw': (0.0062500000931322575, 0.6),
     'L0_tok_W2_sb': (0.0062500000931322575, 0.6),
     'L1_ffn_B_param': (0.0, 2.0),
     'L1_ffn_attn_cos': (1.0, 0.6),
     'L1_ffn_attn_sin': (1.0, 0.6)}
    factors = {'x': 5.172,
     'L0_tok_W1_w': 5.426,
     'L0_tok_W1_b': 26.837,
     'L0_tok_W2_w': 5.183,
     'L0_tok_W2_b': 25.953,
     'L0_tok_W3_w': 5.095,
     'L0_tok_W3_b': 64.0,
     'L0_tok_eps_in1': 8.0,
     'L0_tok_eps_out1': 8.0,
     'L0_tok_eps_in2': 8.0,
     'L0_tok_eps_out2': 8.0,
     'L0_attn_Wq': 38.896,
     'L0_attn_bq': 64.0,
     'L0_attn_bk': 64.0,
     'L0_ffn_expert_weights': 33.384,
     'L0_ffn_w1': 18.965,
     'L1_attn_w_qkv': 54.323,
     'L1_attn_w_proj': 54.365,
     'L1_attn_b_proj': 64.0,
     'L1_ffn_W': 64.0,
     'L2_ffn_pos_w': 42.752,
     'L2_ffn_pos_b': 64.0,
     'L2_ffn_qkv_w': 41.191,
     'L2_ffn_qkv_b': 64.0,
     'L2_ffn_wo_w': 41.431,
     'L2_ffn_wo_b': 200.0,
     'L3_attn_Wq': 52.689,
     'L3_attn_Wk': 53.628,
     'L3_attn_Wv': 21.652,
     'L3_attn_Wo': 18.787,
     'L3_ffn_Wg': 200.0,
     'L3_ffn_bg': 200.0,
     'L3_ffn_We': 200.0,
     'L3_ffn_be': 200.0,
     'txt': 6.136,
     'L0_attn_Wk': 8.0,
     'L0_ffn_w2': 5.908,
     'L1_ffn_proj_sin_w': 8.0,
     'L2_attn_basis': 8.0,
     'L2_attn_shared_q_w': 8.0,
     'L2_attn_shared_k_w': 8.0,
     'L2_attn_v_coeffs': 8.0,
     'L2_attn_o_coeffs': 8.0,
     'L2_attn_decay_logits': 8.0}
    for name, (base, spread) in spreads.items():
        noise = np.random.default_rng([zlib.crc32(name.encode()), seed]).standard_normal(out[name].shape)
        drawn = base * np.exp(spread * noise) if base else spread * noise
        out[name] = jnp.asarray(drawn.astype(out[name].dtype))
    for name, factor in factors.items():
        out[name] = (out[name] * factor).astype(out[name].dtype)
    return out
```

```python
import math
from contextlib import ExitStack

import concourse.bass as bass
from concourse import mybir

F32 = mybir.dt.float32
I32 = mybir.dt.int32
U32 = mybir.dt.uint32
I16 = mybir.dt.int16
ALU = mybir.AluOpType
ACT = mybir.ActivationFunctionType
AX = mybir.AxisListType

P = 128
BATCH = 32
PATCHES = 64
TEXT = 77
SEQ = PATCHES + TEXT
TOK = BATCH * SEQ
HALF = 71
PADSEQ = 2 * HALF
CHUNK = 512
TOKPAD = -(-TOK // CHUNK) * CHUNK
EPS = 1e-5
SLOTS = 2
GONE = -3.0e38


def made(n, slots=SLOTS):
    return n + (1 + slots)


def freed(n):
    return n + 1


class Core:
    pass


def ds(start, size):
    return bass.ds(start, size)


def tokens_of_patches(nc, core, dram):
    with ExitStack() as ctx:
        sb = lambda name, shape, dt=F32: ctx.enter_context(nc.sbuf_tensor("tok_" + name, shape, dt))
        ps = lambda name, shape: ctx.enter_context(nc.psum_tensor("tok_" + name, shape, F32))
        sem = lambda name: core.keep(nc.semaphore("tok_" + name))
        GB = 8
        CH = BATCH // GB
        w = sb("w", [P, 2, 2, P])
        sw = sb("sw", [P, 2, 2, P])
        eo_row = sb("eo_row", [P, 2, P])
        eps_col = sb("eps_col", [P, 2, 3])
        bias = sb("bias", [P, 2, 2])
        b3 = sb("b3", [P, 1])
        w3 = sb("w3", [P, P])
        pe_tab = sb("pe", [P, PATCHES])
        x = [sb(f"x{s}", [P, 2, CHUNK]) for s in range(2)]
        t_row = sb("t_row", [P, 2, P])
        t_col = sb("t_col", [P, 2, 3])
        s_row = sb("s_row", [P, 2, P])
        s_col = sb("s_col", [P, 2, 3])
        noise = sb("noise", [P, 2, 2, P])
        bn = sb("bn", [P, 2])
        gate = [sb(f"gate{s}", [P, CHUNK]) for s in range(2)]
        inner = [sb(f"inner{s}", [P, CHUNK]) for s in range(2)]
        u = [sb(f"u{s}", [P, CHUNK]) for s in range(2)]
        v = [sb(f"v{s}", [P, CHUNK]) for s in range(2)]
        g_ps = [ps(f"g{s}", [P, CHUNK]) for s in range(2)]
        i_ps = [ps(f"i{s}", [P, CHUNK]) for s in range(2)]
        y_ps = [ps(f"y{s}", [P, CHUNK]) for s in range(2)]
        small_in = sem("small_in")
        x_in = [sem(f"x_in{s}") for s in range(2)]
        text_in = sem("text_in")
        root = sem("root")
        prep = sem("prep")
        prepared = sem("prepared")
        gate_ready = sem("gate_ready")
        proj = sem("proj")
        act_done = sem("act_done")
        dve = sem("dve")
        mixed = sem("mixed")
        y_ready = sem("y_ready")
        SMALL = 13

        with nc.Block() as block:
            @block.sync
            def _(sp):
                for l in range(2):
                    sp.dma_start(w[:, l], dram[f"w{l}"]).then_inc(small_in, 16)
                    sp.dma_start(sw[:, l], dram[f"sw{l}"]).then_inc(small_in, 16)
                    sp.dma_start(eo_row[:, l], dram[f"eo{l}"].partition_broadcast(P)).then_inc(small_in, 16)
                    sp.dma_start(eps_col[:, l], dram[f"eps{l}"]).then_inc(small_in, 16)
                    sp.dma_start(bias[:, l], dram[f"bias{l}"]).then_inc(small_in, 16)
                sp.dma_start(w3[:], dram["w3"]).then_inc(small_in, 16)
                sp.dma_start(b3[:], dram["b3"]).then_inc(small_in, 16)
                sp.dma_start(pe_tab[:], dram["pe"]).then_inc(small_in, 16)
                for c in range(CH):
                    if c >= 2:
                        sp.wait_ge(proj, c - 1)
                    sp.dma_start(x[c % 2][:], dram["x"][:, :, c * CHUNK:(c + 1) * CHUNK]).then_inc(x_in[c % 2], 16)

            @block.gpsimd
            def _(pool):
                pool.dma_start(core.h[:, 0:TOK].rearrange("p (b n) -> p b n", n=SEQ)[:, :, PATCHES:SEQ],
                               dram["txt"]).then_inc(text_in, 16)
                pool.wait_ge(text_in, 16)
                pool.wait_ge(core.weights_in, 16 * core.n_weights)

            @block.scalar
            def _(act):
                for name in core.weight_names:
                    act.dma_start(core.w[name][:], dram[name]).then_inc(core.weights_in, 16)
                act.wait_ge(prep, 2)
                act.activation(s_row[:], t_row[:], ACT.Sqrt).then_inc(root, 1)
                act.activation(s_col[:], t_col[:], ACT.Sqrt).then_inc(root, 1)
                act.wait_ge(prepared, 1)
                for c in range(CH):
                    s = c % 2
                    act.wait_ge(proj, c + 1)
                    if c >= 2:
                        act.wait_ge(mixed, c - 1)
                    act.activation(gate[s][:], g_ps[s][:], ACT.Identity, bias=bn[:, 0:1]).then_inc(gate_ready, 1)
                    act.activation(inner[s][:], i_ps[s][:], ACT.Identity, bias=bn[:, 1:2]).then_inc(act_done, 1)
                    act.wait_ge(dve, 5 * c + 1)
                    act.activation(u[s][:], v[s][:], ACT.Exp).then_inc(act_done, 1)

            @block.tensor
            def _(pe):
                pe.wait_ge(prepared, 1)
                for c in range(CH):
                    s = c % 2
                    pe.wait_ge(x_in[s], 16 * (c // 2 + 1))
                    if c >= 2:
                        pe.wait_ge(act_done, 2 * (c - 1))
                    for l, out in ((0, g_ps[s]), (1, i_ps[s])):
                        for k in range(2):
                            mm = pe.matmul(out[:], noise[:, l, k], x[s][:, k], start=(k == 0), stop=(k == 1))
                    mm.then_inc(proj, 1)
                    if c >= 2:
                        pe.wait_ge(y_ready, 2 * (c - 1))
                    pe.wait_ge(mixed, c + 1)
                    pe.matmul(y_ps[s][:], w3[:], gate[s][:], start=True, stop=True).then_inc(y_ready, 1)

            @block.vector
            def _(ve):
                ve.wait_ge(small_in, 16 * SMALL)
                ve.scalar_tensor_tensor(t_row[:], eo_row[:], -1.0, eo_row[:], ALU.mult, ALU.max).then_inc(prep, 1)
                ve.scalar_tensor_tensor(t_col[:], eps_col[:], -1.0, eps_col[:], ALU.mult, ALU.max).then_inc(prep, 1)
                ve.wait_ge(root, 2)
                ve.tensor_scalar(t_row[:], eo_row[:], 0.0, 2.0, ALU.is_ge, ALU.mult).then_inc(prep, 1)
                ve.tensor_scalar(t_col[:], eps_col[:], 0.0, 2.0, ALU.is_ge, ALU.mult).then_inc(prep, 1)
                ve.wait_ge(prep, 4)
                ve.scalar_tensor_tensor(s_row[:], t_row[:], -1.0, s_row[:], ALU.add, ALU.mult).then_inc(prep, 1)
                ve.scalar_tensor_tensor(s_col[:], t_col[:], -1.0, s_col[:], ALU.add, ALU.mult).then_inc(prep, 1)
                ve.wait_ge(prep, 6)
                for l in range(2):
                    for k in range(2):
                        ve.scalar_tensor_tensor(noise[:, l, k], s_row[:, l], s_col[:, l, k:k + 1], sw[:, l, k],
                                                ALU.mult, ALU.mult).then_inc(prep, 1)
                    ve.tensor_tensor(bn[:, l:l + 1], bias[:, l, 1:2], s_col[:, l, 2:3], ALU.mult).then_inc(prep, 1)
                ve.wait_ge(prep, 12)
                ve.tensor_tensor(noise[:], noise[:], w[:], ALU.add).then_inc(prep, 1)
                ve.tensor_tensor(bn[:], bn[:], bias[:, :, 0], ALU.add).then_inc(prep, 1)
                ve.wait_ge(prep, 14)
                ve.sem_inc(prepared, 1)
                for c in range(CH):
                    s = c % 2
                    ve.wait_ge(gate_ready, c + 1)
                    ve.tensor_scalar(v[s][:], gate[s][:], 20.0, None, ALU.min).then_inc(dve, 1)
                    ve.wait_ge(act_done, 2 * c + 2)
                    ve.scalar_tensor_tensor(v[s][:], u[s][:], 2.0, u[s][:], ALU.add, ALU.mult).then_inc(dve, 1)
                    ve.wait_ge(dve, 5 * c + 2)
                    ve.tensor_scalar(u[s][:], v[s][:], 2.0, None, ALU.add).then_inc(dve, 1)
                    ve.wait_ge(dve, 5 * c + 3)
                    ve.tensor_tensor(v[s][:], v[s][:], inner[s][:], ALU.mult).then_inc(dve, 1)
                    ve.reciprocal(u[s][:], u[s][:]).then_inc(dve, 1)
                    ve.wait_ge(dve, 5 * c + 4)
                    ve.tensor_tensor(gate[s][:], gate[s][:], v[s][:], ALU.mult).then_inc(prep, 1)
                    ve.wait_ge(dve, 5 * c + 5)
                    ve.wait_ge(prep, 15 + 2 * c)
                    ve.tensor_tensor(gate[s][:], gate[s][:], u[s][:], ALU.mult).then_inc(mixed, 1)
                    ve.wait_ge(y_ready, 2 * c + 1)
                    ve.scalar_tensor_tensor(u[s][:], y_ps[s][:], b3[:, 0:1],
                                            pe_tab[:].unsqueeze(1).broadcast_to([P, GB, PATCHES]), ALU.add, ALU.add).then_inc(prep, 1)
                    ve.wait_ge(prep, 16 + 2 * c)
                    ve.tensor_copy(core.h[:, 0:TOK].rearrange("p (b n) -> p b n", n=SEQ)[:, c * GB:(c + 1) * GB, 0:PATCHES],
                                   u[s][:].rearrange("p (b n) -> p b n", n=PATCHES)).then_inc(y_ready, 1)


def layernorm(nc, core, tag, out_ap):
    N = 2 * SEQ
    UNITS = TOK // N
    with ExitStack() as ctx:
        sb = lambda name, shape: ctx.enter_context(nc.sbuf_tensor(f"{tag}_{name}", shape, F32))
        ps = lambda name, shape: ctx.enter_context(nc.psum_tensor(f"{tag}_{name}_ps", shape, F32))
        cent = [sb(f"cent{s}", [P, N]) for s in range(SLOTS)]
        sq = [sb(f"sq{s}", [P, N]) for s in range(SLOTS)]
        std = [sb(f"std{s}", [P, N]) for s in range(SLOTS)]
        mean_ps = [ps(f"mean{s}", [P, 512]) for s in range(SLOTS)]
        var_ps = [ps(f"var{s}", [P, 512]) for s in range(SLOTS)]
        mean_made, cent_made, sq_made, var_made, std_made, rstd_made, normed_made = core.norm_sems
        base = UNITS * core.norms
        core.norms += 1
        with nc.Block() as block:
            @block.tensor
            def _(pe):
                with pe.Fori(0, UNITS // SLOTS) as i:
                    for s in range(SLOTS):
                        n = pe.snap(SLOTS * i + s)
                        pe.wait_ge(cent_made, freed(n + base))
                        pe.matmul(mean_ps[s][:, 0:N], core.mean_mat[:], core.h[:, ds(n * N, N)],
                                  start=True, stop=True).then_inc(mean_made, 1)
                    for s in range(SLOTS):
                        n = pe.snap(SLOTS * i + s)
                        pe.wait_ge(sq_made, made(n + base))
                        pe.matmul(var_ps[s][:, 0:N], core.mean_mat[:], sq[s][:], start=True, stop=True).then_inc(var_made, 1)

            @block.scalar
            def _(act):
                with act.Fori(0, UNITS // SLOTS) as i:
                    for s in range(SLOTS):
                        n = act.snap(SLOTS * i + s)
                        act.wait_ge(cent_made, made(n + base))
                        act.activation(sq[s][:], cent[s][:], ACT.Square).then_inc(sq_made, 1)
                    for s in range(SLOTS):
                        n = act.snap(SLOTS * i + s)
                        act.wait_ge(var_made, n + (base + 1))
                        act.activation(std[s][:], var_ps[s][:, 0:N], ACT.Sqrt, bias=core.eps[:, 0:1]).then_inc(std_made, 1)

            @block.vector
            def _(ve):
                if base == 0:
                    for m in (cent_made, sq_made, normed_made):
                        ve.sem_inc(m, SLOTS)
                with ve.Fori(0, UNITS // SLOTS) as i:
                    for s in range(SLOTS):
                        n = ve.snap(SLOTS * i + s)
                        ve.wait_ge(mean_made, n + (base + 1))
                        ve.wait_ge(normed_made, freed(n + base))
                        ve.tensor_tensor(cent[s][:], core.h[:, ds(n * N, N)], mean_ps[s][:, 0:N],
                                         ALU.subtract).then_inc(cent_made, 1)
                    for s in range(SLOTS):
                        n = ve.snap(SLOTS * i + s)
                        ve.wait_ge(std_made, n + (base + 1))
                        ve.reciprocal(std[s][:], std[s][:]).then_inc(rstd_made, 1)
                        ve.wait_ge(rstd_made, n + (base + 1))
                        ve.tensor_tensor(out_ap(n), cent[s][:].rearrange("p (b n) -> p b n", n=SEQ),
                                         std[s][:].rearrange("p (b n) -> p b n", n=SEQ), ALU.mult).then_inc(normed_made, 1)


def narrow_attention(nc, core, tag, projected, top_k, conv):
    HEADS, HD, G, TILES, TOP = 8, 16, 3, 3, 8
    ROWS = G * TILES * P
    SCALE = float(P) ** -0.5
    W = core.w
    wq, wk, wv = (W[tag + n] for n in ("_wq", "_wk", "_wv"))
    bq, bk, bv = (W[tag + n] for n in ("_bq", "_bk", "_bv"))
    S2 = range(SLOTS)
    with ExitStack() as ctx:
        sb = lambda name, shape: ctx.enter_context(nc.sbuf_tensor(f"{tag}_{name}", shape, F32))
        ps = lambda name, shape: ctx.enter_context(nc.psum_tensor(f"{tag}_{name}_ps", shape, F32))
        sem = lambda name: core.keep(nc.semaphore(f"{tag}_{name}"))
        xs = [sb(f"xs{s}", [P, PADSEQ]) for s in S2]
        qs = [sb(f"qs{s}", [P, SEQ]) for s in S2]
        kt = [sb(f"kt{s}", [P, SEQ]) for s in S2]
        qbd = [sb(f"qbd{s}", [P, ROWS]) for s in S2]
        vs = [sb(f"vs{s}", [HALF, 2, HEADS * (P + HD)]) for s in S2]
        prob = [sb(f"prob{s}", [P, TILES, PADSEQ]) for s in S2]
        negmax = [sb(f"negmax{s}", [P, TILES]) for s in S2]
        rsum = [sb(f"rsum{s}", [P, TILES]) for s in S2]
        rinv = [sb(f"rinv{s}", [P, TILES]) for s in S2]
        pt = [sb(f"pt{s}", [HALF, 2, ROWS]) for s in S2]
        bqs = sb("bqs", [P, 1])
        if projected:
            oc = [sb(f"oc{s}", [P, SEQ]) for s in S2]
        if top_k:
            top = [sb(f"top{s}", [P, TILES, TOP]) for s in S2]
            next_top = [sb(f"next_top{s}", [P, TILES, TOP]) for s in S2]
            left = [sb(f"left{s}", [P, TILES, SEQ]) for s in S2]
        qk_ps = [ps(f"qk{s}", [P, 512]) for s in S2]
        v_ps = [ps(f"v{s}", [P, 2, 2 * P]) for s in S2]
        s_ps = [ps(f"s{s}", [P, 512]) for s in S2]
        pt_ps = [ps(f"pt{f}", [P, 512]) for f in range(2)]
        q_at, k_at, o_at = (slice(n * PADSEQ, n * PADSEQ + SEQ) for n in range(3))
        x_made, qk_made, v_made, q_sb, k_sb, v_sb, qbd_made, o_made, h_made = (
            sem(n) for n in ("x_made", "qk_made", "v_made", "q_sb", "k_sb", "v_sb", "qbd_made", "o_made", "h_made"))
        if projected:
            oc_made, y_made = sem("oc_made"), sem("y_made")
        s_made, max_made, exp_made, rsum_made, prob_made, pt_made, pt0_sb, pt1_sb = (
            sem(n) for n in ("s_made", "max_made", "exp_made", "rsum_made", "prob_made", "pt_made", "pt0_sb", "pt1_sb"))
        set_up, bqs_made = sem("set_up"), sem("bqs_made")
        if top_k:
            passed, found, kept = sem("passed"), sem("found"), sem("kept")
        if conv:
            conv_step = sem("conv_step")
        scores = lambda s: s_ps[s][:, 0:TILES * SEQ].rearrange("p (t k) -> p t k", k=SEQ)

        def step(i, g, s):
            return SLOTS * G * i + (SLOTS * g + s)

        with nc.Block() as block:
            @block.gpsimd
            def _(pool):
                for s in S2:
                    pool.memset(qbd[s][:], 0.0).then_inc(set_up, 1)
                    pool.memset(vs[s][:], 0.0).then_inc(set_up, 1)
                    pool.memset(prob[s][:], 0.0).then_inc(set_up, 1)
                    pool.memset(xs[s][:], 0.0).then_inc(set_up, 1)
                pool.wait_ge(set_up, 8)
                with pool.Fori(0, BATCH // SLOTS) as i:
                    if not conv:
                        for s in S2:
                            b = pool.snap(SLOTS * i + s)
                            pool.wait_ge(h_made, freed(b))
                            pool.tensor_copy(xs[s][:, 0:SEQ], core.normed[:, ds(b * PADSEQ, SEQ)]).then_inc(x_made, 1)
                    for s in S2:
                        b = pool.snap(SLOTS * i + s)
                        pool.wait_ge(q_sb, b + 1)
                        pool.tensor_tensor(qbd[s][:, 0:HEADS * SEQ].rearrange("p (h q) -> p h q", h=HEADS),
                                           qs[s][:].unsqueeze(1).broadcast_to([P, HEADS, SEQ]),
                                           W["hmask16"][:].unsqueeze(2).broadcast_to([P, HEADS, SEQ]),
                                           ALU.mult).then_inc(qbd_made, 1)
                    for g in range(G):
                        for s in S2:
                            j = pool.snap(step(i, g, s))
                            pool.wait_ge(rsum_made, j + 1)
                            pool.tensor_tensor(prob[s][:, :, 0:SEQ], prob[s][:, :, 0:SEQ],
                                               rinv[s][:].unsqueeze(2).broadcast_to([P, TILES, SEQ]),
                                               ALU.mult).then_inc(prob_made, 1)

            @block.tensor
            def _(pe):
                def transposes(i, g, s):
                    j = pe.snap(step(i, g, s))
                    pe.wait_ge(prob_made, j + 1)
                    for f, emptied in ((0, pt0_sb), (1, pt1_sb)):
                        pe.wait_ge(emptied, j + 1)
                        for t in range(TILES):
                            mm = pe.transpose(pt_ps[f][0:HALF, t * P:(t + 1) * P],
                                              prob[s][:, t, f * HALF:(f + 1) * HALF], W["ident"][:])
                        mm.then_inc(pt_made, 1)

                pe.wait_ge(set_up, 8)
                with pe.Fori(0, BATCH // SLOTS) as i:
                    for s in S2:
                        b = pe.snap(SLOTS * i + s)
                        pe.wait_ge(h_made, freed(b))
                        pe.wait_ge(x_made, b + 1)
                        pe.matmul(qk_ps[s][:, q_at], wq[:], xs[s][:, 0:SEQ], start=True, stop=True)
                        pe.matmul(qk_ps[s][:, k_at], wk[:], xs[s][:, 0:SEQ], start=True, stop=True).then_inc(qk_made, 1)
                        for f in range(2):
                            mm = pe.matmul(v_ps[s][0:HALF, f, 0:P], xs[s][:, f * HALF:(f + 1) * HALF], wv[:],
                                           start=True, stop=True)
                        mm.then_inc(v_made, 1)
                    for g in range(G):
                        for s in S2:
                            j = pe.snap(step(i, g, s))
                            if g == 0:
                                b = pe.snap(SLOTS * i + s)
                                pe.wait_ge(k_sb, b + 1)
                                pe.wait_ge(qbd_made, b + 1)
                            pe.wait_ge(exp_made, freed(j))
                            for t in range(TILES):
                                r0 = (g * TILES + t) * P
                                mm = pe.matmul(scores(s)[:, t], qbd[s][:, r0:r0 + P], kt[s][:], start=True, stop=True)
                            mm.then_inc(s_made, 1)
                            if g:
                                transposes(i, g - 1, s)
                    for s in S2:
                        transposes(i, G - 1, s)
                    for s in S2:
                        j = pe.snap(step(i, G - 1, s))
                        b = pe.snap(SLOTS * i + s)
                        pe.wait_ge(v_sb, b + 1)
                        pe.wait_ge(pt0_sb, j + 2)
                        pe.wait_ge(pt1_sb, j + 2)
                        for h in range(HEADS):
                            for f in range(2):
                                mm = pe.matmul(qk_ps[s][:, o_at], vs[s][:, f, h * P:(h + 1) * P],
                                               pt[s][:, f, h * SEQ:(h + 1) * SEQ],
                                               start=(h == 0 and f == 0), stop=(h == HEADS - 1 and f == 1))
                        mm.then_inc(o_made, 1)
                    if projected:
                        for s in S2:
                            b = pe.snap(SLOTS * i + s)
                            pe.wait_ge(oc_made, b + 1)
                            pe.matmul(qk_ps[s][:, q_at], W[tag + "_wo"][:], oc[s][:], start=True, stop=True).then_inc(y_made, 1)

            @block.scalar
            def _(act):
                def leave_half_0(i, g, s):
                    j = act.snap(step(i, g, s))
                    act.wait_ge(pt_made, 2 * j + (1 + 2 * SLOTS))
                    act.activation(pt[s][:, 0, g * TILES * P:(g + 1) * TILES * P], pt_ps[0][0:HALF, 0:TILES * P],
                                   ACT.Copy).then_inc(pt0_sb, 1)

                act.activation(bqs[:], bq[:], ACT.Copy, scale=SCALE).then_inc(bqs_made, 1)
                act.wait_ge(bqs_made, 1)
                act.wait_ge(set_up, 8)
                with act.Fori(0, BATCH // SLOTS) as i:
                    for s in S2:
                        b = act.snap(SLOTS * i + s)
                        act.wait_ge(qk_made, b + 1)
                        act.activation(qs[s][:], qk_ps[s][:, q_at], ACT.Identity, bias=bqs[:, 0:1], scale=SCALE).then_inc(q_sb, 1)
                        act.activation(kt[s][:], qk_ps[s][:, k_at], ACT.Identity, bias=bk[:, 0:1]).then_inc(k_sb, 1)
                    for g in range(G):
                        for s in S2:
                            j = act.snap(step(i, g, s))
                            act.wait_ge(max_made, j + 1)
                            act.wait_ge(pt_made, 2 * j + 2)
                            for t in range(TILES):
                                a = act.activation(prob[s][:, t, 0:SEQ], scores(s)[:, t], ACT.Exp, bias=negmax[s][:, t:t + 1],
                                                   accum_out=None if top_k else rsum[s][:, t:t + 1])
                            a.then_inc(exp_made, 1)
                            if g:
                                leave_half_0(i, g - 1, s)
                    for s in S2:
                        leave_half_0(i, G - 1, s)
                    if projected:
                        for s in S2:
                            b = act.snap(SLOTS * i + s)
                            act.wait_ge(o_made, b + 1)
                            act.activation(oc[s][:], qk_ps[s][:, o_at], ACT.Identity, bias=bv[:, 0:1]).then_inc(oc_made, 1)

            @block.vector
            def _(ve):
                def row_max(i, g, s):
                    j = ve.snap(step(i, g, s))
                    ve.wait_ge(s_made, j + 1)
                    if not top_k:
                        ve.tensor_reduce(negmax[s][:], scores(s), AX.X, ALU.max, negate=True).then_inc(max_made, 1)
                        return
                    ve.sem_inc(passed, 1)
                    for t in range(TILES):
                        op = ve.max(top[s][:, t], scores(s)[:, t])
                    op.then_inc(found, 1)
                    ve.wait_ge(found, 4 * j + 1)
                    ve.sem_inc(passed, 1)
                    for t in range(TILES):
                        op = ve.match_replace(left[s][:, t], top[s][:, t], scores(s)[:, t], GONE)
                    op.then_inc(found, 1)
                    ve.tensor_scalar(negmax[s][:], top[s][:, :, 0], -1.0, None, ALU.mult).then_inc(max_made, 1)
                    ve.wait_ge(found, 4 * j + 2)
                    ve.sem_inc(passed, 1)
                    for t in range(TILES):
                        op = ve.max(next_top[s][:, t], left[s][:, t])
                    op.then_inc(found, 1)
                    ve.wait_ge(found, 4 * j + 3)
                    ve.sem_inc(passed, 1)
                    for t in range(TILES):
                        op = ve.match_replace(left[s][:, t], next_top[s][:, t], left[s][:, t], GONE)
                    op.then_inc(found, 1)

                def row_sum(i, g, s):
                    j = ve.snap(step(i, g, s))
                    ve.wait_ge(exp_made, made(j))
                    if top_k:
                        ve.wait_ge(found, 4 * j + 4)
                        for t in range(TILES):
                            op = ve.scalar_tensor_tensor(prob[s][:, t, 0:SEQ], left[s][:, t], GONE, prob[s][:, t, 0:SEQ],
                                                         ALU.is_equal, ALU.mult, accum_out=rsum[s][:, t:t + 1])
                        op.then_inc(kept, 1)
                        ve.wait_ge(kept, j + 1)
                    ve.reciprocal(rinv[s][:], rsum[s][:]).then_inc(rsum_made, 1)

                def leave_half_1(i, g, s):
                    j = ve.snap(step(i, g, s))
                    ve.wait_ge(pt_made, 2 * j + (2 + 2 * SLOTS))
                    ve.tensor_copy(pt[s][:, 1, g * TILES * P:(g + 1) * TILES * P], pt_ps[1][0:HALF, 0:TILES * P]).then_inc(pt1_sb, 1)

                ve.sem_inc(h_made, SLOTS)
                ve.sem_inc(exp_made, SLOTS)
                ve.sem_inc(pt_made, 2 * SLOTS)
                for c in (pt0_sb, pt1_sb) + ((conv_step,) if conv else ()):
                    ve.sem_inc(c, 1)
                ve.wait_ge(set_up, 8)
                with ve.Fori(0, BATCH // SLOTS) as i:
                    if conv:
                        cw = W[tag + "_pos_w"]
                        for s in S2:
                            b = ve.snap(SLOTS * i + s)
                            x = core.normed[:, ds(b * PADSEQ, SEQ)]
                            ve.wait_ge(conv_step, 3 * b + 1)
                            ve.tensor_scalar(xs[s][:, 0:SEQ], x, cw[:, 1:2], W[tag + "_pos_b"][:, 0:1],
                                             ALU.mult, ALU.add).then_inc(conv_step, 1)
                            ve.wait_ge(conv_step, 3 * b + 2)
                            ve.scalar_tensor_tensor(xs[s][:, 1:SEQ], core.normed[:, ds(b * PADSEQ, SEQ - 1)], cw[:, 0:1],
                                                    xs[s][:, 1:SEQ], ALU.mult, ALU.add).then_inc(conv_step, 1)
                            ve.wait_ge(conv_step, 3 * b + 3)
                            ve.scalar_tensor_tensor(xs[s][:, 0:SEQ - 1], core.normed[:, ds(b * PADSEQ + 1, SEQ - 1)], cw[:, 2:3],
                                                    xs[s][:, 0:SEQ - 1], ALU.mult, ALU.add).then_inc(conv_step, 1)
                            ve.wait_ge(conv_step, 3 * b + 4)
                            ve.tensor_tensor(xs[s][:, 0:SEQ], xs[s][:, 0:SEQ], x, ALU.add).then_inc(x_made, 1)
                    for s in S2:
                        b = ve.snap(SLOTS * i + s)
                        ve.wait_ge(v_made, b + 1)
                        for f in range(2):
                            spread = vs[s][:, f].rearrange("p (h x) -> p h x", h=HEADS)[:, :, 0:HD]
                            op = ve.tensor_copy(spread, v_ps[s][0:HALF, f, 0:P].rearrange("p (h d) -> p h d", d=HD))
                        op.then_inc(v_sb, 1)
                    for g in range(G):
                        for s in S2:
                            row_max(i, g, s)
                        if g:
                            for s in S2:
                                leave_half_1(i, g - 1, s)
                        for s in S2:
                            row_sum(i, g, s)
                    for s in S2:
                        leave_half_1(i, G - 1, s)
                    for s in S2:
                        b = ve.snap(SLOTS * i + s)
                        ve.wait_ge(y_made if projected else o_made, b + 1)
                        h_b = core.h[:, ds(b * SEQ, SEQ)]
                        ve.scalar_tensor_tensor(h_b, qk_ps[s][:, q_at if projected else o_at],
                                                (W[tag + "_bo"] if projected else bv)[:, 0:1], h_b,
                                                ALU.add, ALU.add).then_inc(h_made, 1)


def routed_experts(nc, core, dram):
    EXPERTS, TOP_K, FF, ROUTED = 8, 2, 512, 1024
    FC = FF // P
    CHUNKS = ROUTED // CHUNK
    S2 = range(SLOTS)
    AHEAD = SLOTS + 1
    with ExitStack() as ctx:
        sb = lambda name, shape, dt=F32: ctx.enter_context(nc.sbuf_tensor(f"m_{name}", shape, dt))
        ps = lambda name, shape: ctx.enter_context(nc.psum_tensor(f"m_{name}_ps", shape, F32))
        sem = lambda name: core.keep(nc.semaphore(f"m_{name}"))
        ids_i = sb("ids_i", [P, TOP_K, ROUTED], I32)
        ids = sb("ids", [P, TOP_K, ROUTED])
        slot_w = sb("slot_w", [P, TOP_K, ROUTED])
        picked = sb("picked", [P, TOP_K, ROUTED])
        share = sb("share", [P, EXPERTS, ROUTED])
        w1 = [sb(f"w1{s}", [P, FF]) for s in S2]
        w2 = [sb(f"w2{s}", [P, FC, P]) for s in S2]
        hid = [sb(f"hid{s}", [P, FC, CHUNK]) for s in S2]
        part = [sb(f"part{s}", [P, CHUNK]) for s in S2]
        up_ps = [ps(f"up{f}", [P, CHUNK]) for f in range(FC)]
        down_ps = [ps(f"down{s}", [P, CHUNK]) for s in S2]
        ids_in, ids_made, picked_made, share_made = (sem(n) for n in ("ids_in", "ids_made", "picked_made", "share_made"))
        w_in = [sem(f"w_in{s}") for s in S2]
        up_made, gelu_made, down_made, part_made, h_made = (
            sem(n) for n in ("up_made", "gelu_made", "down_made", "part_made", "h_made"))

        with nc.Block() as block:
            @block.sync
            def _(sp):
                sp.dma_start(ids_i[:], dram["expert_ids"].partition_broadcast(P)).then_inc(ids_in, 16)
                sp.dma_start(slot_w[:], dram["expert_rows"].partition_broadcast(P)).then_inc(ids_in, 16)
                with sp.Fori(0, EXPERTS // SLOTS) as i:
                    for s in S2:
                        e = sp.snap(SLOTS * i + s)
                        sp.wait_ge(down_made, CHUNKS * e + (AHEAD - 2))
                        sp.dma_start(w1[s][:], dram["m_w1"][ds(e, 1)].rearrange("e p f -> p (e f)")).then_inc(w_in[s], 16)
                        sp.dma_start(w2[s][:], dram["m_w2"][ds(e, 1)].rearrange("e p c o -> p (e c) o")).then_inc(w_in[s], 16)

            @block.tensor
            def _(pe):
                def up(i, s, c):
                    t = pe.snap(SLOTS * CHUNKS * i + (CHUNKS * s + c))
                    if c == 0:
                        pe.wait_ge(w_in[s], 32 * i + 32)
                    for f in range(FC):
                        pe.wait_ge(gelu_made, FC * t + (f + 1))
                        pe.matmul(up_ps[f][:], w1[s][:, f * P:(f + 1) * P], core.normed[:, c * CHUNK:(c + 1) * CHUNK],
                                  start=True, stop=True).then_inc(up_made, 1)

                def down(i, s, c):
                    t = pe.snap(SLOTS * CHUNKS * i + (CHUNKS * s + c))
                    pe.wait_ge(gelu_made, FC * t + 2 * FC)
                    pe.wait_ge(part_made, freed(t))
                    for f in range(FC):
                        mm = pe.matmul(down_ps[c][:], w2[s][:, f], hid[c][:, f], start=(f == 0), stop=(f == FC - 1))
                    mm.then_inc(down_made, 1)

                steps = [(s, c) for s in S2 for c in range(CHUNKS)]
                with pe.Fori(0, EXPERTS // SLOTS) as i:
                    up(i, *steps[0])
                    for n in range(1, len(steps)):
                        up(i, *steps[n])
                        down(i, *steps[n - 1])
                    down(i, *steps[-1])

            @block.scalar
            def _(act):
                with act.Fori(0, EXPERTS // SLOTS) as i:
                    for n in range(SLOTS * CHUNKS):
                        t = act.snap(SLOTS * CHUNKS * i + n)
                        act.wait_ge(down_made, made(t, AHEAD) - SLOTS)
                        for f in range(FC):
                            act.wait_ge(up_made, FC * t + (f + 1))
                            act.activation(hid[n % CHUNKS][:, f], up_ps[f][:], ACT.Gelu).then_inc(gelu_made, 1)

            @block.vector
            def _(ve):
                ve.sem_inc(gelu_made, FC)
                ve.sem_inc(down_made, AHEAD)
                ve.sem_inc(part_made, SLOTS)
                ve.sem_inc(h_made, SLOTS)
                ve.wait_ge(ids_in, 32)
                ve.tensor_copy(ids[:], ids_i[:]).then_inc(ids_made, 1)
                ve.wait_ge(ids_made, 1)
                for e in range(EXPERTS):
                    if e:
                        ve.wait_ge(share_made, e)
                    ve.scalar_tensor_tensor(picked[:], ids[:], float(e), slot_w[:], ALU.is_equal, ALU.mult).then_inc(picked_made, 1)
                    ve.wait_ge(picked_made, e + 1)
                    ve.tensor_tensor(share[:, e], picked[:, 0], picked[:, 1], ALU.add).then_inc(share_made, 1)
                ve.wait_ge(share_made, EXPERTS)
                with ve.Fori(0, EXPERTS // SLOTS) as i:
                    for s in S2:
                        for c in range(CHUNKS):
                            t = ve.snap(SLOTS * CHUNKS * i + (CHUNKS * s + c))
                            ve.wait_ge(down_made, made(t, AHEAD))
                            ve.wait_ge(h_made, freed(t))
                            ve.tensor_tensor(part[c][:], down_ps[c][:],
                                             share[:, ds(SLOTS * i + s, 1), c * CHUNK:(c + 1) * CHUNK].rearrange("p e n -> p (e n)"),
                                             ALU.mult).then_inc(part_made, 1)
                            ve.wait_ge(part_made, made(t))
                            h_c = core.h[:, c * CHUNK:(c + 1) * CHUNK]
                            ve.tensor_tensor(h_c, h_c, part[c][:], ALU.add).then_inc(h_made, 1)


def head_mixing(nc, core):
    HEADS, HD = 8, 16
    SCALE = float(HD) ** -0.5
    TILES = TOKPAD // P
    W = core.w
    S2 = range(SLOTS)
    with ExitStack() as ctx:
        sb = lambda name, shape: ctx.enter_context(nc.sbuf_tensor(f"a1_{name}", shape, F32))
        ps = lambda name, shape: ctx.enter_context(nc.psum_tensor(f"a1_{name}_ps", shape, F32))
        sem = lambda name: core.keep(nc.semaphore(f"a1_{name}"))
        xs = [sb(f"xs{s}", [P, P]) for s in S2]
        qkv = [sb(f"qkv{s}", [P, 3, P]) for s in S2]
        prod = [sb(f"prod{s}", [P, HEADS, HEADS, HD]) for s in S2]
        prod2 = [sb(f"prod2{s}", [P, HEADS, HD, HEADS]) for s in S2]
        score = [sb(f"score{s}", [P, HEADS, HEADS]) for s in S2]
        shifted = [sb(f"shifted{s}", [P, HEADS, HEADS]) for s in S2]
        weight = [sb(f"weight{s}", [P, HEADS, HEADS]) for s in S2]
        top = [sb(f"top{s}", [P, HEADS]) for s in S2]
        total = [sb(f"total{s}", [P, HEADS]) for s in S2]
        inv = [sb(f"inv{s}", [P, HEADS]) for s in S2]
        mixed = [sb(f"mixed{s}", [P, HEADS, HD]) for s in S2]
        scaled = [sb(f"scaled{s}", [P, P]) for s in S2]
        qkv_ps = [ps(f"qkv{s}", [P, 512]) for s in S2]
        turn_ps = [ps(f"turn{s}", [P, 512]) for s in S2]
        names = ["x_made", "qkv_made", "qkv_sb", "prod_made", "score_made", "top_made", "shifted_made", "weight_made",
                 "total_made", "inv_made", "prod2_made", "mixed_made", "scaled_made", "turn_made", "turned_made"]
        (x_made, qkv_made, qkv_sb, prod_made, score_made, top_made, shifted_made, weight_made, total_made, inv_made,
         prod2_made, mixed_made, scaled_made, turn_made, turned_made) = (sem(n) for n in names)

        with nc.Block() as block:
            @block.gpsimd
            def _(pool):
                with pool.Fori(0, TILES // SLOTS) as i:
                    for s in S2:
                        t = pool.snap(SLOTS * i + s)
                        pool.wait_ge(turned_made, freed(t))
                        pool.tensor_copy(xs[s][:], core.normed[:, ds(t * P, P)]).then_inc(x_made, 1)
                    for s in S2:
                        t = pool.snap(SLOTS * i + s)
                        pool.wait_ge(qkv_sb, t + 1)
                        q = qkv[s][:, 0].rearrange("p (h d) -> p h d", d=HD)
                        k = qkv[s][:, 1].rearrange("p (g d) -> p g d", d=HD)
                        for h in range(HEADS):
                            op = pool.tensor_tensor(prod[s][:, h], q[:, h].unsqueeze(1).broadcast_to([P, HEADS, HD]), k, ALU.mult)
                        op.then_inc(prod_made, 1)

            @block.tensor
            def _(pe):
                with pe.Fori(0, TILES // SLOTS) as i:
                    for s in S2:
                        t = pe.snap(SLOTS * i + s)
                        pe.wait_ge(x_made, t + 1)
                        pe.matmul(qkv_ps[s][:, 0:3 * P], xs[s][:], W["a1_wqkv"][:], start=True, stop=True).then_inc(qkv_made, 1)
                    for s in S2:
                        t = pe.snap(SLOTS * i + s)
                        pe.wait_ge(scaled_made, t + 1)
                        pe.wait_ge(turned_made, freed(t))
                        pe.transpose(turn_ps[s][:, 0:P], scaled[s][:], W["ident"][:]).then_inc(turn_made, 1)

            @block.scalar
            def _(act):
                with act.Fori(0, TILES // SLOTS) as i:
                    for s in S2:
                        t = act.snap(SLOTS * i + s)
                        act.wait_ge(qkv_made, t + 1)
                        act.activation(qkv[s][:], qkv_ps[s][:, 0:3 * P].rearrange("p (c e) -> p c e", e=P), ACT.Copy).then_inc(qkv_sb, 1)
                    for s in S2:
                        t = act.snap(SLOTS * i + s)
                        act.wait_ge(shifted_made, t + 1)
                        act.activation(weight[s][:], shifted[s][:], ACT.Exp, scale=SCALE).then_inc(weight_made, 1)
                    for s in S2:
                        t = act.snap(SLOTS * i + s)
                        act.wait_ge(turn_made, t + 1)
                        act.activation(core.normed[:, ds(t * P, P)], turn_ps[s][:, 0:P], ACT.Copy).then_inc(turned_made, 1)

            @block.vector
            def _(ve):
                ve.sem_inc(turned_made, SLOTS)
                with ve.Fori(0, TILES // SLOTS) as i:
                    for s in S2:
                        t = ve.snap(SLOTS * i + s)
                        ve.wait_ge(prod_made, t + 1)
                        ve.tensor_reduce(score[s][:], prod[s][:], AX.X, ALU.add).then_inc(score_made, 1)
                        ve.wait_ge(score_made, t + 1)
                        ve.tensor_reduce(top[s][:], score[s][:], AX.X, ALU.max).then_inc(top_made, 1)
                        ve.wait_ge(top_made, t + 1)
                        ve.tensor_tensor(shifted[s][:], score[s][:], top[s][:].unsqueeze(2).broadcast_to([P, HEADS, HEADS]),
                                         ALU.subtract).then_inc(shifted_made, 1)
                    for s in S2:
                        t = ve.snap(SLOTS * i + s)
                        ve.wait_ge(weight_made, t + 1)
                        ve.tensor_reduce(total[s][:], weight[s][:], AX.X, ALU.add).then_inc(total_made, 1)
                        v = qkv[s][:, 2].rearrange("p (g d) -> p d g", d=HD)
                        for h in range(HEADS):
                            op = ve.tensor_tensor(prod2[s][:, h], weight[s][:, h].unsqueeze(1).broadcast_to([P, HD, HEADS]), v, ALU.mult)
                        op.then_inc(prod2_made, 1)
                        ve.wait_ge(total_made, t + 1)
                        ve.reciprocal(inv[s][:], total[s][:]).then_inc(inv_made, 1)
                        ve.wait_ge(prod2_made, t + 1)
                        ve.tensor_reduce(mixed[s][:], prod2[s][:], AX.X, ALU.add).then_inc(mixed_made, 1)
                        ve.wait_ge(mixed_made, t + 1)
                        ve.wait_ge(inv_made, t + 1)
                        ve.tensor_tensor(scaled[s][:].rearrange("p (h d) -> p h d", d=HD), mixed[s][:],
                                         inv[s][:].unsqueeze(2).broadcast_to([P, HEADS, HD]), ALU.mult).then_inc(scaled_made, 1)


def window_projection(nc, core):
    HEADS, HD, WINDOW = 8, 16, 64
    SHIFT = WINDOW // 2
    WINDOWS = -(-SEQ // WINDOW)
    HALF_BATCHES = BATCH // 2
    W = core.w
    S2 = range(SLOTS)
    kept = lambda w, h: max(0, min(HEADS, SEQ - (WINDOW * w + HEADS * h)))
    with ExitStack() as ctx:
        sb = lambda name, shape: ctx.enter_context(nc.sbuf_tensor(f"wp_{name}", shape, F32))
        ps = lambda name, shape: ctx.enter_context(nc.psum_tensor(f"wp_{name}_ps", shape, F32))
        sem = lambda name: core.keep(nc.semaphore(f"wp_{name}"))
        rolled = sb("rolled", [P, BATCH, WINDOWS * WINDOW])
        w_head = [sb(f"w_head{s}", [P, HEADS, P]) for s in S2]
        y_ps = [[ps(f"y{s}{q}", [P, 512]) for q in range(2)] for s in S2]
        padded_made, rolled_made, w_made, y_made, h_made = (
            sem(n) for n in ("padded_made", "rolled_made", "w_made", "y_made", "h_made"))
        flat = core.normed[:, 0:TOK].rearrange("p (b n) -> p b n", n=SEQ)
        res = core.h[:, 0:TOK].rearrange("p (b n) -> p b n", n=SEQ)
        with nc.Block() as block:
            @block.gpsimd
            def _(pool):
                pool.memset(rolled[:, :, SEQ:], 0.0).then_inc(padded_made, 1)
                pool.tensor_copy(rolled[:, :, SEQ - SHIFT:SEQ], flat[:, :, 0:SHIFT]).then_inc(padded_made, 1)

            @block.scalar
            def _(act):
                act.activation(rolled[:, :, 0:SEQ - SHIFT], flat[:, :, SHIFT:SEQ], ACT.Copy).then_inc(rolled_made, 1)

            @block.tensor
            def _(pe):
                pe.wait_ge(padded_made, 2)
                pe.wait_ge(rolled_made, 1)
                tok = rolled[:].rearrange("p b (w a e) -> p b w a e", a=HEADS, e=HEADS)
                for h in range(HEADS):
                    s = h % SLOTS
                    wins = sum(kept(w, h) > 0 for w in range(WINDOWS))
                    pe.wait_ge(w_made, h + 1)
                    if h >= SLOTS:
                        pe.wait_ge(h_made, h - 1)
                    for q in range(2):
                        y = y_ps[s][q][:, 0:HALF_BATCHES * wins * HEADS].rearrange("p (b w a) -> p b w a", w=wins, a=HEADS)
                        for e in range(HEADS):
                            mm = pe.matmul(y, w_head[s][:, e], tok[:, q * HALF_BATCHES:(q + 1) * HALF_BATCHES, 0:wins, :, e],
                                           start=(e == 0), stop=(e == HEADS - 1))
                    mm.then_inc(y_made, 1)

            @block.vector
            def _(ve):
                def head_weights(h):
                    if h >= SLOTS:
                        ve.wait_ge(y_made, h - 1)
                    ve.tensor_scalar(w_head[h % SLOTS][:], W["wp_w"][:], W["hmask16"][:, h:h + 1], None, ALU.mult).then_inc(w_made, 1)

                head_weights(0)
                for h in range(HEADS):
                    s = h % SLOTS
                    wins = sum(kept(w, h) > 0 for w in range(WINDOWS))
                    if h + 1 < HEADS:
                        head_weights(h + 1)
                    ve.wait_ge(y_made, h + 1)
                    for q in range(2):
                        bs = slice(q * HALF_BATCHES, (q + 1) * HALF_BATCHES)
                        y = y_ps[s][q][:, 0:HALF_BATCHES * wins * HEADS].rearrange("p (b w a) -> p b w a", w=wins, a=HEADS)
                        for w in range(wins):
                            first = (WINDOW * w + HEADS * h + SHIFT) % SEQ
                            n = kept(w, h)
                            cut = min(n, SEQ - first)
                            for a0, a1, at in ((0, cut, first), (cut, n, 0)):
                                if a1 > a0:
                                    r = res[:, bs, at:at + a1 - a0]
                                    op = ve.scalar_tensor_tensor(r, y[:, :, w, a0:a1], W["wp_b"][:, 0:1], r, ALU.add, ALU.add)
                    op.then_inc(h_made, 1)


def trig_ffn(nc, core):
    NF, QUAD, LUT = 64, 4, 1024
    R = NF // QUAD
    W = core.w
    STEP = 2.0 * math.pi / LUT
    CHUNKS = TOKPAD // CHUNK
    WIDE = QUAD * CHUNK
    S2 = range(SLOTS)
    with ExitStack() as ctx:
        sb = lambda name, shape, dt=F32: ctx.enter_context(nc.sbuf_tensor(f"f1_{name}", shape, dt))
        ps = lambda name, shape: ctx.enter_context(nc.psum_tensor(f"f1_{name}_ps", shape, F32))
        sem = lambda name: core.keep(nc.semaphore(f"f1_{name}"))
        scale = sb("scale", [P, NF])
        shift = sb("shift", [P, NF])
        absw = sb("absw", [P, NF])
        cols = sb("cols", [P, NF, 2, 32])
        minus_pi = sb("minus_pi", [P, 1])
        angle = [sb(f"angle{s}", [P, QUAD, CHUNK], I32) for s in S2]
        sin_at = [sb(f"sin_at{s}", [P, QUAD, CHUNK], I16) for s in S2]
        cos_at = [sb(f"cos_at{s}", [P, QUAD, CHUNK], I16) for s in S2]
        cos_raw = [sb(f"cos_raw{s}", [P, QUAD, CHUNK], I16) for s in S2]
        sin_v = [sb(f"sin_v{s}", [P, QUAD, CHUNK]) for s in S2]
        cos_v = [sb(f"cos_v{s}", [P, QUAD, CHUNK]) for s in S2]
        sums = sb("sums", [P, CHUNK])
        e = sb("e", [P, CHUNK])
        sum_ps = ps("sum", [P, CHUNK])
        y_ps = ps("y", [P, CHUNK])
        set_up, angle_made, sin_at_made, cos_raw_made, cos_at_made, sin_made, cos_made, used = (
            sem(n) for n in ("set_up", "angle_made", "sin_at_made", "cos_raw_made", "cos_at_made", "sin_made", "cos_made", "used"))
        clamped, sums_sb, y_made, e_made, silu_step, h_made = (
            sem(n) for n in ("clamped", "sums_sb", "y_made", "e_made", "silu_step", "h_made"))

        with nc.Block() as block:
            @block.tensor
            def _(pe):
                pe.wait_ge(set_up, 9)
                with pe.Fori(0, CHUNKS) as c:
                    pe.wait_ge(sums_sb, c + 1)
                    for r in range(R):
                        s = r % SLOTS
                        q = pe.snap(R * c + r)
                        for cs, made_, values in ((1, sin_made, sin_v), (0, cos_made, cos_v)):
                            pe.wait_ge(made_, made(q))
                            for j in range(QUAD):
                                mm = pe.matmul(sum_ps[32 * j:32 * (j + 1), :], cols[:, QUAD * r + j, cs], values[s][:, j],
                                               start=(r == 0 and cs == 1), stop=(r == R - 1 and cs == 0))
                        mm.then_inc(used, 1)
                    mm_all = pe.snap(c + 2)
                    pe.wait_ge(sums_sb, mm_all)
                    pe.wait_ge(h_made, c + 1)
                    pe.matmul(y_ps[:], W["f1_proj"][:], sums[:], start=True, stop=True).then_inc(y_made, 1)

            @block.scalar
            def _(act):
                act.wait_ge(set_up, 9)
                with act.Fori(0, CHUNKS) as c:
                    for r in range(R):
                        s = r % SLOTS
                        q = act.snap(R * c + r)
                        act.wait_ge(used, freed(q))
                        act.wait_ge(sin_at_made, q + 1)
                        act.activation(sin_v[s][:], sin_at[s][:], ACT.Sin, bias=minus_pi[:, 0:1], scale=STEP).then_inc(sin_made, 1)
                        act.wait_ge(cos_at_made, q + 1)
                        act.activation(cos_v[s][:], cos_at[s][:], ACT.Sin, bias=minus_pi[:, 0:1], scale=STEP).then_inc(cos_made, 1)
                    act.wait_ge(used, made(R * c + (R - 1)))
                    act.wait_ge(y_made, c + 1)
                    act.activation(sums[:], sum_ps[:], ACT.Copy).then_inc(sums_sb, 1)
                    act.wait_ge(clamped, c + 1)
                    act.activation(e[:], e[:], ACT.Exp).then_inc(e_made, 1)

            @block.vector
            def _(ve):
                ve.scalar_tensor_tensor(absw[:], W["f1_w"][:], -1.0, W["f1_w"][:], ALU.mult, ALU.max).then_inc(set_up, 1)
                ve.wait_ge(set_up, 1)
                ve.tensor_scalar(absw[:], absw[:], 1.0, STEP, ALU.add, ALU.mult).then_inc(set_up, 1)
                ve.wait_ge(set_up, 2)
                ve.reciprocal(scale[:], absw[:]).then_inc(set_up, 1)
                ve.tensor_scalar(shift[:], W["f1_b"][:], 1.0 / STEP, None, ALU.mult).then_inc(set_up, 1)
                ve.memset(cols[:], 0.0).then_inc(set_up, 1)
                ve.memset(minus_pi[:], -math.pi).then_inc(set_up, 1)
                ve.wait_ge(set_up, 6)
                for r in range(R):
                    for cs, name in ((0, "f1_attn_cos"), (1, "f1_attn_sin")):
                        op = ve.tensor_copy(cols[:, QUAD * r:QUAD * (r + 1), cs, R * cs + r],
                                            W[name][:, QUAD * r:QUAD * (r + 1)])
                op.then_inc(set_up, 1)
                ve.sem_inc(used, SLOTS)
                ve.sem_inc(sin_made, SLOTS)
                ve.sem_inc(cos_made, SLOTS)
                for m in (sums_sb, y_made, h_made, silu_step):
                    ve.sem_inc(m, 1)
                ve.wait_ge(set_up, 7)
                ve.sem_inc(set_up, 2)
                with ve.Fori(0, CHUNKS) as c:
                    x = core.normed[:, ds(c * CHUNK, CHUNK)]
                    for r in range(R):
                        s = r % SLOTS
                        q = ve.snap(R * c + r)
                        for j in range(QUAD):
                            n = QUAD * r + j
                            op = ve.tensor_scalar(angle[s][:, j], x, scale[:, n:n + 1], shift[:, n:n + 1], ALU.mult, ALU.add)
                        op.then_inc(angle_made, 1)
                        ve.wait_ge(angle_made, q + 1)
                        ve.wait_ge(sin_made, freed(q))
                        low = angle[s][:].bitcast(I16).rearrange("p j (t w) -> p j t w", w=2)[:, :, :, 0]
                        ve.tensor_scalar(sin_at[s][:], low, LUT - 1, None, ALU.bitwise_and).then_inc(sin_at_made, 1)
                        ve.wait_ge(sin_at_made, q + 1)
                        ve.tensor_scalar(cos_raw[s][:], sin_at[s][:], float(LUT // 4), None, ALU.add).then_inc(cos_raw_made, 1)
                        ve.wait_ge(cos_raw_made, q + 1)
                        ve.wait_ge(cos_made, freed(q))
                        ve.tensor_scalar(cos_at[s][:], cos_raw[s][:], LUT - 1, None, ALU.bitwise_and).then_inc(cos_at_made, 1)
                    ve.wait_ge(y_made, c + 2)
                    ve.wait_ge(h_made, c + 1)
                    ve.tensor_scalar(e[:], y_ps[:], 80.0, None, ALU.min).then_inc(clamped, 1)
                    ve.wait_ge(e_made, c + 1)
                    ve.tensor_scalar(e[:], e[:], 1.0, None, ALU.add).then_inc(silu_step, 1)
                    ve.wait_ge(silu_step, 3 * c + 2)
                    ve.reciprocal(e[:], e[:]).then_inc(silu_step, 1)
                    ve.wait_ge(silu_step, 3 * c + 3)
                    ve.scalar_tensor_tensor(e[:], y_ps[:], -1.0, e[:], ALU.mult, ALU.mult).then_inc(silu_step, 1)
                    ve.wait_ge(silu_step, 3 * c + 4)
                    h_c = core.h[:, ds(c * CHUNK, CHUNK)]
                    ve.tensor_tensor(h_c, h_c, e[:], ALU.add).then_inc(h_made, 1)


def decay_retrieval(nc, core):
    HEADS, HD = 4, 32
    W = core.w
    S2 = range(SLOTS)
    with ExitStack() as ctx:
        sb = lambda name, shape: ctx.enter_context(nc.sbuf_tensor(f"a2_{name}", shape, F32))
        ps = lambda name, shape: ctx.enter_context(nc.psum_tensor(f"a2_{name}_ps", shape, F32))
        sem = lambda name: core.keep(nc.semaphore(f"a2_{name}"))
        ones = sb("ones", [P, P])
        v_w = sb("v_w", [P, P])
        o_w = sb("o_w", [P, P])
        log_decay = sb("log_decay", [P, HEADS])
        decay = sb("decay", [HALF, HEADS, 2, SEQ])
        xs = [sb(f"xs{s}", [P, PADSEQ]) for s in S2]
        qk = [sb(f"qk{s}", [P, 2, PADSEQ]) for s in S2]
        sq = [sb(f"sq{s}", [P, 2, PADSEQ]) for s in S2]
        norm = [sb(f"norm{s}", [P, 2, PADSEQ]) for s in S2]
        vs = [sb(f"vs{s}", [HALF, 2, P]) for s in S2]
        weight = [sb(f"weight{s}", [HALF, HEADS, 2, SEQ]) for s in S2]
        got = [sb(f"got{s}", [P, SEQ]) for s in S2]
        qk_ps = ps("qk", [P, 512])
        n_ps = ps("n", [P, 512])
        v_ps = ps("v", [P, 512])
        s_ps = ps("s", [P, HEADS, 512])
        o_ps = ps("o", [P, 512])
        (decay_made, w_ps_made, x_made, qk_made, qk_sb, sq_made, n_made, root_made, inv_step, unit_made, v_made, v_sb,
         s_made, weight_made, got_made, got_sb, y_made, h_made, w_sb) = (
            sem(n) for n in ("decay_made", "w_ps_made", "x_made", "qk_made", "qk_sb", "sq_made", "n_made", "root_made",
                             "inv_step", "unit_made", "v_made", "v_sb", "s_made", "weight_made", "got_made", "got_sb",
                             "y_made", "h_made", "w_sb"))
        two = lambda t: t[:, 0:2 * PADSEQ].rearrange("p (c n) -> p c n", n=PADSEQ)

        with nc.Block() as block:
            @block.gpsimd
            def _(pool):
                for s in S2:
                    pool.memset(xs[s][:, SEQ:PADSEQ], 0.0)
                with pool.Fori(0, BATCH // SLOTS) as i:
                    for s in S2:
                        b = pool.snap(SLOTS * i + s)
                        pool.wait_ge(h_made, freed(b))
                        pool.tensor_copy(xs[s][:, 0:SEQ], core.normed[:, ds(b * PADSEQ, SEQ)]).then_inc(x_made, 1)

            @block.tensor
            def _(pe):
                pe.matmul(v_ps[:, 0:P], W["a2_basis"][:], W["a2_vc"][:], start=True, stop=True)
                pe.matmul(o_ps[:, 0:P], W["a2_oc"][:], W["a2_basis"][:], start=True, stop=True).then_inc(w_ps_made, 1)
                pe.wait_ge(w_sb, 3)
                with pe.Fori(0, BATCH // SLOTS) as i:
                    for s in S2:
                        b = pe.snap(SLOTS * i + s)
                        pe.wait_ge(x_made, b + 1)
                        pe.wait_ge(qk_sb, b + 1)
                        pe.matmul(qk_ps[:, 0:PADSEQ], W["a2_wq"][:], xs[s][:], start=True, stop=True)
                        pe.matmul(qk_ps[:, PADSEQ:2 * PADSEQ], W["a2_wk"][:], xs[s][:], start=True, stop=True).then_inc(qk_made, 1)
                        pe.wait_ge(v_sb, b + 1)
                        for f in range(2):
                            mm = pe.matmul(v_ps[0:HALF, f * P:(f + 1) * P], xs[s][:, f * HALF:(f + 1) * HALF], v_w[:], start=True, stop=True)
                        mm.then_inc(v_made, 1)
                    for s in S2:
                        b = pe.snap(SLOTS * i + s)
                        pe.wait_ge(sq_made, b + 1)
                        pe.wait_ge(root_made, b + 1)
                        pe.matmul(n_ps[:, 0:2 * PADSEQ], ones[:], sq[s][:].rearrange("p c n -> p (c n)"), start=True, stop=True).then_inc(n_made, 1)
                    for s in S2:
                        b = pe.snap(SLOTS * i + s)
                        pe.wait_ge(unit_made, b + 1)
                        pe.wait_ge(weight_made, b + 1)
                        for h in range(HEADS):
                            rows = slice(h * HD, (h + 1) * HD)
                            for f in range(2):
                                mm = pe.matmul(s_ps[0:HALF, h, f * SEQ:(f + 1) * SEQ], qk[s][rows, 1, f * HALF:(f + 1) * HALF],
                                               qk[s][rows, 0, 0:SEQ], start=True, stop=True)
                        mm.then_inc(s_made, 1)
                    for s in S2:
                        b = pe.snap(SLOTS * i + s)
                        pe.wait_ge(weight_made, b + 2)
                        pe.wait_ge(v_sb, b + 2)
                        pe.wait_ge(h_made, b + 2)
                        for h in range(HEADS):
                            rows = slice(h * HD, (h + 1) * HD)
                            for f in range(2):
                                mm = pe.matmul(o_ps[rows, 0:SEQ], vs[s][:, f, rows], weight[s][:, h, f], start=(f == 0), stop=(f == 1))
                        mm.then_inc(got_made, 1)
                        pe.wait_ge(got_sb, b + 1)
                        pe.matmul(o_ps[:, PADSEQ:PADSEQ + SEQ], o_w[:], got[s][:], start=True, stop=True).then_inc(y_made, 1)

            @block.scalar
            def _(act):
                act.activation(log_decay[:], W["a2_decay"][:], ACT.Exp, scale=-1.0).then_inc(decay_made, 1)
                act.wait_ge(decay_made, 3)
                act.activation(log_decay[:], log_decay[:], ACT.Ln).then_inc(decay_made, 1)
                act.wait_ge(decay_made, 4)
                for h in range(HEADS):
                    a = act.activation(decay[:, h], W["a2_distance"][:], ACT.Exp, scale=log_decay[0:HALF, h:h + 1])
                a.then_inc(decay_made, 1)
                with act.Fori(0, BATCH // SLOTS) as i:
                    for s in S2:
                        b = act.snap(SLOTS * i + s)
                        act.wait_ge(qk_made, b + 1)
                        act.activation(qk[s][:], two(qk_ps), ACT.Copy).then_inc(qk_sb, 1)
                        act.wait_ge(qk_sb, b + 2)
                        act.activation(sq[s][:], qk[s][:], ACT.Square).then_inc(sq_made, 1)
                    for s in S2:
                        b = act.snap(SLOTS * i + s)
                        act.wait_ge(n_made, b + 1)
                        act.activation(norm[s][:], two(n_ps), ACT.Sqrt).then_inc(root_made, 1)
                    for s in S2:
                        b = act.snap(SLOTS * i + s)
                        act.wait_ge(got_made, b + 1)
                        act.activation(got[s][:], o_ps[:, 0:SEQ], ACT.Copy).then_inc(got_sb, 1)

            @block.vector
            def _(ve):
                ve.memset(ones[:], 1.0).then_inc(w_sb, 1)
                ve.wait_ge(w_ps_made, 1)
                ve.tensor_copy(v_w[:], v_ps[:, 0:P]).then_inc(w_sb, 1)
                ve.tensor_scalar(o_w[:], o_ps[:, 0:P], W["a2_out_scale"][:, 0:1], None, ALU.mult).then_inc(w_sb, 1)
                ve.wait_ge(decay_made, 1)
                ve.tensor_scalar(log_decay[:], log_decay[:], 1.0, None, ALU.add).then_inc(decay_made, 1)
                ve.wait_ge(decay_made, 2)
                ve.reciprocal(log_decay[:], log_decay[:]).then_inc(decay_made, 1)
                ve.wait_ge(decay_made, 5)
                ve.tensor_tensor(decay[:], decay[:], W["a2_later"][:].unsqueeze(1).broadcast_to([HALF, HEADS, 2, SEQ]),
                                 ALU.mult).then_inc(decay_made, 1)
                ve.sem_inc(h_made, SLOTS)
                for m in (qk_sb, v_sb, root_made, weight_made):
                    ve.sem_inc(m, 1)
                ve.wait_ge(decay_made, 6)
                with ve.Fori(0, BATCH // SLOTS) as i:
                    for s in S2:
                        b = ve.snap(SLOTS * i + s)
                        ve.wait_ge(v_made, b + 1)
                        ve.tensor_copy(vs[s][:], v_ps[0:HALF, 0:2 * P].rearrange("p (f e) -> p f e", e=P)).then_inc(v_sb, 1)
                    for s in S2:
                        b = ve.snap(SLOTS * i + s)
                        ve.wait_ge(root_made, b + 2)
                        ve.tensor_scalar(norm[s][:], norm[s][:], 1e-12, None, ALU.max).then_inc(inv_step, 1)
                        ve.wait_ge(inv_step, 2 * b + 1)
                        ve.reciprocal(norm[s][:], norm[s][:]).then_inc(inv_step, 1)
                        ve.wait_ge(inv_step, 2 * b + 2)
                        ve.tensor_tensor(qk[s][:], qk[s][:], norm[s][:], ALU.mult).then_inc(unit_made, 1)
                    for s in S2:
                        b = ve.snap(SLOTS * i + s)
                        ve.wait_ge(s_made, b + 1)
                        ve.tensor_tensor(weight[s][:].rearrange("p h f q -> p h (f q)"), s_ps[0:HALF, :, 0:2 * SEQ],
                                         decay[:].rearrange("p h f q -> p h (f q)"), ALU.mult).then_inc(weight_made, 1)
                    for s in S2:
                        b = ve.snap(SLOTS * i + s)
                        ve.wait_ge(y_made, b + 1)
                        h_b = core.h[:, ds(b * SEQ, SEQ)]
                        ve.tensor_tensor(h_b, h_b, o_ps[:, PADSEQ:PADSEQ + SEQ], ALU.add).then_inc(h_made, 1)





def wide_attention(nc, core):
    HD, G, TILES, R, QW = 64, 4, 3, 96, 144
    ROWS = TILES * R
    INNER = G * P
    SCALE = float(HD) ** -0.5
    W = core.w
    S2 = range(SLOTS)
    with ExitStack() as ctx:
        sb = lambda name, shape: ctx.enter_context(nc.sbuf_tensor(f"a3_{name}", shape, F32))
        ps = lambda name, shape: ctx.enter_context(nc.psum_tensor(f"a3_{name}_ps", shape, F32))
        sem = lambda name: core.keep(nc.semaphore(f"a3_{name}"))
        xs = [sb(f"xs{s}", [P, PADSEQ]) for s in S2]
        qs = [sb(f"qs{s}", [P, SEQ]) for s in S2]
        kt = [sb(f"kt{s}", [P, SEQ]) for s in S2]
        qbd = [sb(f"qbd{s}", [P, ROWS]) for s in S2]
        vs = [sb(f"vs{s}", [HALF, 2, INNER]) for s in S2]
        prob = [sb(f"prob{s}", [R, TILES, PADSEQ]) for s in S2]
        negmax = [sb(f"negmax{s}", [R, TILES]) for s in S2]
        rsum = [sb(f"rsum{s}", [R, TILES]) for s in S2]
        rinv = [sb(f"rinv{s}", [R, TILES]) for s in S2]
        pt = [sb(f"pt{s}", [HALF, 2, ROWS]) for s in S2]
        oc = [sb(f"oc{s}", [P, G, SEQ]) for s in S2]
        qk_ps = [ps(f"qk{s}", [P, 512]) for s in S2]
        v_ps = ps("v", [P, 2, INNER])
        s_ps = [ps(f"s{s}", [P, 512]) for s in S2]
        pt_ps = [ps(f"pt{f}", [P, 512]) for f in range(2)]
        q_at, k_at, o_at = (slice(n * PADSEQ, n * PADSEQ + SEQ) for n in range(3))
        x_made, v_made, v_sb, y_made, half_made, h_made = (
            sem(n) for n in ("x_made", "v_made", "v_sb", "y_made", "half_made", "h_made"))
        qk_made, q_sb, k_sb, qbd_made, s_made, max_made, exp_made, rsum_made, prob_made, pt_made, pt0_sb, pt1_sb, o_made, oc_made = (
            sem(n) for n in ("qk_made", "q_sb", "k_sb", "qbd_made", "s_made", "max_made", "exp_made", "rsum_made",
                             "prob_made", "pt_made", "pt0_sb", "pt1_sb", "o_made", "oc_made"))
        set_up = sem("set_up")
        scores = lambda s: s_ps[s][0:R, 0:TILES * SEQ].rearrange("p (t k) -> p t k", k=SEQ)

        def step(i, g, s):
            return SLOTS * G * i + (SLOTS * g + s)

        with nc.Block() as block:
            @block.gpsimd
            def _(pool):
                for s in S2:
                    pool.memset(qbd[s][:], 0.0).then_inc(set_up, 1)
                    pool.memset(prob[s][:], 0.0).then_inc(set_up, 1)
                    pool.memset(xs[s][:], 0.0).then_inc(set_up, 1)
                pool.wait_ge(set_up, 6)
                with pool.Fori(0, BATCH // SLOTS) as i:
                    for s in S2:
                        b = pool.snap(SLOTS * i + s)
                        pool.wait_ge(h_made, freed(b))
                        pool.tensor_copy(xs[s][:, 0:SEQ], core.normed[:, ds(b * PADSEQ, SEQ)]).then_inc(x_made, 1)
                    for g in range(G):
                        for s in S2:
                            j = pool.snap(step(i, g, s))
                            pool.wait_ge(q_sb, j + 1)
                            pool.wait_ge(s_made, freed(j))
                            pool.tensor_tensor(qbd[s][:].rearrange("p (h q) -> p h q", q=QW)[:, :, 0:SEQ],
                                               qs[s][:].unsqueeze(1).broadcast_to([P, 2, SEQ]),
                                               W["hmask64"][:].unsqueeze(2).broadcast_to([P, 2, SEQ]),
                                               ALU.mult).then_inc(qbd_made, 1)
                        for s in S2:
                            j = pool.snap(step(i, g, s))
                            pool.wait_ge(rsum_made, j + 1)
                            pool.tensor_tensor(prob[s][:, :, 0:SEQ], prob[s][:, :, 0:SEQ],
                                               rinv[s][:].unsqueeze(2).broadcast_to([R, TILES, SEQ]),
                                               ALU.mult).then_inc(prob_made, 1)

            @block.tensor
            def _(pe):
                def projections(i, g, s):
                    j = pe.snap(step(i, g, s))
                    pe.wait_ge(k_sb, freed(j))
                    c = slice(g * P, (g + 1) * P)
                    pe.matmul(qk_ps[s][:, q_at], W["a3_wq"][:, c], xs[s][:, 0:SEQ], start=True, stop=True)
                    pe.matmul(qk_ps[s][:, k_at], W["a3_wk"][:, c], xs[s][:, 0:SEQ], start=True, stop=True).then_inc(qk_made, 1)

                def transposes_and_output(i, g, s):
                    j = pe.snap(step(i, g, s))
                    pe.wait_ge(prob_made, j + 1)
                    for f, emptied in ((0, pt0_sb), (1, pt1_sb)):
                        pe.wait_ge(emptied, j + 1)
                        for t in range(TILES):
                            mm = pe.transpose(pt_ps[f][0:HALF, t * R:(t + 1) * R],
                                              prob[s][:, t, f * HALF:(f + 1) * HALF], W["ident"][0:R, 0:R])
                        mm.then_inc(pt_made, 1)

                def output(i, g, s):
                    j = pe.snap(step(i, g, s))
                    pe.wait_ge(pt0_sb, j + 2)
                    pe.wait_ge(pt1_sb, j + 2)
                    pe.wait_ge(oc_made, freed(j))
                    for h in range(2):
                        for f in range(2):
                            d0 = g * P + h * HD
                            mm = pe.matmul(qk_ps[s][h * HD:(h + 1) * HD, o_at], vs[s][:, f, d0:d0 + HD],
                                           pt[s][:, f, h * QW:h * QW + SEQ], start=(f == 0), stop=(f == 1))
                    mm.then_inc(o_made, 1)

                pe.wait_ge(set_up, 6)
                with pe.Fori(0, BATCH // SLOTS) as i:
                    for s in S2:
                        b = pe.snap(SLOTS * i + s)
                        pe.wait_ge(h_made, freed(b))
                        pe.wait_ge(x_made, b + 1)
                        pe.wait_ge(v_sb, b + 1)
                        for f in range(2):
                            mm = pe.matmul(v_ps[0:HALF, f], xs[s][:, f * HALF:(f + 1) * HALF], W["a3_wv"][:],
                                           start=True, stop=True)
                        mm.then_inc(v_made, 1)
                        projections(i, 0, s)
                    for g in range(G):
                        for s in S2:
                            j = pe.snap(step(i, g, s))
                            pe.wait_ge(k_sb, made(j))
                            pe.wait_ge(qbd_made, j + 1)
                            pe.wait_ge(exp_made, freed(j))
                            for t in range(TILES):
                                mm = pe.matmul(scores(s)[:, t], qbd[s][:, t * R:(t + 1) * R], kt[s][:], start=True, stop=True)
                            mm.then_inc(s_made, 1)
                            if g + 1 < G:
                                projections(i, g + 1, s)
                        for s in S2:
                            transposes_and_output(i, g, s)
                        for s in S2:
                            if g == 0:
                                pe.wait_ge(v_sb, pe.snap(SLOTS * i + (s + 2)))
                            output(i, g, s)
                    for s in S2:
                        j = pe.snap(step(i, G - 1, s))
                        pe.wait_ge(oc_made, made(j))
                        for g in range(G):
                            mm = pe.matmul(qk_ps[s][:, q_at], W["a3_wo"][:, g], oc[s][:, g], start=(g == 0), stop=(g == G - 1))
                        mm.then_inc(y_made, 1)

            @block.scalar
            def _(act):
                with act.Fori(0, BATCH // SLOTS) as i:
                    for g in range(G):
                        for s in S2:
                            j = act.snap(step(i, g, s))
                            act.wait_ge(qk_made, j + 1)
                            act.wait_ge(s_made, freed(j))
                            act.activation(qs[s][:], qk_ps[s][:, q_at], ACT.Copy, scale=SCALE).then_inc(q_sb, 1)
                            act.activation(kt[s][:], qk_ps[s][:, k_at], ACT.Copy).then_inc(k_sb, 1)
                        for s in S2:
                            j = act.snap(step(i, g, s))
                            act.wait_ge(max_made, j + 1)
                            act.wait_ge(pt_made, 2 * j + 2)
                            for t in range(TILES):
                                a = act.activation(prob[s][:, t, 0:SEQ], scores(s)[:, t], ACT.Exp, bias=negmax[s][:, t:t + 1],
                                                   accum_out=rsum[s][:, t:t + 1])
                            a.then_inc(exp_made, 1)
                        for s in S2:
                            j = act.snap(step(i, g, s))
                            act.wait_ge(pt_made, 2 * j + (1 + 2 * SLOTS))
                            act.wait_ge(o_made, freed(j))
                            act.activation(pt[s][:, 0], pt_ps[0][0:HALF, 0:ROWS], ACT.Copy).then_inc(pt0_sb, 1)
                        for s in S2:
                            j = act.snap(step(i, g, s))
                            act.wait_ge(o_made, made(j))
                            act.activation(oc[s][:, g], qk_ps[s][:, o_at], ACT.Copy).then_inc(oc_made, 1)

            @block.vector
            def _(ve):
                ve.sem_inc(h_made, SLOTS)
                ve.sem_inc(exp_made, SLOTS)
                ve.sem_inc(pt_made, 2 * SLOTS)
                for c in (pt0_sb, pt1_sb, v_sb):
                    ve.sem_inc(c, 1)
                for c in (k_sb, s_made, oc_made, o_made):
                    ve.sem_inc(c, SLOTS)
                with ve.Fori(0, BATCH // SLOTS) as i:
                    for s in S2:
                        b = ve.snap(SLOTS * i + s)
                        ve.wait_ge(v_made, b + 1)
                        ve.tensor_copy(vs[s][:], v_ps[0:HALF]).then_inc(v_sb, 1)
                    for g in range(G):
                        for s in S2:
                            j = ve.snap(step(i, g, s))
                            ve.wait_ge(s_made, made(j))
                            ve.tensor_reduce(negmax[s][:], scores(s), AX.X, ALU.max, negate=True).then_inc(max_made, 1)
                        for s in S2:
                            j = ve.snap(step(i, g, s))
                            ve.wait_ge(exp_made, made(j))
                            ve.reciprocal(rinv[s][:], rsum[s][:]).then_inc(rsum_made, 1)
                        for s in S2:
                            j = ve.snap(step(i, g, s))
                            ve.wait_ge(pt_made, 2 * j + (2 + 2 * SLOTS))
                            ve.wait_ge(o_made, freed(j))
                            ve.tensor_copy(pt[s][:, 1], pt_ps[1][0:HALF, 0:ROWS]).then_inc(pt1_sb, 1)
                    for s in S2:
                        b = ve.snap(SLOTS * i + s)
                        h_b = core.h[:, ds(b * SEQ, SEQ)]
                        ve.wait_ge(y_made, b + 1)
                        ve.tensor_tensor(h_b, h_b, xs[s][:, 0:SEQ], ALU.add).then_inc(half_made, 1)
                        ve.wait_ge(half_made, b + 1)
                        ve.tensor_tensor(h_b, h_b, qk_ps[s][:, q_at], ALU.add).then_inc(h_made, 1)


def gated_expert(nc, core):
    EXPERTS = 16
    W = core.w
    S2 = range(SLOTS)
    with ExitStack() as ctx:
        sb = lambda name, shape, dt=F32: ctx.enter_context(nc.sbuf_tensor(f"f3_{name}", shape, dt))
        ps = lambda name, shape: ctx.enter_context(nc.psum_tensor(f"f3_{name}_ps", shape, F32))
        sem = lambda name: core.keep(nc.semaphore(f"f3_{name}"))
        mean = sb("mean", [P, BATCH])
        ones = sb("ones", [BATCH, P])
        logit = sb("logit", [BATCH, EXPERTS])
        ranked = sb("ranked", [BATCH, 8])
        which = sb("which", [BATCH, 8], U32)
        neg_top = sb("neg_top", [BATCH, 1])
        term = sb("term", [BATCH, EXPERTS])
        total = sb("total", [BATCH, 1])
        gate = sb("gate", [BATCH, 1])
        which_f = sb("which_f", [BATCH, 1])
        chosen = sb("chosen", [BATCH, EXPERTS])
        gate_diag = sb("gate_diag", [BATCH, BATCH])
        chosen_t = sb("chosen_t", [EXPERTS, BATCH])
        which_row = sb("which_row", [1, BATCH], I32)
        gates = sb("gates", [P, BATCH])
        biases = sb("biases", [P, BATCH])
        w_sel = [sb(f"w_sel{s}", [P, P]) for s in S2]
        small_ps = ps("small", [P, 512])
        y_ps = [ps(f"y{s}", [P, 512]) for s in S2]
        v, pe_, a_ = (sem(n) for n in ("route", "route_pe", "route_act"))
        w_made, y_made, h_made = (sem(n) for n in ("w_made", "y_made", "h_made"))
        res = core.h[:, 0:TOK].rearrange("p (b n) -> p b n", n=SEQ)

        with nc.Block() as block:
            @block.tensor
            def _(pe):
                pe.wait_ge(v, 3)
                pe.matmul(small_ps[0:BATCH, 0:EXPERTS], mean[:], W["f3_wg"][:], start=True, stop=True).then_inc(pe_, 1)
                pe.wait_ge(v, 11)
                pe.transpose(small_ps[0:EXPERTS, 32:32 + BATCH], chosen[:], W["ident"][0:BATCH, 0:BATCH])
                pe.transpose(small_ps[0:1, 64:64 + BATCH], which_f[:], W["ident"][0:BATCH, 0:BATCH])
                pe.matmul(small_ps[:, 96:96 + BATCH], ones[:], gate_diag[:], start=True, stop=True).then_inc(pe_, 1)
                pe.wait_ge(v, 14)
                pe.matmul(small_ps[:, 128:128 + BATCH], W["f3_be"][:], chosen_t[:], start=True, stop=True).then_inc(pe_, 1)
                with pe.Fori(0, BATCH // SLOTS) as i:
                    for s in S2:
                        b = pe.snap(SLOTS * i + s)
                        pe.wait_ge(w_made, b + 1)
                        pe.wait_ge(h_made, freed(b))
                        pe.matmul(y_ps[s][:, 0:SEQ], w_sel[s][:], core.normed[:, ds(b * SEQ, SEQ)],
                                  start=True, stop=True).then_inc(y_made, 1)

            @block.scalar
            def _(act):
                act.wait_ge(v, 7)
                act.activation(term[:], logit[:], ACT.Exp, bias=neg_top[:, 0:1], accum_out=total[:, 0:1]).then_inc(a_, 1)

            @block.gpsimd
            def _(pool):
                pool.wait_ge(v, 13)
                with pool.Fori(0, BATCH // SLOTS) as i:
                    for s in S2:
                        b = pool.snap(SLOTS * i + s)
                        e = pool.value_load(which_row[0:1, ds(b, 1)], min_val=0, max_val=EXPERTS - 1)
                        pool.wait_ge(y_made, freed(b))
                        pool.tensor_tensor(w_sel[s][:], W["f3_we"][:, ds(e * P, P)],
                                           gates[:, ds(b, 1)].broadcast_to([P, P]), ALU.mult).then_inc(w_made, 1)

            @block.vector
            def _(ve):
                ve.sem_inc(y_made, SLOTS)
                ve.sem_inc(h_made, SLOTS)
                ve.memset(ones[:], 1.0).then_inc(v, 1)
                ve.tensor_reduce(mean[:], core.normed[:, 0:TOK].rearrange("p (b n) -> p b n", n=SEQ), AX.X, ALU.add).then_inc(v, 1)
                ve.wait_ge(v, 2)
                ve.tensor_scalar(mean[:], mean[:], 1.0 / SEQ, None, ALU.mult).then_inc(v, 1)
                ve.wait_ge(pe_, 1)
                ve.tensor_tensor(logit[:], small_ps[0:BATCH, 0:EXPERTS], W["f3_bg"][:], ALU.add).then_inc(v, 1)
                ve.wait_ge(v, 4)
                ve.max(ranked[:], logit[:]).then_inc(v, 1)
                ve.wait_ge(v, 5)
                ve.max_index(which[:], ranked[:], logit[:]).then_inc(v, 1)
                ve.tensor_scalar(neg_top[:], ranked[:, 0:1], -1.0, None, ALU.mult).then_inc(v, 1)
                ve.wait_ge(v, 6)
                ve.tensor_copy(which_f[:], which[:, 0:1]).then_inc(v, 1)
                ve.wait_ge(a_, 1)
                ve.reciprocal(gate[:], total[:]).then_inc(v, 1)
                ve.wait_ge(v, 9)
                ve.tensor_scalar(chosen[:], W["f3_numbers"][:], which_f[:, 0:1], gate[:, 0:1], ALU.is_equal, ALU.mult).then_inc(v, 1)
                ve.tensor_scalar(gate_diag[:], W["ident"][0:BATCH, 0:BATCH], gate[:, 0:1], None, ALU.mult).then_inc(v, 1)
                ve.wait_ge(pe_, 2)
                ve.tensor_copy(gates[:], small_ps[:, 96:96 + BATCH]).then_inc(v, 1)
                ve.tensor_copy(which_row[:], small_ps[0:1, 64:64 + BATCH]).then_inc(v, 1)
                ve.tensor_copy(chosen_t[:], small_ps[0:EXPERTS, 32:32 + BATCH]).then_inc(v, 1)
                ve.wait_ge(pe_, 3)
                ve.tensor_copy(biases[:], small_ps[:, 128:128 + BATCH]).then_inc(v, 1)
                ve.wait_ge(v, 15)
                ve.tensor_tensor(res, res, biases[:].unsqueeze(2).broadcast_to([P, BATCH, SEQ]), ALU.add).then_inc(v, 1)
                ve.wait_ge(v, 16)
                with ve.Fori(0, BATCH // SLOTS) as i:
                    for s in S2:
                        b = ve.snap(SLOTS * i + s)
                        ve.wait_ge(y_made, made(b))
                        h_b = core.h[:, ds(b * SEQ, SEQ)]
                        ve.tensor_tensor(h_b, h_b, y_ps[s][:, 0:SEQ], ALU.add).then_inc(h_made, 1)


def store_output(nc, core, out):
    with nc.semaphore("stored") as stored, nc.Block() as block:
        @block.sync
        def _(sp):
            for q in range(4):
                sp.dma_start(out[:, q * TOK // 4:(q + 1) * TOK // 4], core.h[:, q * TOK // 4:(q + 1) * TOK // 4]).then_inc(stored, 16)
            sp.wait_ge(stored, 64)


def build(nc, dram, shapes, out, stop=8):
    with ExitStack() as ctx:
        core = Core()
        core.keep = ctx.enter_context
        core.norms = 0
        core.norm_sems = [core.keep(nc.semaphore("ln_" + n)) for n in
                          ("mean_made", "cent_made", "sq_made", "var_made", "std_made", "rstd_made", "normed_made")]
        core.h = ctx.enter_context(nc.sbuf_tensor("h", [P, TOKPAD], F32))
        core.normed = ctx.enter_context(nc.sbuf_tensor("normed", [P, TOKPAD], F32))
        core.mean_mat = ctx.enter_context(nc.sbuf_tensor("mean_mat", [P, P], F32))
        core.eps = ctx.enter_context(nc.sbuf_tensor("eps", [P, 1], F32))
        core.weights_in = ctx.enter_context(nc.semaphore("weights_in"))
        core.weight_names = [n for n in shapes if n not in BLOCK_OWN]
        core.n_weights = len(core.weight_names)
        core.w = {n: ctx.enter_context(nc.sbuf_tensor("w_" + n, list(shapes[n]), F32)) for n in core.weight_names}
        with nc.Block() as block:
            @block.vector
            def _(ve):
                ve.memset(core.mean_mat[:], 1.0 / P)
                ve.memset(core.eps[:], EPS)
                ve.memset(core.h[:, TOK:TOKPAD], 0.0)
                ve.memset(core.normed[:], 0.0)
        padded = core.normed[:, 0:BATCH * PADSEQ].rearrange("p (b n) -> p b n", n=PADSEQ)
        padded_out = lambda n: padded[:, ds(2 * n, 2), 0:SEQ]
        flat = core.normed[:, 0:TOK].rearrange("p (b n) -> p b n", n=SEQ)
        flat_out = lambda n: flat[:, ds(2 * n, 2), :]
        tokens_of_patches(nc, core, dram)
        layernorm(nc, core, "a0_ln", padded_out)
        narrow_attention(nc, core, "a0", projected=False, top_k=False, conv=False)
        layernorm(nc, core, "m_ln", flat_out)
        routed_experts(nc, core, dram)
        layernorm(nc, core, "a1_ln", flat_out)
        head_mixing(nc, core)
        window_projection(nc, core)
        layernorm(nc, core, "f1_ln", flat_out)
        trig_ffn(nc, core)
        layernorm(nc, core, "a2_ln", padded_out)
        decay_retrieval(nc, core)
        layernorm(nc, core, "f2_ln", padded_out)
        narrow_attention(nc, core, "f2", projected=True, top_k=True, conv=True)
        layernorm(nc, core, "a3_ln", padded_out)
        wide_attention(nc, core)
        layernorm(nc, core, "f3_ln", flat_out)
        gated_expert(nc, core)
        store_output(nc, core, out)


BLOCK_OWN = {"x", "txt", "w0", "w1", "sw0", "sw1", "eo0", "eo1", "eps0", "eps1", "bias0", "bias1", "w3", "b3", "pe",
             "expert_rows", "expert_ids", "m_w1", "m_w2"}


def lay_out(np, a):
    c = np.ascontiguousarray
    blocks = lambda m: m.reshape(m.shape[0] // P, P, -1).transpose(1, 0, 2)
    col = lambda v: v.reshape(-1, P).T
    x = a["x"].reshape(BATCH, 8, 16, 8, 16).transpose(0, 1, 3, 2, 4).reshape(BATCH * PATCHES, 256)
    pos = np.arange(PATCHES, dtype=np.float32)[:, None]
    div = np.exp(np.arange(0, P, 2, dtype=np.float32) * np.float32(-np.log(10000.0) / P))
    ang = (pos * div).astype(np.float32)
    pe = np.stack([np.sin(ang), np.cos(ang)], axis=-1).reshape(PATCHES, P).astype(np.float32)
    d = {"x": blocks(x.T), "txt": a["txt"].transpose(2, 0, 1), "pe": pe.T}
    for l, name in enumerate(("W1", "W2")):
        t = f"L0_tok_{name}"
        d[f"w{l}"] = blocks(a[t + "_w"].T)
        d[f"sw{l}"] = blocks(a[t + "_sw"].T)
        d[f"eo{l}"] = a[f"L0_tok_eps_out{l + 1}"]
        d[f"eps{l}"] = np.concatenate([col(a[f"L0_tok_eps_in{l + 1}"]), col(a[f"L0_tok_eps_out{l + 1}"])], axis=1)
        d[f"bias{l}"] = np.stack([a[t + "_b"], a[t + "_sb"]], axis=1)
    d["w3"] = a["L0_tok_W3_w"].T
    d["b3"] = a["L0_tok_W3_b"][:, None]
    d["hmask16"] = np.repeat(np.eye(8, dtype=np.float32), 16, axis=0)
    d["ident"] = np.eye(P, dtype=np.float32)
    d["a0_wq"], d["a0_wk"], d["a0_wv"] = a["L0_attn_Wq"].T, a["L0_attn_Wk"].T, a["L0_attn_Wk"].T
    d["a0_bq"], d["a0_bk"], d["a0_bv"] = (a["L0_attn_" + n][:, None] for n in ("bq", "bk", "bk"))
    d["expert_ids"], d["expert_rows"] = a["L0_ffn_expert_indices"].T, a["L0_ffn_expert_weights"].T
    d["m_w1"] = a["L0_ffn_w1"]
    d["m_w2"] = a["L0_ffn_w2"].reshape(8, 4, P, P).transpose(0, 2, 1, 3)
    d["ident"] = np.eye(P, dtype=np.float32)
    d["hmask16"] = np.repeat(np.eye(8, dtype=np.float32), 16, axis=0)
    d["a1_wqkv"], d["wp_b"] = a["L1_attn_w_qkv"].T, a["L1_attn_b_proj"][:, None]
    d["wp_w"] = np.tile(a["L1_attn_w_proj"].reshape(P, 8, 16).transpose(2, 1, 0), (8, 1, 1))
    d["f1_w"], d["f1_b"] = a["L1_ffn_W"].T, a["L1_ffn_B_param"].T
    d["f1_attn_cos"], d["f1_attn_sin"] = a["L1_ffn_attn_cos"].T, a["L1_ffn_attn_sin"].T
    proj = np.stack([a["L1_ffn_proj_cos_w"].T, a["L1_ffn_proj_sin_w"].T])
    d["f1_proj"] = proj.reshape(2, 16, 4, P).transpose(2, 0, 1, 3).reshape(P, P)
    d["a2_basis"], d["a2_vc"], d["a2_oc"] = (a["L2_attn_" + n].T for n in ("basis", "v_coeffs", "o_coeffs"))
    d["a2_wq"], d["a2_wk"] = a["L2_attn_shared_q_w"], a["L2_attn_shared_k_w"]
    d["a2_decay"] = np.broadcast_to(a["L2_attn_decay_logits"], (P, 4))
    d["a2_out_scale"] = np.broadcast_to(a["L2_attn_out_scale"], (P, 1))
    after = (np.arange(71)[:, None, None] + 71 * np.arange(2)[None, :, None]) - np.arange(SEQ)[None, None, :]
    d["a2_distance"] = np.maximum(after - 1, 0).astype(np.float32)
    d["a2_later"] = ((after > 0) & (after - 1 < SEQ)).astype(np.float32)
    d["hmask16"] = np.repeat(np.eye(8, dtype=np.float32), 16, axis=0)
    d["ident"] = np.eye(P, dtype=np.float32)
    for n, m in enumerate("qkv"):
        d["f2_w" + m] = a["L2_ffn_qkv_w"][n * P:(n + 1) * P].T
        d["f2_b" + m] = a["L2_ffn_qkv_b"][n * P:(n + 1) * P, None]
    d["f2_wo"], d["f2_bo"] = a["L2_ffn_wo_w"].T, a["L2_ffn_wo_b"][:, None]
    d["f2_pos_w"], d["f2_pos_b"] = a["L2_ffn_pos_w"][:, 0], a["L2_ffn_pos_b"][:, None]
    d["hmask64"] = np.repeat(np.eye(2, dtype=np.float32), 64, axis=0)
    d["ident"] = np.eye(P, dtype=np.float32)
    d["a3_wq"], d["a3_wk"], d["a3_wv"] = (a["L3_attn_" + n].T for n in ("Wq", "Wk", "Wv"))
    d["a3_wo"] = a["L3_attn_Wo"].T.reshape(4, P, P).transpose(1, 0, 2)
    d["ident"] = np.eye(P, dtype=np.float32)
    d["f3_wg"], d["f3_be"] = a["L3_ffn_Wg"], a["L3_ffn_be"]
    d["f3_bg"] = np.broadcast_to(a["L3_ffn_bg"], (BATCH, 16))
    d["f3_numbers"] = np.broadcast_to(np.arange(16, dtype=np.float32), (BATCH, 16))
    d["f3_we"] = a["L3_ffn_We"].transpose(1, 0, 2).reshape(P, 16 * P)
    return {k: c(v) for k, v in d.items()}


def kernel(**inputs):
    import numpy as _np
    import concourse.bacc as _bacc
    from concourse import mybir as _mybir
    from concourse.bass_utils import run_bass_kernel_spmd as _run

    arrays = lay_out(_np, {k: _np.asarray(v) for k, v in inputs.items()})
    nc = _bacc.Bacc("TRN2", target_bir_lowering=False, num_devices=1)
    dram = {k: nc.dram_tensor("in_" + k, list(v.shape), _mybir.dt.from_np(v.dtype), kind="ExternalInput").ap()
            for k, v in arrays.items()}
    out = nc.dram_tensor("out_h", [P, TOK], _mybir.dt.float32, kind="ExternalOutput").ap()
    build(nc, dram, {k: v.shape for k, v in arrays.items()}, out)
    r = _run(nc, [{"in_" + k: v for k, v in arrays.items()}], core_ids=[0])
    return _np.ascontiguousarray(r.results[0]["out_h"].reshape(P, BATCH, SEQ).transpose(1, 2, 0))
```

```python
import math
from contextlib import ExitStack

import concourse.bass as bass
from concourse import mybir

F32 = mybir.dt.float32
I32 = mybir.dt.int32
U32 = mybir.dt.uint32
I16 = mybir.dt.int16
ALU = mybir.AluOpType
ACT = mybir.ActivationFunctionType
AX = mybir.AxisListType

P = 128
BATCH = 32
PATCHES = 64
TEXT = 77
SEQ = PATCHES + TEXT
TOK = BATCH * SEQ
HALF = 71
PADSEQ = 2 * HALF
CHUNK = 512
TOKPAD = -(-TOK // CHUNK) * CHUNK
EPS = 1e-5
SLOTS = 2
GONE = -3.0e38


def made(n, slots=SLOTS):
    return n + (1 + slots)


def freed(n):
    return n + 1


class Core:
    pass


def ds(start, size):
    return bass.ds(start, size)


def tokens_of_patches(nc, core, dram):
    with ExitStack() as ctx:
        sb = lambda name, shape, dt=F32: ctx.enter_context(nc.sbuf_tensor("tok_" + name, shape, dt))
        ps = lambda name, shape: ctx.enter_context(nc.psum_tensor("tok_" + name, shape, F32))
        sem = lambda name: core.keep(nc.semaphore("tok_" + name))
        GB = 8
        CH = BATCH // GB
        w = sb("w", [P, 2, 2, P])
        sw = sb("sw", [P, 2, 2, P])
        eo_row = sb("eo_row", [P, 2, P])
        eps_col = sb("eps_col", [P, 2, 3])
        bias = sb("bias", [P, 2, 2])
        b3 = sb("b3", [P, 1])
        w3 = sb("w3", [P, P])
        pe_tab = sb("pe", [P, PATCHES])
        x = [sb(f"x{s}", [P, 2, CHUNK]) for s in range(2)]
        t_row = sb("t_row", [P, 2, P])
        t_col = sb("t_col", [P, 2, 3])
        s_row = sb("s_row", [P, 2, P])
        s_col = sb("s_col", [P, 2, 3])
        noise = sb("noise", [P, 2, 2, P])
        bn = sb("bn", [P, 2])
        gate = [sb(f"gate{s}", [P, CHUNK]) for s in range(2)]
        inner = [sb(f"inner{s}", [P, CHUNK]) for s in range(2)]
        u = [sb(f"u{s}", [P, CHUNK]) for s in range(2)]
        v = [sb(f"v{s}", [P, CHUNK]) for s in range(2)]
        g_ps = [ps(f"g{s}", [P, CHUNK]) for s in range(2)]
        i_ps = [ps(f"i{s}", [P, CHUNK]) for s in range(2)]
        y_ps = [ps(f"y{s}", [P, CHUNK]) for s in range(2)]
        small_in = sem("small_in")
        x_in = [sem(f"x_in{s}") for s in range(2)]
        text_in = sem("text_in")
        root = sem("root")
        prep = sem("prep")
        prepared = sem("prepared")
        gate_ready = sem("gate_ready")
        proj = sem("proj")
        act_done = sem("act_done")
        dve = sem("dve")
        mixed = sem("mixed")
        y_ready = sem("y_ready")
        SMALL = 13

        with nc.Block() as block:
            @block.sync
            def _(sp):
                for l in range(2):
                    sp.dma_start(w[:, l], dram[f"w{l}"]).then_inc(small_in, 16)
                    sp.dma_start(sw[:, l], dram[f"sw{l}"]).then_inc(small_in, 16)
                    sp.dma_start(eo_row[:, l], dram[f"eo{l}"].partition_broadcast(P)).then_inc(small_in, 16)
                    sp.dma_start(eps_col[:, l], dram[f"eps{l}"]).then_inc(small_in, 16)
                    sp.dma_start(bias[:, l], dram[f"bias{l}"]).then_inc(small_in, 16)
                sp.dma_start(w3[:], dram["w3"]).then_inc(small_in, 16)
                sp.dma_start(b3[:], dram["b3"]).then_inc(small_in, 16)
                sp.dma_start(pe_tab[:], dram["pe"]).then_inc(small_in, 16)
                for c in range(CH):
                    if c >= 2:
                        sp.wait_ge(proj, c - 1)
                    sp.dma_start(x[c % 2][:], dram["x"][:, :, c * CHUNK:(c + 1) * CHUNK]).then_inc(x_in[c % 2], 16)

            @block.gpsimd
            def _(pool):
                pool.dma_start(core.h[:, 0:TOK].rearrange("p (b n) -> p b n", n=SEQ)[:, :, PATCHES:SEQ],
                               dram["txt"]).then_inc(text_in, 16)
                pool.wait_ge(text_in, 16)
                pool.wait_ge(core.weights_in, 16 * core.n_weights)

            @block.scalar
            def _(act):
                for name in core.weight_names:
                    act.dma_start(core.w[name][:], dram[name]).then_inc(core.weights_in, 16)
                act.wait_ge(prep, 2)
                act.activation(s_row[:], t_row[:], ACT.Sqrt).then_inc(root, 1)
                act.activation(s_col[:], t_col[:], ACT.Sqrt).then_inc(root, 1)
                act.wait_ge(prepared, 1)
                for c in range(CH):
                    s = c % 2
                    act.wait_ge(proj, c + 1)
                    if c >= 2:
                        act.wait_ge(mixed, c - 1)
                    act.activation(gate[s][:], g_ps[s][:], ACT.Identity, bias=bn[:, 0:1]).then_inc(gate_ready, 1)
                    act.activation(inner[s][:], i_ps[s][:], ACT.Identity, bias=bn[:, 1:2]).then_inc(act_done, 1)
                    act.wait_ge(dve, 5 * c + 1)
                    act.activation(u[s][:], v[s][:], ACT.Exp).then_inc(act_done, 1)

            @block.tensor
            def _(pe):
                pe.wait_ge(prepared, 1)
                for c in range(CH):
                    s = c % 2
                    pe.wait_ge(x_in[s], 16 * (c // 2 + 1))
                    if c >= 2:
                        pe.wait_ge(act_done, 2 * (c - 1))
                    for l, out in ((0, g_ps[s]), (1, i_ps[s])):
                        for k in range(2):
                            mm = pe.matmul(out[:], noise[:, l, k], x[s][:, k], start=(k == 0), stop=(k == 1))
                    mm.then_inc(proj, 1)
                    if c >= 2:
                        pe.wait_ge(y_ready, 2 * (c - 1))
                    pe.wait_ge(mixed, c + 1)
                    pe.matmul(y_ps[s][:], w3[:], gate[s][:], start=True, stop=True).then_inc(y_ready, 1)

            @block.vector
            def _(ve):
                ve.wait_ge(small_in, 16 * SMALL)
                ve.scalar_tensor_tensor(t_row[:], eo_row[:], -1.0, eo_row[:], ALU.mult, ALU.max).then_inc(prep, 1)
                ve.scalar_tensor_tensor(t_col[:], eps_col[:], -1.0, eps_col[:], ALU.mult, ALU.max).then_inc(prep, 1)
                ve.wait_ge(root, 2)
                ve.tensor_scalar(t_row[:], eo_row[:], 0.0, 2.0, ALU.is_ge, ALU.mult).then_inc(prep, 1)
                ve.tensor_scalar(t_col[:], eps_col[:], 0.0, 2.0, ALU.is_ge, ALU.mult).then_inc(prep, 1)
                ve.wait_ge(prep, 4)
                ve.scalar_tensor_tensor(s_row[:], t_row[:], -1.0, s_row[:], ALU.add, ALU.mult).then_inc(prep, 1)
                ve.scalar_tensor_tensor(s_col[:], t_col[:], -1.0, s_col[:], ALU.add, ALU.mult).then_inc(prep, 1)
                ve.wait_ge(prep, 6)
                for l in range(2):
                    for k in range(2):
                        ve.scalar_tensor_tensor(noise[:, l, k], s_row[:, l], s_col[:, l, k:k + 1], sw[:, l, k],
                                                ALU.mult, ALU.mult).then_inc(prep, 1)
                    ve.tensor_tensor(bn[:, l:l + 1], bias[:, l, 1:2], s_col[:, l, 2:3], ALU.mult).then_inc(prep, 1)
                ve.wait_ge(prep, 12)
                ve.tensor_tensor(noise[:], noise[:], w[:], ALU.add).then_inc(prep, 1)
                ve.tensor_tensor(bn[:], bn[:], bias[:, :, 0], ALU.add).then_inc(prep, 1)
                ve.wait_ge(prep, 14)
                ve.sem_inc(prepared, 1)
                for c in range(CH):
                    s = c % 2
                    ve.wait_ge(gate_ready, c + 1)
                    ve.tensor_scalar(v[s][:], gate[s][:], 20.0, None, ALU.min).then_inc(dve, 1)
                    ve.wait_ge(act_done, 2 * c + 2)
                    ve.scalar_tensor_tensor(v[s][:], u[s][:], 2.0, u[s][:], ALU.add, ALU.mult).then_inc(dve, 1)
                    ve.wait_ge(dve, 5 * c + 2)
                    ve.tensor_scalar(u[s][:], v[s][:], 2.0, None, ALU.add).then_inc(dve, 1)
                    ve.wait_ge(dve, 5 * c + 3)
                    ve.tensor_tensor(v[s][:], v[s][:], inner[s][:], ALU.mult).then_inc(dve, 1)
                    ve.reciprocal(u[s][:], u[s][:]).then_inc(dve, 1)
                    ve.wait_ge(dve, 5 * c + 4)
                    ve.tensor_tensor(gate[s][:], gate[s][:], v[s][:], ALU.mult).then_inc(prep, 1)
                    ve.wait_ge(dve, 5 * c + 5)
                    ve.wait_ge(prep, 15 + 2 * c)
                    ve.tensor_tensor(gate[s][:], gate[s][:], u[s][:], ALU.mult).then_inc(mixed, 1)
                    ve.wait_ge(y_ready, 2 * c + 1)
                    ve.scalar_tensor_tensor(u[s][:], y_ps[s][:], b3[:, 0:1],
                                            pe_tab[:].unsqueeze(1).broadcast_to([P, GB, PATCHES]), ALU.add, ALU.add).then_inc(prep, 1)
                    ve.wait_ge(prep, 16 + 2 * c)
                    ve.tensor_copy(core.h[:, 0:TOK].rearrange("p (b n) -> p b n", n=SEQ)[:, c * GB:(c + 1) * GB, 0:PATCHES],
                                   u[s][:].rearrange("p (b n) -> p b n", n=PATCHES)).then_inc(y_ready, 1)


def layernorm(nc, core, tag, out_ap):
    N = 2 * SEQ
    PAIRS = 4
    UNITS = TOK // (N * PAIRS)
    ROWS = P // PAIRS
    with ExitStack() as ctx:
        sb = lambda name, shape: ctx.enter_context(nc.sbuf_tensor(f"{tag}_{name}", shape, F32))
        ps = lambda name, shape: ctx.enter_context(nc.psum_tensor(f"{tag}_{name}_ps", shape, F32))
        cent = [sb(f"cent{u}", [P, PAIRS, N]) for u in range(UNITS)]
        sq = [sb(f"sq{s}", [P, PAIRS, N]) for s in range(2)]
        std = [sb(f"std{u}", [P, N]) for u in range(UNITS)]
        mean_ps = [ps(f"mean{s}", [P, 512]) for s in range(2)]
        var_ps = [ps(f"var{s}", [P, 512]) for s in range(2)]
        rstd_ps = [ps(f"rstd{k}", [P, 512]) for k in range(PAIRS)]
        mean_made, cent_made, sq_act, sq_pool, var_made, std_made, rstd_made, spread_made, normed_made = core.norm_sems
        unit0 = UNITS * core.norms
        pair0 = PAIRS * unit0
        core.norms += 1

        with nc.Block() as block:
            @block.tensor
            def _(pe):
                def means(u):
                    for k in range(PAIRS):
                        n = PAIRS * u + k
                        if n >= 2:
                            pe.wait_ge(cent_made, pair0 + n - 1)
                        pe.matmul(mean_ps[k % 2][:, 0:N], core.mean_mat[:], core.h[:, n * N:(n + 1) * N],
                                  start=True, stop=True).then_inc(mean_made, 1)

                def variances(u):
                    pe.wait_ge(sq_act, 2 * (unit0 + u + 1))
                    pe.wait_ge(sq_pool, 2 * (unit0 + u + 1))
                    if u >= 2:
                        pe.wait_ge(std_made, unit0 + u - 1)
                    for k in range(PAIRS):
                        mm = pe.matmul(var_ps[u % 2][k * ROWS:(k + 1) * ROWS, 0:N], core.mean_mat[:, 0:ROWS], sq[u % 2][:, k],
                                       start=True, stop=True)
                    mm.then_inc(var_made, 1)

                def spread(u):
                    pe.wait_ge(rstd_made, unit0 + u + 1)
                    if u:
                        pe.wait_ge(normed_made, pair0 + PAIRS * u)
                    for k in range(PAIRS):
                        rows = slice(k * ROWS, (k + 1) * ROWS)
                        mm = pe.matmul(rstd_ps[k][:, 0:N], core.first_row[rows, :], std[u][rows, :], start=True, stop=True)
                    mm.then_inc(spread_made, 1)

                means(0)
                means(1)
                variances(0)
                for u in range(2, UNITS):
                    means(u)
                    spread(u - 2)
                    variances(u - 1)
                spread(UNITS - 2)
                variances(UNITS - 1)
                spread(UNITS - 1)

            def squares(u, eng, first, counted, square):
                for k in range(first, PAIRS, 2):
                    eng.wait_ge(cent_made, pair0 + PAIRS * u + k + 1)
                    if u >= 2:
                        eng.wait_ge(var_made, unit0 + u - 1)
                    square(sq[u % 2][:, k], cent[u][:, k]).then_inc(counted, 1)

            @block.gpsimd
            def _(pool):
                for u in range(UNITS):
                    squares(u, pool, 1, sq_pool, lambda out, x: pool.tensor_tensor(out, x, x, ALU.mult))

            @block.scalar
            def _(act):
                def root(u):
                    act.wait_ge(var_made, unit0 + u + 1)
                    act.activation(std[u][:], var_ps[u % 2][:, 0:N], ACT.Sqrt, bias=core.eps[:, 0:1]).then_inc(std_made, 1)

                for u in range(UNITS):
                    squares(u, act, 0, sq_act, lambda out, x: act.activation(out, x, ACT.Square))
                    if u:
                        root(u - 1)
                root(UNITS - 1)

            @block.vector
            def _(ve):
                def centre(u):
                    for k in range(PAIRS):
                        n = PAIRS * u + k
                        ve.wait_ge(mean_made, pair0 + n + 1)
                        ve.tensor_tensor(cent[u][:, k], core.h[:, n * N:(n + 1) * N], mean_ps[k % 2][:, 0:N],
                                         ALU.subtract).then_inc(cent_made, 1)

                def reciprocal(u):
                    ve.wait_ge(std_made, unit0 + u + 1)
                    ve.reciprocal(std[u][:], std[u][:]).then_inc(rstd_made, 1)

                def scale(u):
                    ve.wait_ge(spread_made, unit0 + u + 1)
                    for k in range(PAIRS):
                        ve.tensor_tensor(out_ap(PAIRS * u + k), cent[u][:, k].rearrange("p (b n) -> p b n", n=SEQ),
                                         rstd_ps[k][:, 0:N].rearrange("p (b n) -> p b n", n=SEQ), ALU.mult).then_inc(normed_made, 1)

                centre(0)
                centre(1)
                for u in range(2, UNITS):
                    reciprocal(u - 2)
                    centre(u)
                    scale(u - 2)
                for u in range(UNITS - 2, UNITS):
                    reciprocal(u)
                    scale(u)


def project_heads(nc, core, tag, conv, q_all, k_all, v_all):
    SCALE = float(P) ** -0.5
    W = core.w
    N = 2 * SEQ
    PAIRS = BATCH // 2
    S2 = range(SLOTS)
    with ExitStack() as ctx:
        sb = lambda name, shape: ctx.enter_context(nc.sbuf_tensor(f"{tag}p_{name}", shape, F32))
        ps = lambda name, shape: ctx.enter_context(nc.psum_tensor(f"{tag}p_{name}_ps", shape, F32))
        padded = core.normed[:, 0:BATCH * PADSEQ].rearrange("p (b n) -> p b n", n=PADSEQ)
        xs = [sb(f"xs{s}", [P, 2, PADSEQ]) for s in S2]
        bqs = sb("bqs", [P, 1])
        q_ps = [ps(f"q{s}", [P, 512]) for s in S2]
        k_ps = [ps(f"k{s}", [P, 512]) for s in S2]
        v_ps = [ps(f"v{s}", [P, 2, 2, P]) for s in S2]
        bqs_made, conv_step, x_made, qk_made, v_made, q_sb, k_sb, v_sb = core.project_sems
        pair0 = PAIRS * core.projections
        one0 = core.projections
        core.projections += 1
        if conv:
            xc = sb("xc", [P, BATCH, PADSEQ])
            with nc.Block() as block:
                @block.vector
                def _(ve):
                    cw = W[tag + "_pos_w"]
                    x, y = padded[:, :, 0:SEQ], xc[:, :, 0:SEQ]
                    ve.memset(xc[:, :, SEQ:PADSEQ], 0.0)
                    ve.tensor_scalar(y, x, cw[:, 1:2], W[tag + "_pos_b"][:, 0:1], ALU.mult, ALU.add).then_inc(conv_step, 1)
                    ve.wait_ge(conv_step, 1)
                    ve.scalar_tensor_tensor(xc[:, :, 1:SEQ], padded[:, :, 0:SEQ - 1], cw[:, 0:1], xc[:, :, 1:SEQ],
                                            ALU.mult, ALU.add).then_inc(conv_step, 1)
                    ve.wait_ge(conv_step, 2)
                    ve.scalar_tensor_tensor(xc[:, :, 0:SEQ - 1], padded[:, :, 1:SEQ], cw[:, 2:3], xc[:, :, 0:SEQ - 1],
                                            ALU.mult, ALU.add).then_inc(conv_step, 1)
                    ve.wait_ge(conv_step, 3)
                    ve.tensor_tensor(y, y, x, ALU.add).then_inc(conv_step, 1)
            source = xc[:]
        else:
            source = padded

        with nc.Block() as block:
            @block.gpsimd
            def _(pool):
                for s in S2:
                    pool.memset(xs[s][:], 0.0).then_inc(x_made, 1)
                pool.wait_ge(x_made, pair0 + SLOTS * one0 + SLOTS)
                with pool.Fori(0, PAIRS // SLOTS) as i:
                    for s in S2:
                        n = pool.snap(SLOTS * i + s)
                        pool.wait_ge(v_made, freed(n + pair0))
                        pool.tensor_copy(xs[s][:, :, 0:SEQ], source[:, ds(2 * n, 2), 0:SEQ]).then_inc(x_made, 1)

            @block.tensor
            def _(pe):
                with pe.Fori(0, PAIRS // SLOTS) as i:
                    for s in S2:
                        n = pe.snap(SLOTS * i + s)
                        pe.wait_ge(x_made, n + (pair0 + SLOTS * (one0 + 1) + 1))
                        pe.wait_ge(q_sb, freed(n + pair0))
                        pe.wait_ge(k_sb, freed(n + pair0))
                        x = xs[s][:, :, 0:SEQ]
                        two = lambda t: t[:, 0:N].rearrange("p (b n) -> p b n", n=SEQ)
                        pe.matmul(two(q_ps[s]), W[tag + "_wq"][:], x, start=True, stop=True)
                        pe.matmul(two(k_ps[s]), W[tag + "_wk"][:], x, start=True, stop=True).then_inc(qk_made, 1)
                        pe.wait_ge(v_sb, freed(n + pair0))
                        for c in range(2):
                            for f in range(2):
                                mm = pe.matmul(v_ps[s][0:HALF, c, f], xs[s][:, c, f * HALF:(f + 1) * HALF], W[tag + "_wv"][:],
                                               start=True, stop=True)
                        mm.then_inc(v_made, 1)

            @block.scalar
            def _(act):
                act.activation(bqs[:], W[tag + "_bq"][:], ACT.Copy, scale=SCALE).then_inc(bqs_made, 1)
                act.wait_ge(bqs_made, one0 + 1)
                with act.Fori(0, PAIRS // SLOTS) as i:
                    for s in S2:
                        n = act.snap(SLOTS * i + s)
                        act.wait_ge(qk_made, n + (pair0 + 1))
                        act.activation(q_all[:, ds(n * N, N)], q_ps[s][:, 0:N], ACT.Identity, bias=bqs[:, 0:1], scale=SCALE).then_inc(q_sb, 1)

            @block.vector
            def _(ve):
                if pair0 == 0:
                    for m in (q_sb, k_sb, v_sb, v_made):
                        ve.sem_inc(m, SLOTS)
                with ve.Fori(0, PAIRS // SLOTS) as i:
                    for s in S2:
                        n = ve.snap(SLOTS * i + s)
                        ve.wait_ge(qk_made, n + (pair0 + 1))
                        ve.tensor_scalar(k_all[:, ds(n * N, N)], k_ps[s][:, 0:N], W[tag + "_bk"][:, 0:1], None, ALU.add).then_inc(k_sb, 1)
                        ve.wait_ge(v_made, made(n + pair0))
                        ve.tensor_copy(v_all[:, ds(n * 4 * P, 4 * P)], v_ps[s][0:HALF].rearrange("p c f e -> p (c f e)")).then_inc(v_sb, 1)


def narrow_attention(nc, core, tag, projected, top_k, conv):
    HEADS, HD, G, TILES, TOP = 8, 16, 3, 3, 8
    ROWS = G * TILES * P
    GROUP = TILES * P
    W = core.w
    S2 = range(SLOTS)
    PAIRS = BATCH // SLOTS
    with ExitStack() as ctx:
        sb = lambda name, shape: ctx.enter_context(nc.sbuf_tensor(f"{tag}_{name}", shape, F32))
        ps = lambda name, shape: ctx.enter_context(nc.psum_tensor(f"{tag}_{name}_ps", shape, F32))
        sem = lambda name: core.keep(nc.semaphore(f"{tag}_{name}"))
        q_all = sb("q_all", [P, TOK])
        k_all = sb("k_all", [P, TOK])
        v_all = sb("v_all", [HALF, BATCH * 2 * P])
        project_heads(nc, core, tag, conv, q_all, k_all, v_all)

        qbd = [sb(f"qbd{s}", [P, ROWS]) for s in S2]
        vs = [sb(f"vs{s}", [HALF, 2, HEADS, 32]) for s in S2]
        prob = [[sb(f"prob{s}{g}", [P, TILES, PADSEQ]) for g in range(G)] for s in S2]
        negmax = [sb(f"negmax{s}", [P, G, TILES]) for s in S2]
        rsum = [sb(f"rsum{s}", [P, G, TILES]) for s in S2]
        rinv = [sb(f"rinv{s}", [P, G, TILES]) for s in S2]
        pt = [sb(f"pt{s}", [HALF, 2, ROWS]) for s in S2]
        if projected:
            oc = [sb(f"oc{s}", [P, SEQ]) for s in S2]
        if top_k:
            top = [sb(f"top{s}", [P, TILES, TOP]) for s in S2]
            next_top = [sb(f"next_top{s}", [P, TILES, TOP]) for s in S2]
            left = [sb(f"left{s}", [P, TILES, SEQ]) for s in S2]
        o_ps = [ps(f"o{s}", [P, 512]) for s in S2]
        s_ps = [ps(f"s{s}", [P, 512]) for s in S2]
        pt_ps = [[ps(f"pt{s}{f}", [P, 512]) for f in range(2)] for s in S2]
        qbd_made, v_spread, o_made, h_made = (sem(n) for n in ("qbd_made", "v_spread", "o_made", "h_made"))
        if projected:
            oc_made, y_made = sem("oc_made"), sem("y_made")
        s_made, max_made, exp_made, rsum_made, prob_made, pt_made, pt0_sb, pt1_sb = (
            sem(n) for n in ("s_made", "max_made", "exp_made", "rsum_made", "prob_made", "pt_made", "pt0_sb", "pt1_sb"))
        set_up = sem("set_up")
        if top_k:
            passed, found, kept = sem("passed"), sem("found"), sem("kept")
        scores = lambda s: s_ps[s][:, 0:TILES * SEQ].rearrange("p (t k) -> p t k", k=SEQ)

        def step(i, g, s):
            return SLOTS * G * i + (SLOTS * g + s)

        def pairs(eng, body):
            body(0, None)
            with eng.Fori(1, PAIRS) as i:
                body(i, eng.snap(i - 1))
            body(None, PAIRS - 1)

        with nc.Block() as block:
            @block.gpsimd
            def _(pool):
                for s in S2:
                    pool.memset(qbd[s][:], 0.0).then_inc(set_up, 1)
                    pool.memset(vs[s][:], 0.0).then_inc(set_up, 1)
                    for g in range(G):
                        pool.memset(prob[s][g][:], 0.0).then_inc(set_up, 1)
                pool.wait_ge(set_up, 10)
                with pool.Fori(0, PAIRS) as i:
                    for s in S2:
                        b = pool.snap(SLOTS * i + s)
                        pool.wait_ge(s_made, pool.snap(SLOTS * G * i + (s + 1)))
                        pool.tensor_tensor(qbd[s][:, 0:HEADS * SEQ].rearrange("p (h q) -> p h q", h=HEADS),
                                           q_all[:, ds(b * SEQ, SEQ)].unsqueeze(1).broadcast_to([P, HEADS, SEQ]),
                                           W["hmask16"][:].unsqueeze(2).broadcast_to([P, HEADS, SEQ]),
                                           ALU.mult).then_inc(qbd_made, 1)
                    for g in range(G):
                        for s in S2:
                            j = pool.snap(step(i, g, s))
                            pool.wait_ge(rsum_made, j + 1)
                            pr = prob[s][g]
                            pool.tensor_tensor(pr[:, :, 0:SEQ], pr[:, :, 0:SEQ],
                                               rinv[s][:, g].unsqueeze(2).broadcast_to([P, TILES, SEQ]),
                                               ALU.mult).then_inc(prob_made, 1)

            @block.tensor
            def _(pe):
                def score(i, g, s):
                    j = pe.snap(step(i, g, s))
                    b = pe.snap(SLOTS * i + s)
                    if g == 0:
                        pe.wait_ge(qbd_made, b + 1)
                    pe.wait_ge(exp_made, freed(j))
                    for t in range(TILES):
                        r0 = g * GROUP + t * P
                        mm = pe.matmul(scores(s)[:, t], qbd[s][:, r0:r0 + P], k_all[:, ds(b * SEQ, SEQ)], start=True, stop=True)
                    mm.then_inc(s_made, 1)

                def transposes(i, g, s):
                    j = pe.snap(step(i, g, s))
                    pe.wait_ge(prob_made, j + 1)
                    for f, emptied in ((0, pt0_sb), (1, pt1_sb)):
                        pe.wait_ge(emptied, freed(j))
                        for t in range(TILES):
                            mm = pe.transpose(pt_ps[s][f][0:HALF, t * P:(t + 1) * P],
                                              prob[s][g][:, t, f * HALF:(f + 1) * HALF], W["ident"][:])
                        mm.then_inc(pt_made, 1)

                def values(i, s):
                    j = pe.snap(step(i, G - 1, s))
                    b = pe.snap(SLOTS * i + s)
                    pe.wait_ge(v_spread, b + 1)
                    pe.wait_ge(h_made, freed(b))
                    pe.wait_ge(pt0_sb, made(j))
                    pe.wait_ge(pt1_sb, made(j))
                    for par in range(2):
                        for f in range(2):
                            for r in range(4):
                                h = 2 * r + par
                                mm = pe.matmul(o_ps[s][32 * r:32 * (r + 1), 0:SEQ], vs[s][:, f, h],
                                               pt[s][:, f, h * SEQ:(h + 1) * SEQ],
                                               start=(par == 0 and f == 0), stop=(par == 1 and f == 1))
                    mm.then_inc(o_made, 1)

                def body(i, before):
                    if i is not None:
                        for s in S2:
                            score(i, 0, s)
                    if before is not None:
                        for s in S2:
                            transposes(before, G - 1, s)
                    if i is not None:
                        for s in S2:
                            score(i, 1, s)
                    if before is not None:
                        for s in S2:
                            values(before, s)
                        if projected:
                            for s in S2:
                                b = pe.snap(SLOTS * before + s)
                                pe.wait_ge(oc_made, b + 1)
                                pe.matmul(o_ps[s][:, PADSEQ:PADSEQ + SEQ], W[tag + "_wo"][:], oc[s][:],
                                          start=True, stop=True).then_inc(y_made, 1)
                    if i is not None:
                        for s in S2:
                            transposes(i, 0, s)
                            score(i, 2, s)
                        for s in S2:
                            transposes(i, 1, s)

                pe.wait_ge(set_up, 10)
                pairs(pe, body)

            @block.scalar
            def _(act):
                def exponentials(i, g, s):
                    j = act.snap(step(i, g, s))
                    act.wait_ge(max_made, j + 1)
                    for t in range(TILES):
                        a = act.activation(prob[s][g][:, t, 0:SEQ], scores(s)[:, t], ACT.Exp, bias=negmax[s][:, g, t:t + 1],
                                           accum_out=None if top_k else rsum[s][:, g, t:t + 1])
                    a.then_inc(exp_made, 1)

                def leave_half_0(i, g, s):
                    j = act.snap(step(i, g, s))
                    act.wait_ge(pt_made, 2 * j + 1)
                    act.activation(pt[s][:, 0, g * GROUP:(g + 1) * GROUP], pt_ps[s][0][0:HALF, 0:GROUP], ACT.Copy).then_inc(pt0_sb, 1)

                def body(i, before):
                    if i is not None:
                        for s in S2:
                            exponentials(i, 0, s)
                    if before is not None:
                        for s in S2:
                            leave_half_0(before, G - 1, s)
                    if i is not None:
                        for s in S2:
                            exponentials(i, 1, s)
                    if before is not None and projected:
                        for s in S2:
                            b = act.snap(SLOTS * before + s)
                            act.wait_ge(o_made, b + 1)
                            act.activation(oc[s][:], o_ps[s][:, 0:SEQ], ACT.Identity, bias=W[tag + "_bv"][:, 0:1]).then_inc(oc_made, 1)
                    if i is not None:
                        for s in S2:
                            leave_half_0(i, 0, s)
                            exponentials(i, 2, s)
                        for s in S2:
                            leave_half_0(i, 1, s)

                act.wait_ge(set_up, 10)
                pairs(act, body)

            @block.vector
            def _(ve):
                def row_max(i, g, s):
                    j = ve.snap(step(i, g, s))
                    ve.wait_ge(s_made, made(j))
                    if not top_k:
                        ve.tensor_reduce(negmax[s][:, g], scores(s), AX.X, ALU.max, negate=True).then_inc(max_made, 1)
                        return
                    ve.sem_inc(passed, 1)
                    for t in range(TILES):
                        op = ve.max(top[s][:, t], scores(s)[:, t])
                    op.then_inc(found, 1)
                    ve.wait_ge(found, 4 * j + 1)
                    ve.sem_inc(passed, 1)
                    for t in range(TILES):
                        op = ve.match_replace(left[s][:, t], top[s][:, t], scores(s)[:, t], GONE)
                    op.then_inc(found, 1)
                    ve.tensor_scalar(negmax[s][:, g], top[s][:, :, 0], -1.0, None, ALU.mult).then_inc(max_made, 1)
                    ve.wait_ge(found, 4 * j + 2)
                    ve.sem_inc(passed, 1)
                    for t in range(TILES):
                        op = ve.max(next_top[s][:, t], left[s][:, t])
                    op.then_inc(found, 1)
                    ve.wait_ge(found, 4 * j + 3)
                    ve.sem_inc(passed, 1)
                    for t in range(TILES):
                        op = ve.match_replace(left[s][:, t], next_top[s][:, t], left[s][:, t], GONE)
                    op.then_inc(found, 1)

                def row_sum(i, g, s):
                    j = ve.snap(step(i, g, s))
                    ve.wait_ge(exp_made, made(j))
                    if top_k:
                        ve.wait_ge(found, 4 * j + 4)
                        pr = prob[s][g]
                        for t in range(TILES):
                            op = ve.scalar_tensor_tensor(pr[:, t, 0:SEQ], left[s][:, t], GONE, pr[:, t, 0:SEQ],
                                                         ALU.is_equal, ALU.mult, accum_out=rsum[s][:, g, t:t + 1])
                        op.then_inc(kept, 1)
                        ve.wait_ge(kept, j + 1)
                    ve.reciprocal(rinv[s][:, g], rsum[s][:, g]).then_inc(rsum_made, 1)

                def leave_half_1(i, g, s):
                    j = ve.snap(step(i, g, s))
                    ve.wait_ge(pt_made, 2 * j + 2)
                    ve.tensor_copy(pt[s][:, 1, g * GROUP:(g + 1) * GROUP], pt_ps[s][1][0:HALF, 0:GROUP]).then_inc(pt1_sb, 1)

                def spread_values(i, s):
                    b = ve.snap(SLOTS * i + s)
                    for par in range(2):
                        op = ve.tensor_copy(vs[s][:].rearrange("p f (r two) e -> p f r two e", two=2)[:, :, :, par, par * HD:(par + 1) * HD],
                                            v_all[:, ds(b * 2 * P, 2 * P)].rearrange("p (f r two d) -> p f r two d", f=2, two=2, d=HD)[:, :, :, par])
                    op.then_inc(v_spread, 1)

                def add(before, s):
                    b = ve.snap(SLOTS * before + s)
                    ve.wait_ge(y_made if projected else o_made, b + 1)
                    h_b = core.h[:, ds(b * SEQ, SEQ)]
                    ve.scalar_tensor_tensor(h_b, o_ps[s][:, PADSEQ:PADSEQ + SEQ] if projected else o_ps[s][:, 0:SEQ],
                                            W[tag + ("_bo" if projected else "_bv")][:, 0:1], h_b,
                                            ALU.add, ALU.add).then_inc(h_made, 1)

                def body(i, before):
                    if i is not None:
                        for s in S2:
                            row_max(i, 0, s)
                            if top_k:
                                row_sum(i, 0, s)
                    if before is not None:
                        for s in S2:
                            leave_half_1(before, G - 1, s)
                    if i is not None:
                        if not top_k:
                            for s in S2:
                                row_sum(i, 0, s)
                        for s in S2:
                            row_max(i, 1, s)
                            if top_k:
                                row_sum(i, 1, s)
                    if before is not None:
                        for s in S2:
                            add(before, s)
                    if i is not None:
                        for s in S2:
                            spread_values(i, s)
                        for s in S2:
                            leave_half_1(i, 0, s)
                        if not top_k:
                            for s in S2:
                                row_sum(i, 1, s)
                        for s in S2:
                            row_max(i, 2, s)
                            if top_k:
                                row_sum(i, 2, s)
                        for s in S2:
                            leave_half_1(i, 1, s)
                        if not top_k:
                            for s in S2:
                                row_sum(i, 2, s)

                for m in (h_made, exp_made, s_made, pt0_sb, pt1_sb):
                    ve.sem_inc(m, SLOTS)
                ve.wait_ge(set_up, 10)
                pairs(ve, body)


def routed_experts(nc, core, dram):
    EXPERTS, TOP_K, FF, ROUTED = 8, 2, 512, 1024
    FC = FF // P
    CHUNKS = ROUTED // CHUNK
    S2 = range(SLOTS)
    AHEAD = SLOTS + 1
    with ExitStack() as ctx:
        sb = lambda name, shape, dt=F32: ctx.enter_context(nc.sbuf_tensor(f"m_{name}", shape, dt))
        ps = lambda name, shape: ctx.enter_context(nc.psum_tensor(f"m_{name}_ps", shape, F32))
        sem = lambda name: core.keep(nc.semaphore(f"m_{name}"))
        ids_i = sb("ids_i", [P, TOP_K, ROUTED], I32)
        ids = sb("ids", [P, TOP_K, ROUTED])
        slot_w = sb("slot_w", [P, TOP_K, ROUTED])
        picked = sb("picked", [P, TOP_K, ROUTED])
        share = sb("share", [P, EXPERTS, ROUTED])
        w1 = [sb(f"w1{s}", [P, FF]) for s in S2]
        w2 = [sb(f"w2{s}", [P, FC, P]) for s in S2]
        hid = [sb(f"hid{s}", [P, FC, CHUNK]) for s in S2]
        part = [sb(f"part{s}", [P, CHUNK]) for s in S2]
        up_ps = [ps(f"up{f}", [P, CHUNK]) for f in range(FC)]
        down_ps = [ps(f"down{s}", [P, CHUNK]) for s in S2]
        ids_in, ids_made, picked_made, share_made = (sem(n) for n in ("ids_in", "ids_made", "picked_made", "share_made"))
        w_in = [sem(f"w_in{s}") for s in S2]
        up_made, gelu_made, down_made, part_made, h_made = (
            sem(n) for n in ("up_made", "gelu_made", "down_made", "part_made", "h_made"))

        with nc.Block() as block:
            @block.sync
            def _(sp):
                sp.dma_start(ids_i[:], dram["expert_ids"].partition_broadcast(P)).then_inc(ids_in, 16)
                sp.dma_start(slot_w[:], dram["expert_rows"].partition_broadcast(P)).then_inc(ids_in, 16)
                with sp.Fori(0, EXPERTS // SLOTS) as i:
                    for s in S2:
                        e = sp.snap(SLOTS * i + s)
                        sp.wait_ge(down_made, CHUNKS * e + (AHEAD - 2))
                        sp.dma_start(w1[s][:], dram["m_w1"][ds(e, 1)].rearrange("e p f -> p (e f)")).then_inc(w_in[s], 16)
                        sp.dma_start(w2[s][:], dram["m_w2"][ds(e, 1)].rearrange("e p c o -> p (e c) o")).then_inc(w_in[s], 16)

            @block.tensor
            def _(pe):
                def up(i, s, c):
                    t = pe.snap(SLOTS * CHUNKS * i + (CHUNKS * s + c))
                    if c == 0:
                        pe.wait_ge(w_in[s], 32 * i + 32)
                    for f in range(FC):
                        pe.wait_ge(gelu_made, FC * t + (f + 1))
                        pe.matmul(up_ps[f][:], w1[s][:, f * P:(f + 1) * P], core.normed[:, c * CHUNK:(c + 1) * CHUNK],
                                  start=True, stop=True).then_inc(up_made, 1)

                def down(i, s, c):
                    t = pe.snap(SLOTS * CHUNKS * i + (CHUNKS * s + c))
                    pe.wait_ge(gelu_made, FC * t + 2 * FC)
                    pe.wait_ge(part_made, freed(t))
                    for f in range(FC):
                        mm = pe.matmul(down_ps[c][:], w2[s][:, f], hid[c][:, f], start=(f == 0), stop=(f == FC - 1))
                    mm.then_inc(down_made, 1)

                steps = [(s, c) for s in S2 for c in range(CHUNKS)]
                with pe.Fori(0, EXPERTS // SLOTS) as i:
                    up(i, *steps[0])
                    for n in range(1, len(steps)):
                        up(i, *steps[n])
                        down(i, *steps[n - 1])
                    down(i, *steps[-1])

            @block.scalar
            def _(act):
                with act.Fori(0, EXPERTS // SLOTS) as i:
                    for n in range(SLOTS * CHUNKS):
                        t = act.snap(SLOTS * CHUNKS * i + n)
                        act.wait_ge(down_made, made(t, AHEAD) - SLOTS)
                        for f in range(FC):
                            act.wait_ge(up_made, FC * t + (f + 1))
                            act.activation(hid[n % CHUNKS][:, f], up_ps[f][:], ACT.Gelu).then_inc(gelu_made, 1)

            @block.vector
            def _(ve):
                ve.sem_inc(gelu_made, FC)
                ve.sem_inc(down_made, AHEAD)
                ve.sem_inc(part_made, SLOTS)
                ve.sem_inc(h_made, SLOTS)
                ve.wait_ge(ids_in, 32)
                ve.tensor_copy(ids[:], ids_i[:]).then_inc(ids_made, 1)
                ve.wait_ge(ids_made, 1)
                for e in range(EXPERTS):
                    if e:
                        ve.wait_ge(share_made, e)
                    ve.scalar_tensor_tensor(picked[:], ids[:], float(e), slot_w[:], ALU.is_equal, ALU.mult).then_inc(picked_made, 1)
                    ve.wait_ge(picked_made, e + 1)
                    ve.tensor_tensor(share[:, e], picked[:, 0], picked[:, 1], ALU.add).then_inc(share_made, 1)
                ve.wait_ge(share_made, EXPERTS)
                with ve.Fori(0, EXPERTS // SLOTS) as i:
                    for s in S2:
                        for c in range(CHUNKS):
                            t = ve.snap(SLOTS * CHUNKS * i + (CHUNKS * s + c))
                            ve.wait_ge(down_made, made(t, AHEAD))
                            ve.wait_ge(h_made, freed(t))
                            ve.tensor_tensor(part[c][:], down_ps[c][:],
                                             share[:, ds(SLOTS * i + s, 1), c * CHUNK:(c + 1) * CHUNK].rearrange("p e n -> p (e n)"),
                                             ALU.mult).then_inc(part_made, 1)
                            ve.wait_ge(part_made, made(t))
                            h_c = core.h[:, c * CHUNK:(c + 1) * CHUNK]
                            ve.tensor_tensor(h_c, h_c, part[c][:], ALU.add).then_inc(h_made, 1)


def head_mixing(nc, core):
    HEADS, HD = 8, 16
    SCALE = float(HD) ** -0.5
    TILES = TOKPAD // P
    W = core.w
    SLOTS = 4
    S2 = range(SLOTS)
    with ExitStack() as ctx:
        sb = lambda name, shape: ctx.enter_context(nc.sbuf_tensor(f"a1_{name}", shape, F32))
        ps = lambda name, shape: ctx.enter_context(nc.psum_tensor(f"a1_{name}_ps", shape, F32))
        sem = lambda name: core.keep(nc.semaphore(f"a1_{name}"))
        xs = [sb(f"xs{s}", [P, P]) for s in S2]
        qkv = [sb(f"qkv{s}", [P, 3, P]) for s in S2]
        prod = [sb(f"prod{s}", [P, HEADS, HEADS, HD]) for s in S2]
        prod2 = [sb(f"prod2{s}", [P, HEADS, HD, HEADS]) for s in S2]
        score = [sb(f"score{s}", [P, HEADS, HEADS]) for s in S2]
        shifted = [sb(f"shifted{s}", [P, HEADS, HEADS]) for s in S2]
        weight = [sb(f"weight{s}", [P, HEADS, HEADS]) for s in S2]
        top = [sb(f"top{s}", [P, HEADS]) for s in S2]
        total = [sb(f"total{s}", [P, HEADS]) for s in S2]
        inv = [sb(f"inv{s}", [P, HEADS]) for s in S2]
        mixed = [sb(f"mixed{s}", [P, HEADS, HD]) for s in S2]
        scaled = [sb(f"scaled{s}", [P, P]) for s in S2]
        qkv_ps = [ps(f"qkv{s}", [P, 512]) for s in S2]
        turn_ps = [ps(f"turn{s}", [P, 512]) for s in S2]
        names = ["x_made", "qkv_made", "qkv_sb", "prod_made", "score_made", "top_made", "shifted_made", "weight_made",
                 "total_made", "inv_made", "prod2_made", "mixed_made", "scaled_made", "turn_made", "turned_made"]
        (x_made, qkv_made, qkv_sb, prod_made, score_made, top_made, shifted_made, weight_made, total_made, inv_made,
         prod2_made, mixed_made, scaled_made, turn_made, turned_made) = (sem(n) for n in names)

        with nc.Block() as block:
            @block.gpsimd
            def _(pool):
                with pool.Fori(0, TILES // SLOTS) as i:
                    for s in S2:
                        t = pool.snap(SLOTS * i + s)
                        pool.wait_ge(turned_made, freed(t))
                        pool.tensor_copy(xs[s][:], core.normed[:, ds(t * P, P)]).then_inc(x_made, 1)
                    for s in S2:
                        t = pool.snap(SLOTS * i + s)
                        pool.wait_ge(qkv_sb, t + 1)
                        q = qkv[s][:, 0].rearrange("p (h d) -> p h d", d=HD)
                        k = qkv[s][:, 1].rearrange("p (g d) -> p g d", d=HD)
                        pool.tensor_tensor(prod[s][:], q.unsqueeze(2).broadcast_to([P, HEADS, HEADS, HD]),
                                           k.unsqueeze(1).broadcast_to([P, HEADS, HEADS, HD]), ALU.mult).then_inc(prod_made, 1)

            @block.tensor
            def _(pe):
                with pe.Fori(0, TILES // SLOTS) as i:
                    for s in S2:
                        t = pe.snap(SLOTS * i + s)
                        pe.wait_ge(x_made, t + 1)
                        pe.matmul(qkv_ps[s][:, 0:3 * P], xs[s][:], W["a1_wqkv"][:], start=True, stop=True).then_inc(qkv_made, 1)
                    for s in S2:
                        t = pe.snap(SLOTS * i + s)
                        pe.wait_ge(scaled_made, t + 1)
                        pe.wait_ge(turned_made, freed(t))
                        pe.transpose(turn_ps[s][:, 0:P], scaled[s][:], W["ident"][:]).then_inc(turn_made, 1)

            @block.scalar
            def _(act):
                with act.Fori(0, TILES // SLOTS) as i:
                    for s in S2:
                        t = act.snap(SLOTS * i + s)
                        act.wait_ge(qkv_made, t + 1)
                        act.activation(qkv[s][:], qkv_ps[s][:, 0:3 * P].rearrange("p (c e) -> p c e", e=P), ACT.Copy).then_inc(qkv_sb, 1)
                    for s in S2:
                        t = act.snap(SLOTS * i + s)
                        act.wait_ge(shifted_made, t + 1)
                        act.activation(weight[s][:], shifted[s][:], ACT.Exp, scale=SCALE).then_inc(weight_made, 1)
                    for s in S2:
                        t = act.snap(SLOTS * i + s)
                        act.wait_ge(turn_made, t + 1)
                        act.activation(core.normed[:, ds(t * P, P)], turn_ps[s][:, 0:P], ACT.Copy).then_inc(turned_made, 1)

            @block.vector
            def _(ve):
                ve.sem_inc(turned_made, SLOTS)
                with ve.Fori(0, TILES // SLOTS) as i:
                    for s in S2:
                        t = ve.snap(SLOTS * i + s)
                        ve.wait_ge(prod_made, t + 1)
                        ve.tensor_reduce(score[s][:], prod[s][:], AX.X, ALU.add).then_inc(score_made, 1)
                        ve.wait_ge(score_made, t + 1)
                        ve.tensor_reduce(top[s][:], score[s][:], AX.X, ALU.max).then_inc(top_made, 1)
                        ve.wait_ge(top_made, t + 1)
                        ve.tensor_tensor(shifted[s][:], score[s][:], top[s][:].unsqueeze(2).broadcast_to([P, HEADS, HEADS]),
                                         ALU.subtract).then_inc(shifted_made, 1)
                    for s in S2:
                        t = ve.snap(SLOTS * i + s)
                        ve.wait_ge(weight_made, t + 1)
                        ve.tensor_reduce(total[s][:], weight[s][:], AX.X, ALU.add).then_inc(total_made, 1)
                        v = qkv[s][:, 2].rearrange("p (g d) -> p d g", d=HD)
                        ve.tensor_tensor(prod2[s][:], weight[s][:].unsqueeze(2).broadcast_to([P, HEADS, HD, HEADS]),
                                         v.unsqueeze(1).broadcast_to([P, HEADS, HD, HEADS]), ALU.mult).then_inc(prod2_made, 1)
                        ve.wait_ge(total_made, t + 1)
                        ve.reciprocal(inv[s][:], total[s][:]).then_inc(inv_made, 1)
                        ve.wait_ge(prod2_made, t + 1)
                        ve.tensor_reduce(mixed[s][:], prod2[s][:], AX.X, ALU.add).then_inc(mixed_made, 1)
                        ve.wait_ge(mixed_made, t + 1)
                        ve.wait_ge(inv_made, t + 1)
                        ve.tensor_tensor(scaled[s][:].rearrange("p (h d) -> p h d", d=HD), mixed[s][:],
                                         inv[s][:].unsqueeze(2).broadcast_to([P, HEADS, HD]), ALU.mult).then_inc(scaled_made, 1)


def window_projection(nc, core):
    HEADS, HD, WINDOW = 8, 16, 64
    SHIFT = WINDOW // 2
    WINDOWS = -(-SEQ // WINDOW)
    HALF_BATCHES = BATCH // 2
    W = core.w
    S2 = range(SLOTS)
    kept = lambda w, h: max(0, min(HEADS, SEQ - (WINDOW * w + HEADS * h)))
    with ExitStack() as ctx:
        sb = lambda name, shape: ctx.enter_context(nc.sbuf_tensor(f"wp_{name}", shape, F32))
        ps = lambda name, shape: ctx.enter_context(nc.psum_tensor(f"wp_{name}_ps", shape, F32))
        sem = lambda name: core.keep(nc.semaphore(f"wp_{name}"))
        rolled = sb("rolled", [P, BATCH, WINDOWS * WINDOW])
        w_head = [sb(f"w_head{s}", [P, HEADS, P]) for s in S2]
        y_ps = [[ps(f"y{s}{q}", [P, 512]) for q in range(2)] for s in S2]
        padded_made, rolled_made, w_made, y_made, h_made = (
            sem(n) for n in ("padded_made", "rolled_made", "w_made", "y_made", "h_made"))
        flat = core.normed[:, 0:TOK].rearrange("p (b n) -> p b n", n=SEQ)
        res = core.h[:, 0:TOK].rearrange("p (b n) -> p b n", n=SEQ)
        with nc.Block() as block:
            @block.gpsimd
            def _(pool):
                pool.memset(rolled[:, :, SEQ:], 0.0).then_inc(padded_made, 1)
                pool.tensor_copy(rolled[:, :, SEQ - SHIFT:SEQ], flat[:, :, 0:SHIFT]).then_inc(padded_made, 1)

            @block.scalar
            def _(act):
                act.activation(rolled[:, :, 0:SEQ - SHIFT], flat[:, :, SHIFT:SEQ], ACT.Copy).then_inc(rolled_made, 1)

            @block.tensor
            def _(pe):
                pe.wait_ge(padded_made, 2)
                pe.wait_ge(rolled_made, 1)
                tok = rolled[:].rearrange("p b (w a e) -> p b w a e", a=HEADS, e=HEADS)
                for h in range(HEADS):
                    s = h % SLOTS
                    wins = sum(kept(w, h) > 0 for w in range(WINDOWS))
                    pe.wait_ge(w_made, h + 1)
                    if h >= SLOTS:
                        pe.wait_ge(h_made, h - 1)
                    for q in range(2):
                        y = y_ps[s][q][:, 0:HALF_BATCHES * wins * HEADS].rearrange("p (b w a) -> p b w a", w=wins, a=HEADS)
                        for e in range(HEADS):
                            mm = pe.matmul(y, w_head[s][:, e], tok[:, q * HALF_BATCHES:(q + 1) * HALF_BATCHES, 0:wins, :, e],
                                           start=(e == 0), stop=(e == HEADS - 1))
                    mm.then_inc(y_made, 1)

            @block.vector
            def _(ve):
                def head_weights(h):
                    if h >= SLOTS:
                        ve.wait_ge(y_made, h - 1)
                    ve.tensor_scalar(w_head[h % SLOTS][:], W["wp_w"][:], W["hmask16"][:, h:h + 1], None, ALU.mult).then_inc(w_made, 1)

                head_weights(0)
                for h in range(HEADS):
                    s = h % SLOTS
                    wins = sum(kept(w, h) > 0 for w in range(WINDOWS))
                    if h + 1 < HEADS:
                        head_weights(h + 1)
                    ve.wait_ge(y_made, h + 1)
                    for q in range(2):
                        bs = slice(q * HALF_BATCHES, (q + 1) * HALF_BATCHES)
                        y = y_ps[s][q][:, 0:HALF_BATCHES * wins * HEADS].rearrange("p (b w a) -> p b w a", w=wins, a=HEADS)
                        for w in range(wins):
                            first = (WINDOW * w + HEADS * h + SHIFT) % SEQ
                            n = kept(w, h)
                            cut = min(n, SEQ - first)
                            for a0, a1, at in ((0, cut, first), (cut, n, 0)):
                                if a1 > a0:
                                    r = res[:, bs, at:at + a1 - a0]
                                    op = ve.scalar_tensor_tensor(r, y[:, :, w, a0:a1], W["wp_b"][:, 0:1], r, ALU.add, ALU.add)
                    op.then_inc(h_made, 1)


def trig_ffn(nc, core):
    NF, QUAD, LUT = 64, 4, 1024
    R = NF // QUAD
    W = core.w
    STEP = 2.0 * math.pi / LUT
    CHUNKS = TOKPAD // CHUNK
    WIDE = QUAD * CHUNK
    S2 = range(SLOTS)
    with ExitStack() as ctx:
        sb = lambda name, shape, dt=F32: ctx.enter_context(nc.sbuf_tensor(f"f1_{name}", shape, dt))
        ps = lambda name, shape: ctx.enter_context(nc.psum_tensor(f"f1_{name}_ps", shape, F32))
        sem = lambda name: core.keep(nc.semaphore(f"f1_{name}"))
        scale = sb("scale", [P, NF])
        shift = sb("shift", [P, NF])
        absw = sb("absw", [P, NF])
        cols = sb("cols", [P, NF, 2, 32])
        minus_pi = sb("minus_pi", [P, 1])
        angle = [sb(f"angle{s}", [P, QUAD, CHUNK], I32) for s in S2]
        sin_at = [sb(f"sin_at{s}", [P, QUAD, CHUNK], I16) for s in S2]
        cos_at = [sb(f"cos_at{s}", [P, QUAD, CHUNK], I16) for s in S2]
        cos_raw = [sb(f"cos_raw{s}", [P, QUAD, CHUNK], I16) for s in S2]
        sin_v = [sb(f"sin_v{s}", [P, QUAD, CHUNK]) for s in S2]
        cos_v = [sb(f"cos_v{s}", [P, QUAD, CHUNK]) for s in S2]
        sums = sb("sums", [P, CHUNK])
        e = sb("e", [P, CHUNK])
        sum_ps = ps("sum", [P, CHUNK])
        y_ps = ps("y", [P, CHUNK])
        set_up, angle_made, sin_at_made, cos_raw_made, cos_at_made, sin_made, cos_made, used = (
            sem(n) for n in ("set_up", "angle_made", "sin_at_made", "cos_raw_made", "cos_at_made", "sin_made", "cos_made", "used"))
        sums_sb, y_made, e_made, h_made = (
            sem(n) for n in ("sums_sb", "y_made", "e_made", "h_made"))

        with nc.Block() as block:
            @block.tensor
            def _(pe):
                def product(before):
                    pe.wait_ge(sums_sb, before + 1)
                    pe.matmul(y_ps[:], W["f1_proj"][:], sums[:], start=True, stop=True).then_inc(y_made, 1)

                def quads(c, before):
                    for r in range(R):
                        s = r % SLOTS
                        q = pe.snap(R * c + r)
                        for cs, value_made, values in ((1, sin_made, sin_v), (0, cos_made, cos_v)):
                            pe.wait_ge(value_made, made(q))
                            if r == 0 and cs == 1 and before is not None:
                                pe.wait_ge(sums_sb, before + 1)
                            for j in range(QUAD):
                                mm = pe.matmul(sum_ps[32 * j:32 * (j + 1), :], cols[:, QUAD * r + j, cs], values[s][:, j],
                                               start=(r == 0 and cs == 1), stop=(r == R - 1 and cs == 0))
                        mm.then_inc(used, 1)
                        if r == 1 and before is not None:
                            product(before)

                pe.wait_ge(set_up, 9)
                quads(0, None)
                with pe.Fori(1, CHUNKS) as c:
                    quads(c, pe.snap(c - 1))
                product(CHUNKS - 1)

            @block.scalar
            def _(act):
                def leave_sums(before):
                    act.wait_ge(used, made(R * before + (R - 1)))
                    act.activation(sums[:], sum_ps[:], ACT.Copy).then_inc(sums_sb, 1)

                def sines(c, r):
                    s = r % SLOTS
                    q = act.snap(R * c + r)
                    act.wait_ge(used, freed(q))
                    act.wait_ge(sin_at_made, q + 1)
                    act.activation(sin_v[s][:], sin_at[s][:], ACT.Sin, bias=minus_pi[:, 0:1], scale=STEP).then_inc(sin_made, 1)
                    act.wait_ge(cos_at_made, q + 1)
                    act.activation(cos_v[s][:], cos_at[s][:], ACT.Sin, bias=minus_pi[:, 0:1], scale=STEP).then_inc(cos_made, 1)

                def silu(before):
                    act.wait_ge(y_made, before + 1)
                    act.activation(e[:], y_ps[:], ACT.Silu, scale=-1.0).then_inc(e_made, 1)

                act.wait_ge(set_up, 9)
                for r in range(R):
                    sines(0, r)
                with act.Fori(1, CHUNKS) as c:
                    before = act.snap(c - 1)
                    for r in range(R):
                        sines(c, r)
                        if r == 0:
                            leave_sums(before)
                        if r == 5:
                            silu(before)
                leave_sums(CHUNKS - 1)
                silu(CHUNKS - 1)

            @block.vector
            def _(ve):
                ve.scalar_tensor_tensor(absw[:], W["f1_w"][:], -1.0, W["f1_w"][:], ALU.mult, ALU.max).then_inc(set_up, 1)
                ve.wait_ge(set_up, 1)
                ve.tensor_scalar(absw[:], absw[:], 1.0, STEP, ALU.add, ALU.mult).then_inc(set_up, 1)
                ve.wait_ge(set_up, 2)
                ve.reciprocal(scale[:], absw[:]).then_inc(set_up, 1)
                ve.tensor_scalar(shift[:], W["f1_b"][:], 1.0 / STEP, None, ALU.mult).then_inc(set_up, 1)
                ve.memset(cols[:], 0.0).then_inc(set_up, 1)
                ve.memset(minus_pi[:], -math.pi).then_inc(set_up, 1)
                ve.wait_ge(set_up, 6)
                for r in range(R):
                    for cs, name in ((0, "f1_attn_cos"), (1, "f1_attn_sin")):
                        op = ve.tensor_copy(cols[:, QUAD * r:QUAD * (r + 1), cs, R * cs + r],
                                            W[name][:, QUAD * r:QUAD * (r + 1)])
                op.then_inc(set_up, 1)
                for m in (used, sin_made, cos_made):
                    ve.sem_inc(m, SLOTS)
                ve.wait_ge(set_up, 7)
                ve.sem_inc(set_up, 2)

                def indices(c, r):
                    x = core.normed[:, ds(c * CHUNK, CHUNK)]
                    s = r % SLOTS
                    q = ve.snap(R * c + r)
                    ve.wait_ge(sin_made, freed(q))
                    for j in range(QUAD):
                        n = QUAD * r + j
                        op = ve.tensor_scalar(angle[s][:, j], x, scale[:, n:n + 1], shift[:, n:n + 1], ALU.mult, ALU.add)
                    op.then_inc(angle_made, 1)
                    ve.wait_ge(angle_made, q + 1)
                    low = angle[s][:].bitcast(I16).rearrange("p j (t w) -> p j t w", w=2)[:, :, :, 0]
                    ve.tensor_scalar(sin_at[s][:], low, LUT - 1, None, ALU.bitwise_and).then_inc(sin_at_made, 1)
                    ve.wait_ge(sin_at_made, q + 1)
                    ve.tensor_scalar(cos_raw[s][:], sin_at[s][:], float(LUT // 4), None, ALU.add).then_inc(cos_raw_made, 1)
                    ve.wait_ge(cos_raw_made, q + 1)
                    ve.wait_ge(cos_made, freed(q))
                    ve.tensor_scalar(cos_at[s][:], cos_raw[s][:], LUT - 1, None, ALU.bitwise_and).then_inc(cos_at_made, 1)

                def add(before):
                    ve.wait_ge(e_made, before + 1)
                    h_c = core.h[:, ds(before * CHUNK, CHUNK)]
                    ve.tensor_tensor(h_c, h_c, e[:], ALU.add).then_inc(h_made, 1)

                for r in range(R):
                    indices(0, r)
                with ve.Fori(1, CHUNKS) as c:
                    before = ve.snap(c - 1)
                    for r in range(R):
                        indices(c, r)
                        if r == 7:
                            add(before)
                add(CHUNKS - 1)


def decay_retrieval(nc, core):
    HEADS, HD = 4, 32
    W = core.w
    S2 = range(SLOTS)
    with ExitStack() as ctx:
        sb = lambda name, shape: ctx.enter_context(nc.sbuf_tensor(f"a2_{name}", shape, F32))
        ps = lambda name, shape: ctx.enter_context(nc.psum_tensor(f"a2_{name}_ps", shape, F32))
        sem = lambda name: core.keep(nc.semaphore(f"a2_{name}"))
        ones = sb("ones", [P, P])
        v_w = sb("v_w", [P, P])
        o_w = sb("o_w", [P, P])
        log_decay = sb("log_decay", [P, HEADS])
        decay = sb("decay", [HALF, HEADS, 2, SEQ])
        xs = [sb(f"xs{s}", [P, PADSEQ]) for s in S2]
        qk = [sb(f"qk{s}", [P, 2, PADSEQ]) for s in S2]
        sq = [sb(f"sq{s}", [P, 2, PADSEQ]) for s in S2]
        norm = [sb(f"norm{s}", [P, 2, PADSEQ]) for s in S2]
        vs = [sb(f"vs{s}", [HALF, 2, P]) for s in S2]
        weight = [sb(f"weight{s}", [HALF, HEADS, 2, SEQ]) for s in S2]
        got = [sb(f"got{s}", [P, SEQ]) for s in S2]
        qk_ps = ps("qk", [P, 512])
        n_ps = ps("n", [P, 512])
        v_ps = ps("v", [P, 512])
        s_ps = ps("s", [P, HEADS, 512])
        o_ps = ps("o", [P, 512])
        (decay_made, w_ps_made, x_made, qk_made, qk_sb, sq_made, n_made, root_made, inv_step, unit_made, v_made, v_sb,
         s_made, weight_made, got_made, got_sb, y_made, h_made, w_sb) = (
            sem(n) for n in ("decay_made", "w_ps_made", "x_made", "qk_made", "qk_sb", "sq_made", "n_made", "root_made",
                             "inv_step", "unit_made", "v_made", "v_sb", "s_made", "weight_made", "got_made", "got_sb",
                             "y_made", "h_made", "w_sb"))
        two = lambda t: t[:, 0:2 * PADSEQ].rearrange("p (c n) -> p c n", n=PADSEQ)

        with nc.Block() as block:
            @block.gpsimd
            def _(pool):
                for s in S2:
                    pool.memset(xs[s][:, SEQ:PADSEQ], 0.0)
                with pool.Fori(0, BATCH // SLOTS) as i:
                    for s in S2:
                        b = pool.snap(SLOTS * i + s)
                        pool.wait_ge(h_made, freed(b))
                        pool.tensor_copy(xs[s][:, 0:SEQ], core.normed[:, ds(b * PADSEQ, SEQ)]).then_inc(x_made, 1)

            @block.tensor
            def _(pe):
                pe.matmul(v_ps[:, 0:P], W["a2_basis"][:], W["a2_vc"][:], start=True, stop=True)
                pe.matmul(o_ps[:, 0:P], W["a2_oc"][:], W["a2_basis"][:], start=True, stop=True).then_inc(w_ps_made, 1)
                pe.wait_ge(w_sb, 3)
                with pe.Fori(0, BATCH // SLOTS) as i:
                    for s in S2:
                        b = pe.snap(SLOTS * i + s)
                        pe.wait_ge(x_made, b + 1)
                        pe.wait_ge(qk_sb, b + 1)
                        pe.matmul(qk_ps[:, 0:PADSEQ], W["a2_wq"][:], xs[s][:], start=True, stop=True)
                        pe.matmul(qk_ps[:, PADSEQ:2 * PADSEQ], W["a2_wk"][:], xs[s][:], start=True, stop=True).then_inc(qk_made, 1)
                        pe.wait_ge(v_sb, b + 1)
                        for f in range(2):
                            mm = pe.matmul(v_ps[0:HALF, f * P:(f + 1) * P], xs[s][:, f * HALF:(f + 1) * HALF], v_w[:], start=True, stop=True)
                        mm.then_inc(v_made, 1)
                    for s in S2:
                        b = pe.snap(SLOTS * i + s)
                        pe.wait_ge(sq_made, b + 1)
                        pe.wait_ge(root_made, b + 1)
                        pe.matmul(n_ps[:, 0:2 * PADSEQ], ones[:], sq[s][:].rearrange("p c n -> p (c n)"), start=True, stop=True).then_inc(n_made, 1)
                    for s in S2:
                        b = pe.snap(SLOTS * i + s)
                        pe.wait_ge(unit_made, b + 1)
                        pe.wait_ge(weight_made, b + 1)
                        for h in range(HEADS):
                            rows = slice(h * HD, (h + 1) * HD)
                            for f in range(2):
                                mm = pe.matmul(s_ps[0:HALF, h, f * SEQ:(f + 1) * SEQ], qk[s][rows, 1, f * HALF:(f + 1) * HALF],
                                               qk[s][rows, 0, 0:SEQ], start=True, stop=True)
                        mm.then_inc(s_made, 1)
                    for s in S2:
                        b = pe.snap(SLOTS * i + s)
                        pe.wait_ge(weight_made, b + 2)
                        pe.wait_ge(v_sb, b + 2)
                        pe.wait_ge(h_made, b + 2)
                        for h in range(HEADS):
                            rows = slice(h * HD, (h + 1) * HD)
                            for f in range(2):
                                mm = pe.matmul(o_ps[rows, 0:SEQ], vs[s][:, f, rows], weight[s][:, h, f], start=(f == 0), stop=(f == 1))
                        mm.then_inc(got_made, 1)
                        pe.wait_ge(got_sb, b + 1)
                        pe.matmul(o_ps[:, PADSEQ:PADSEQ + SEQ], o_w[:], got[s][:], start=True, stop=True).then_inc(y_made, 1)

            @block.scalar
            def _(act):
                act.activation(log_decay[:], W["a2_decay"][:], ACT.Exp, scale=-1.0).then_inc(decay_made, 1)
                act.wait_ge(decay_made, 3)
                act.activation(log_decay[:], log_decay[:], ACT.Ln).then_inc(decay_made, 1)
                act.wait_ge(decay_made, 4)
                for h in range(HEADS):
                    a = act.activation(decay[:, h], W["a2_distance"][:], ACT.Exp, scale=log_decay[0:HALF, h:h + 1])
                a.then_inc(decay_made, 1)
                with act.Fori(0, BATCH // SLOTS) as i:
                    for s in S2:
                        b = act.snap(SLOTS * i + s)
                        act.wait_ge(qk_made, b + 1)
                        act.activation(qk[s][:], two(qk_ps), ACT.Copy).then_inc(qk_sb, 1)
                        act.wait_ge(qk_sb, b + 2)
                        act.activation(sq[s][:], qk[s][:], ACT.Square).then_inc(sq_made, 1)
                    for s in S2:
                        b = act.snap(SLOTS * i + s)
                        act.wait_ge(n_made, b + 1)
                        act.activation(norm[s][:], two(n_ps), ACT.Sqrt).then_inc(root_made, 1)
                    for s in S2:
                        b = act.snap(SLOTS * i + s)
                        act.wait_ge(got_made, b + 1)
                        act.activation(got[s][:], o_ps[:, 0:SEQ], ACT.Copy).then_inc(got_sb, 1)

            @block.vector
            def _(ve):
                ve.memset(ones[:], 1.0).then_inc(w_sb, 1)
                ve.wait_ge(w_ps_made, 1)
                ve.tensor_copy(v_w[:], v_ps[:, 0:P]).then_inc(w_sb, 1)
                ve.tensor_scalar(o_w[:], o_ps[:, 0:P], W["a2_out_scale"][:, 0:1], None, ALU.mult).then_inc(w_sb, 1)
                ve.wait_ge(decay_made, 1)
                ve.tensor_scalar(log_decay[:], log_decay[:], 1.0, None, ALU.add).then_inc(decay_made, 1)
                ve.wait_ge(decay_made, 2)
                ve.reciprocal(log_decay[:], log_decay[:]).then_inc(decay_made, 1)
                ve.wait_ge(decay_made, 5)
                ve.tensor_tensor(decay[:], decay[:], W["a2_later"][:].unsqueeze(1).broadcast_to([HALF, HEADS, 2, SEQ]),
                                 ALU.mult).then_inc(decay_made, 1)
                ve.sem_inc(h_made, SLOTS)
                for m in (qk_sb, v_sb, root_made, weight_made):
                    ve.sem_inc(m, 1)
                ve.wait_ge(decay_made, 6)
                with ve.Fori(0, BATCH // SLOTS) as i:
                    for s in S2:
                        b = ve.snap(SLOTS * i + s)
                        ve.wait_ge(v_made, b + 1)
                        ve.tensor_copy(vs[s][:], v_ps[0:HALF, 0:2 * P].rearrange("p (f e) -> p f e", e=P)).then_inc(v_sb, 1)
                    for s in S2:
                        b = ve.snap(SLOTS * i + s)
                        ve.wait_ge(root_made, b + 2)
                        ve.tensor_scalar(norm[s][:], norm[s][:], 1e-12, None, ALU.max).then_inc(inv_step, 1)
                        ve.wait_ge(inv_step, 2 * b + 1)
                        ve.reciprocal(norm[s][:], norm[s][:]).then_inc(inv_step, 1)
                        ve.wait_ge(inv_step, 2 * b + 2)
                        ve.tensor_tensor(qk[s][:], qk[s][:], norm[s][:], ALU.mult).then_inc(unit_made, 1)
                    for s in S2:
                        b = ve.snap(SLOTS * i + s)
                        ve.wait_ge(s_made, b + 1)
                        ve.tensor_tensor(weight[s][:].rearrange("p h f q -> p h (f q)"), s_ps[0:HALF, :, 0:2 * SEQ],
                                         decay[:].rearrange("p h f q -> p h (f q)"), ALU.mult).then_inc(weight_made, 1)
                    for s in S2:
                        b = ve.snap(SLOTS * i + s)
                        ve.wait_ge(y_made, b + 1)
                        h_b = core.h[:, ds(b * SEQ, SEQ)]
                        ve.tensor_tensor(h_b, h_b, o_ps[:, PADSEQ:PADSEQ + SEQ], ALU.add).then_inc(h_made, 1)





def wide_attention(nc, core):
    HD, G, TILES, R, QW = 64, 4, 3, 96, 144
    ROWS = TILES * R
    INNER = G * P
    SCALE = float(HD) ** -0.5
    W = core.w
    S2 = range(SLOTS)
    with ExitStack() as ctx:
        sb = lambda name, shape: ctx.enter_context(nc.sbuf_tensor(f"a3_{name}", shape, F32))
        ps = lambda name, shape: ctx.enter_context(nc.psum_tensor(f"a3_{name}_ps", shape, F32))
        sem = lambda name: core.keep(nc.semaphore(f"a3_{name}"))
        xs = [sb(f"xs{s}", [P, PADSEQ]) for s in S2]
        qs = [sb(f"qs{s}", [P, SEQ]) for s in S2]
        kt = [sb(f"kt{s}", [P, SEQ]) for s in S2]
        qbd = [sb(f"qbd{s}", [P, ROWS]) for s in S2]
        vs = [sb(f"vs{s}", [HALF, 2, INNER]) for s in S2]
        prob = [sb(f"prob{s}", [R, TILES, PADSEQ]) for s in S2]
        negmax = [sb(f"negmax{s}", [R, TILES]) for s in S2]
        rsum = [sb(f"rsum{s}", [R, TILES]) for s in S2]
        rinv = [sb(f"rinv{s}", [R, TILES]) for s in S2]
        pt = [sb(f"pt{s}", [HALF, 2, ROWS]) for s in S2]
        oc = [sb(f"oc{s}", [P, G, SEQ]) for s in S2]
        qk_ps = [ps(f"qk{s}", [P, 512]) for s in S2]
        v_ps = ps("v", [P, 2, INNER])
        s_ps = [ps(f"s{s}", [P, 512]) for s in S2]
        pt_ps = [ps(f"pt{f}", [P, 512]) for f in range(2)]
        q_at, k_at, o_at = (slice(n * PADSEQ, n * PADSEQ + SEQ) for n in range(3))
        x_made, v_made, v_sb, y_made, half_made, h_made = (
            sem(n) for n in ("x_made", "v_made", "v_sb", "y_made", "half_made", "h_made"))
        qk_made, q_sb, k_sb, qbd_made, s_made, max_made, exp_made, rsum_made, prob_made, pt_made, pt0_sb, pt1_sb, o_made, oc_made = (
            sem(n) for n in ("qk_made", "q_sb", "k_sb", "qbd_made", "s_made", "max_made", "exp_made", "rsum_made",
                             "prob_made", "pt_made", "pt0_sb", "pt1_sb", "o_made", "oc_made"))
        set_up = sem("set_up")
        scores = lambda s: s_ps[s][0:R, 0:TILES * SEQ].rearrange("p (t k) -> p t k", k=SEQ)

        def step(i, g, s):
            return SLOTS * G * i + (SLOTS * g + s)

        with nc.Block() as block:
            @block.gpsimd
            def _(pool):
                for s in S2:
                    pool.memset(qbd[s][:], 0.0).then_inc(set_up, 1)
                    pool.memset(prob[s][:], 0.0).then_inc(set_up, 1)
                    pool.memset(xs[s][:], 0.0).then_inc(set_up, 1)
                pool.wait_ge(set_up, 6)
                with pool.Fori(0, BATCH // SLOTS) as i:
                    for s in S2:
                        b = pool.snap(SLOTS * i + s)
                        pool.wait_ge(h_made, freed(b))
                        pool.tensor_copy(xs[s][:, 0:SEQ], core.normed[:, ds(b * PADSEQ, SEQ)]).then_inc(x_made, 1)
                    for g in range(G):
                        for s in S2:
                            j = pool.snap(step(i, g, s))
                            pool.wait_ge(q_sb, j + 1)
                            pool.wait_ge(s_made, freed(j))
                            pool.tensor_tensor(qbd[s][:].rearrange("p (h q) -> p h q", q=QW)[:, :, 0:SEQ],
                                               qs[s][:].unsqueeze(1).broadcast_to([P, 2, SEQ]),
                                               W["hmask64"][:].unsqueeze(2).broadcast_to([P, 2, SEQ]),
                                               ALU.mult).then_inc(qbd_made, 1)
                        for s in S2:
                            j = pool.snap(step(i, g, s))
                            pool.wait_ge(rsum_made, j + 1)
                            pool.tensor_tensor(prob[s][:, :, 0:SEQ], prob[s][:, :, 0:SEQ],
                                               rinv[s][:].unsqueeze(2).broadcast_to([R, TILES, SEQ]),
                                               ALU.mult).then_inc(prob_made, 1)

            @block.tensor
            def _(pe):
                def projections(i, g, s):
                    j = pe.snap(step(i, g, s))
                    pe.wait_ge(k_sb, freed(j))
                    c = slice(g * P, (g + 1) * P)
                    pe.matmul(qk_ps[s][:, q_at], W["a3_wq"][:, c], xs[s][:, 0:SEQ], start=True, stop=True)
                    pe.matmul(qk_ps[s][:, k_at], W["a3_wk"][:, c], xs[s][:, 0:SEQ], start=True, stop=True).then_inc(qk_made, 1)

                def transposes_and_output(i, g, s):
                    j = pe.snap(step(i, g, s))
                    pe.wait_ge(prob_made, j + 1)
                    for f, emptied in ((0, pt0_sb), (1, pt1_sb)):
                        pe.wait_ge(emptied, j + 1)
                        for t in range(TILES):
                            mm = pe.transpose(pt_ps[f][0:HALF, t * R:(t + 1) * R],
                                              prob[s][:, t, f * HALF:(f + 1) * HALF], W["ident"][0:R, 0:R])
                        mm.then_inc(pt_made, 1)

                def output(i, g, s):
                    j = pe.snap(step(i, g, s))
                    pe.wait_ge(pt0_sb, j + 2)
                    pe.wait_ge(pt1_sb, j + 2)
                    pe.wait_ge(oc_made, freed(j))
                    for h in range(2):
                        for f in range(2):
                            d0 = g * P + h * HD
                            mm = pe.matmul(qk_ps[s][h * HD:(h + 1) * HD, o_at], vs[s][:, f, d0:d0 + HD],
                                           pt[s][:, f, h * QW:h * QW + SEQ], start=(f == 0), stop=(f == 1))
                    mm.then_inc(o_made, 1)

                pe.wait_ge(set_up, 6)
                with pe.Fori(0, BATCH // SLOTS) as i:
                    for s in S2:
                        b = pe.snap(SLOTS * i + s)
                        pe.wait_ge(h_made, freed(b))
                        pe.wait_ge(x_made, b + 1)
                        pe.wait_ge(v_sb, b + 1)
                        for f in range(2):
                            mm = pe.matmul(v_ps[0:HALF, f], xs[s][:, f * HALF:(f + 1) * HALF], W["a3_wv"][:],
                                           start=True, stop=True)
                        mm.then_inc(v_made, 1)
                        projections(i, 0, s)
                    for g in range(G):
                        for s in S2:
                            j = pe.snap(step(i, g, s))
                            pe.wait_ge(k_sb, made(j))
                            pe.wait_ge(qbd_made, j + 1)
                            pe.wait_ge(exp_made, freed(j))
                            for t in range(TILES):
                                mm = pe.matmul(scores(s)[:, t], qbd[s][:, t * R:(t + 1) * R], kt[s][:], start=True, stop=True)
                            mm.then_inc(s_made, 1)
                            if g + 1 < G:
                                projections(i, g + 1, s)
                        for s in S2:
                            transposes_and_output(i, g, s)
                        for s in S2:
                            if g == 0:
                                pe.wait_ge(v_sb, pe.snap(SLOTS * i + (s + 2)))
                            output(i, g, s)
                    for s in S2:
                        j = pe.snap(step(i, G - 1, s))
                        pe.wait_ge(oc_made, made(j))
                        for g in range(G):
                            mm = pe.matmul(qk_ps[s][:, q_at], W["a3_wo"][:, g], oc[s][:, g], start=(g == 0), stop=(g == G - 1))
                        mm.then_inc(y_made, 1)

            @block.scalar
            def _(act):
                with act.Fori(0, BATCH // SLOTS) as i:
                    for g in range(G):
                        for s in S2:
                            j = act.snap(step(i, g, s))
                            act.wait_ge(qk_made, j + 1)
                            act.wait_ge(s_made, freed(j))
                            act.activation(qs[s][:], qk_ps[s][:, q_at], ACT.Copy, scale=SCALE).then_inc(q_sb, 1)
                            act.activation(kt[s][:], qk_ps[s][:, k_at], ACT.Copy).then_inc(k_sb, 1)
                        for s in S2:
                            j = act.snap(step(i, g, s))
                            act.wait_ge(max_made, j + 1)
                            act.wait_ge(pt_made, 2 * j + 2)
                            for t in range(TILES):
                                a = act.activation(prob[s][:, t, 0:SEQ], scores(s)[:, t], ACT.Exp, bias=negmax[s][:, t:t + 1],
                                                   accum_out=rsum[s][:, t:t + 1])
                            a.then_inc(exp_made, 1)
                        for s in S2:
                            j = act.snap(step(i, g, s))
                            act.wait_ge(pt_made, 2 * j + (1 + 2 * SLOTS))
                            act.wait_ge(o_made, freed(j))
                            act.activation(pt[s][:, 0], pt_ps[0][0:HALF, 0:ROWS], ACT.Copy).then_inc(pt0_sb, 1)
                        for s in S2:
                            j = act.snap(step(i, g, s))
                            act.wait_ge(o_made, made(j))
                            act.activation(oc[s][:, g], qk_ps[s][:, o_at], ACT.Copy).then_inc(oc_made, 1)

            @block.vector
            def _(ve):
                ve.sem_inc(h_made, SLOTS)
                ve.sem_inc(exp_made, SLOTS)
                ve.sem_inc(pt_made, 2 * SLOTS)
                for c in (pt0_sb, pt1_sb, v_sb):
                    ve.sem_inc(c, 1)
                for c in (k_sb, s_made, oc_made, o_made):
                    ve.sem_inc(c, SLOTS)
                with ve.Fori(0, BATCH // SLOTS) as i:
                    for s in S2:
                        b = ve.snap(SLOTS * i + s)
                        ve.wait_ge(v_made, b + 1)
                        ve.tensor_copy(vs[s][:], v_ps[0:HALF]).then_inc(v_sb, 1)
                    for g in range(G):
                        for s in S2:
                            j = ve.snap(step(i, g, s))
                            ve.wait_ge(s_made, made(j))
                            ve.tensor_reduce(negmax[s][:], scores(s), AX.X, ALU.max, negate=True).then_inc(max_made, 1)
                        for s in S2:
                            j = ve.snap(step(i, g, s))
                            ve.wait_ge(exp_made, made(j))
                            ve.reciprocal(rinv[s][:], rsum[s][:]).then_inc(rsum_made, 1)
                        for s in S2:
                            j = ve.snap(step(i, g, s))
                            ve.wait_ge(pt_made, 2 * j + (2 + 2 * SLOTS))
                            ve.wait_ge(o_made, freed(j))
                            ve.tensor_copy(pt[s][:, 1], pt_ps[1][0:HALF, 0:ROWS]).then_inc(pt1_sb, 1)
                    for s in S2:
                        b = ve.snap(SLOTS * i + s)
                        h_b = core.h[:, ds(b * SEQ, SEQ)]
                        ve.wait_ge(y_made, b + 1)
                        ve.tensor_tensor(h_b, h_b, xs[s][:, 0:SEQ], ALU.add).then_inc(half_made, 1)
                        ve.wait_ge(half_made, b + 1)
                        ve.tensor_tensor(h_b, h_b, qk_ps[s][:, q_at], ALU.add).then_inc(h_made, 1)


def gated_expert(nc, core):
    EXPERTS = 16
    W = core.w
    S2 = range(SLOTS)
    with ExitStack() as ctx:
        sb = lambda name, shape, dt=F32: ctx.enter_context(nc.sbuf_tensor(f"f3_{name}", shape, dt))
        ps = lambda name, shape: ctx.enter_context(nc.psum_tensor(f"f3_{name}_ps", shape, F32))
        sem = lambda name: core.keep(nc.semaphore(f"f3_{name}"))
        mean = sb("mean", [P, BATCH])
        ones = sb("ones", [BATCH, P])
        logit = sb("logit", [BATCH, EXPERTS])
        ranked = sb("ranked", [BATCH, 8])
        which = sb("which", [BATCH, 8], U32)
        neg_top = sb("neg_top", [BATCH, 1])
        term = sb("term", [BATCH, EXPERTS])
        total = sb("total", [BATCH, 1])
        gate = sb("gate", [BATCH, 1])
        which_f = sb("which_f", [BATCH, 1])
        chosen = sb("chosen", [BATCH, EXPERTS])
        gate_diag = sb("gate_diag", [BATCH, BATCH])
        chosen_t = sb("chosen_t", [EXPERTS, BATCH])
        which_row = sb("which_row", [1, BATCH], I32)
        gates = sb("gates", [P, BATCH])
        biases = sb("biases", [P, BATCH])
        w_sel = [sb(f"w_sel{s}", [P, P]) for s in S2]
        small_ps = ps("small", [P, 512])
        y_ps = [ps(f"y{s}", [P, 512]) for s in S2]
        v, pe_, a_ = (sem(n) for n in ("route", "route_pe", "route_act"))
        w_made, y_made, h_made = (sem(n) for n in ("w_made", "y_made", "h_made"))
        res = core.h[:, 0:TOK].rearrange("p (b n) -> p b n", n=SEQ)

        with nc.Block() as block:
            @block.tensor
            def _(pe):
                pe.wait_ge(v, 3)
                pe.matmul(small_ps[0:BATCH, 0:EXPERTS], mean[:], W["f3_wg"][:], start=True, stop=True).then_inc(pe_, 1)
                pe.wait_ge(v, 11)
                pe.transpose(small_ps[0:EXPERTS, 32:32 + BATCH], chosen[:], W["ident"][0:BATCH, 0:BATCH])
                pe.transpose(small_ps[0:1, 64:64 + BATCH], which_f[:], W["ident"][0:BATCH, 0:BATCH])
                pe.matmul(small_ps[:, 96:96 + BATCH], ones[:], gate_diag[:], start=True, stop=True).then_inc(pe_, 1)
                pe.wait_ge(v, 14)
                pe.matmul(small_ps[:, 128:128 + BATCH], W["f3_be"][:], chosen_t[:], start=True, stop=True).then_inc(pe_, 1)
                with pe.Fori(0, BATCH // SLOTS) as i:
                    for s in S2:
                        b = pe.snap(SLOTS * i + s)
                        pe.wait_ge(w_made, b + 1)
                        pe.wait_ge(h_made, freed(b))
                        pe.matmul(y_ps[s][:, 0:SEQ], w_sel[s][:], core.normed[:, ds(b * SEQ, SEQ)],
                                  start=True, stop=True).then_inc(y_made, 1)

            @block.scalar
            def _(act):
                act.wait_ge(v, 7)
                act.activation(term[:], logit[:], ACT.Exp, bias=neg_top[:, 0:1], accum_out=total[:, 0:1]).then_inc(a_, 1)

            @block.gpsimd
            def _(pool):
                pool.wait_ge(v, 13)
                with pool.Fori(0, BATCH // SLOTS) as i:
                    for s in S2:
                        b = pool.snap(SLOTS * i + s)
                        e = pool.value_load(which_row[0:1, ds(b, 1)], min_val=0, max_val=EXPERTS - 1)
                        pool.wait_ge(y_made, freed(b))
                        pool.tensor_tensor(w_sel[s][:], W["f3_we"][:, ds(e * P, P)],
                                           gates[:, ds(b, 1)].broadcast_to([P, P]), ALU.mult).then_inc(w_made, 1)

            @block.vector
            def _(ve):
                ve.sem_inc(y_made, SLOTS)
                ve.sem_inc(h_made, SLOTS)
                ve.memset(ones[:], 1.0).then_inc(v, 1)
                ve.tensor_reduce(mean[:], core.normed[:, 0:TOK].rearrange("p (b n) -> p b n", n=SEQ), AX.X, ALU.add).then_inc(v, 1)
                ve.wait_ge(v, 2)
                ve.tensor_scalar(mean[:], mean[:], 1.0 / SEQ, None, ALU.mult).then_inc(v, 1)
                ve.wait_ge(pe_, 1)
                ve.tensor_tensor(logit[:], small_ps[0:BATCH, 0:EXPERTS], W["f3_bg"][:], ALU.add).then_inc(v, 1)
                ve.wait_ge(v, 4)
                ve.max(ranked[:], logit[:]).then_inc(v, 1)
                ve.wait_ge(v, 5)
                ve.max_index(which[:], ranked[:], logit[:]).then_inc(v, 1)
                ve.tensor_scalar(neg_top[:], ranked[:, 0:1], -1.0, None, ALU.mult).then_inc(v, 1)
                ve.wait_ge(v, 6)
                ve.tensor_copy(which_f[:], which[:, 0:1]).then_inc(v, 1)
                ve.wait_ge(a_, 1)
                ve.reciprocal(gate[:], total[:]).then_inc(v, 1)
                ve.wait_ge(v, 9)
                ve.tensor_scalar(chosen[:], W["f3_numbers"][:], which_f[:, 0:1], gate[:, 0:1], ALU.is_equal, ALU.mult).then_inc(v, 1)
                ve.tensor_scalar(gate_diag[:], W["ident"][0:BATCH, 0:BATCH], gate[:, 0:1], None, ALU.mult).then_inc(v, 1)
                ve.wait_ge(pe_, 2)
                ve.tensor_copy(gates[:], small_ps[:, 96:96 + BATCH]).then_inc(v, 1)
                ve.tensor_copy(which_row[:], small_ps[0:1, 64:64 + BATCH]).then_inc(v, 1)
                ve.tensor_copy(chosen_t[:], small_ps[0:EXPERTS, 32:32 + BATCH]).then_inc(v, 1)
                ve.wait_ge(pe_, 3)
                ve.tensor_copy(biases[:], small_ps[:, 128:128 + BATCH]).then_inc(v, 1)
                ve.wait_ge(v, 15)
                ve.tensor_tensor(res, res, biases[:].unsqueeze(2).broadcast_to([P, BATCH, SEQ]), ALU.add).then_inc(v, 1)
                ve.wait_ge(v, 16)
                with ve.Fori(0, BATCH // SLOTS) as i:
                    for s in S2:
                        b = ve.snap(SLOTS * i + s)
                        ve.wait_ge(y_made, made(b))
                        h_b = core.h[:, ds(b * SEQ, SEQ)]
                        ve.tensor_tensor(h_b, h_b, y_ps[s][:, 0:SEQ], ALU.add).then_inc(h_made, 1)


def store_output(nc, core, out):
    with nc.semaphore("stored") as stored, nc.Block() as block:
        @block.sync
        def _(sp):
            for q in range(4):
                sp.dma_start(out[:, q * TOK // 4:(q + 1) * TOK // 4], core.h[:, q * TOK // 4:(q + 1) * TOK // 4]).then_inc(stored, 16)
            sp.wait_ge(stored, 64)


def build(nc, dram, shapes, out, stop=8):
    with ExitStack() as ctx:
        core = Core()
        core.keep = ctx.enter_context
        core.norms = 0
        core.norm_sems = [core.keep(nc.semaphore("ln_" + n)) for n in
                          ("mean_made", "cent_made", "sq_act", "sq_pool", "var_made", "std_made", "rstd_made", "spread_made", "normed_made")]
        core.h = ctx.enter_context(nc.sbuf_tensor("h", [P, TOKPAD], F32))
        core.normed = ctx.enter_context(nc.sbuf_tensor("normed", [P, TOKPAD], F32))
        core.mean_mat = ctx.enter_context(nc.sbuf_tensor("mean_mat", [P, P], F32))
        core.first_row = ctx.enter_context(nc.sbuf_tensor("first_row", [P, P], F32))
        core.eps = ctx.enter_context(nc.sbuf_tensor("eps", [P, 1], F32))
        core.weights_in = ctx.enter_context(nc.semaphore("weights_in"))
        core.weight_names = [n for n in shapes if n not in BLOCK_OWN]
        core.n_weights = len(core.weight_names)
        core.w = {n: ctx.enter_context(nc.sbuf_tensor("w_" + n, list(shapes[n]), F32)) for n in core.weight_names}
        core.projections = 0
        core.project_sems = [core.keep(nc.semaphore("proj_" + n)) for n in
                             ("bqs_made", "conv_step", "x_made", "qk_made", "v_made", "q_sb", "k_sb", "v_sb")]
        cleared = core.keep(nc.semaphore("cleared"))
        with nc.Block() as block:
            @block.vector
            def _(ve):
                ve.memset(core.mean_mat[:], 1.0 / P)
                ve.memset(core.eps[:], EPS)
                ve.memset(core.first_row[:], 0.0).then_inc(cleared, 1)
                ve.wait_ge(cleared, 1)
                for k in range(4):
                    ve.memset(core.first_row[32 * k:32 * k + 1, :], 1.0)
                ve.memset(core.h[:, TOK:TOKPAD], 0.0)
                ve.memset(core.normed[:], 0.0)
        padded = core.normed[:, 0:BATCH * PADSEQ].rearrange("p (b n) -> p b n", n=PADSEQ)
        padded_out = lambda n: padded[:, ds(2 * n, 2), 0:SEQ]
        flat = core.normed[:, 0:TOK].rearrange("p (b n) -> p b n", n=SEQ)
        flat_out = lambda n: flat[:, ds(2 * n, 2), :]
        tokens_of_patches(nc, core, dram)
        layernorm(nc, core, "a0_ln", padded_out)
        narrow_attention(nc, core, "a0", projected=False, top_k=False, conv=False)
        layernorm(nc, core, "m_ln", flat_out)
        routed_experts(nc, core, dram)
        layernorm(nc, core, "a1_ln", flat_out)
        head_mixing(nc, core)
        window_projection(nc, core)
        layernorm(nc, core, "f1_ln", flat_out)
        trig_ffn(nc, core)
        layernorm(nc, core, "a2_ln", padded_out)
        decay_retrieval(nc, core)
        layernorm(nc, core, "f2_ln", padded_out)
        narrow_attention(nc, core, "f2", projected=True, top_k=True, conv=True)
        layernorm(nc, core, "a3_ln", padded_out)
        wide_attention(nc, core)
        layernorm(nc, core, "f3_ln", flat_out)
        gated_expert(nc, core)
        store_output(nc, core, out)


BLOCK_OWN = {"x", "txt", "w0", "w1", "sw0", "sw1", "eo0", "eo1", "eps0", "eps1", "bias0", "bias1", "w3", "b3", "pe",
             "expert_rows", "expert_ids", "m_w1", "m_w2"}


def lay_out(np, a):
    c = np.ascontiguousarray
    blocks = lambda m: m.reshape(m.shape[0] // P, P, -1).transpose(1, 0, 2)
    col = lambda v: v.reshape(-1, P).T
    x = a["x"].reshape(BATCH, 8, 16, 8, 16).transpose(0, 1, 3, 2, 4).reshape(BATCH * PATCHES, 256)
    pos = np.arange(PATCHES, dtype=np.float32)[:, None]
    div = np.exp(np.arange(0, P, 2, dtype=np.float32) * np.float32(-np.log(10000.0) / P))
    ang = (pos * div).astype(np.float32)
    pe = np.stack([np.sin(ang), np.cos(ang)], axis=-1).reshape(PATCHES, P).astype(np.float32)
    d = {"x": blocks(x.T), "txt": a["txt"].transpose(2, 0, 1), "pe": pe.T}
    for l, name in enumerate(("W1", "W2")):
        t = f"L0_tok_{name}"
        d[f"w{l}"] = blocks(a[t + "_w"].T)
        d[f"sw{l}"] = blocks(a[t + "_sw"].T)
        d[f"eo{l}"] = a[f"L0_tok_eps_out{l + 1}"]
        d[f"eps{l}"] = np.concatenate([col(a[f"L0_tok_eps_in{l + 1}"]), col(a[f"L0_tok_eps_out{l + 1}"])], axis=1)
        d[f"bias{l}"] = np.stack([a[t + "_b"], a[t + "_sb"]], axis=1)
    d["w3"] = a["L0_tok_W3_w"].T
    d["b3"] = a["L0_tok_W3_b"][:, None]
    d["hmask16"] = np.repeat(np.eye(8, dtype=np.float32), 16, axis=0)
    d["ident"] = np.eye(P, dtype=np.float32)
    d["a0_wq"], d["a0_wk"], d["a0_wv"] = a["L0_attn_Wq"].T, a["L0_attn_Wk"].T, a["L0_attn_Wk"].T
    d["a0_bq"], d["a0_bk"], d["a0_bv"] = (a["L0_attn_" + n][:, None] for n in ("bq", "bk", "bk"))
    d["expert_ids"], d["expert_rows"] = a["L0_ffn_expert_indices"].T, a["L0_ffn_expert_weights"].T
    d["m_w1"] = a["L0_ffn_w1"]
    d["m_w2"] = a["L0_ffn_w2"].reshape(8, 4, P, P).transpose(0, 2, 1, 3)
    d["ident"] = np.eye(P, dtype=np.float32)
    d["hmask16"] = np.repeat(np.eye(8, dtype=np.float32), 16, axis=0)
    d["a1_wqkv"], d["wp_b"] = a["L1_attn_w_qkv"].T, a["L1_attn_b_proj"][:, None]
    d["wp_w"] = np.tile(a["L1_attn_w_proj"].reshape(P, 8, 16).transpose(2, 1, 0), (8, 1, 1))
    d["f1_w"], d["f1_b"] = a["L1_ffn_W"].T, a["L1_ffn_B_param"].T
    d["f1_attn_cos"], d["f1_attn_sin"] = a["L1_ffn_attn_cos"].T, a["L1_ffn_attn_sin"].T
    proj = np.stack([a["L1_ffn_proj_cos_w"].T, a["L1_ffn_proj_sin_w"].T])
    d["f1_proj"] = proj.reshape(2, 16, 4, P).transpose(2, 0, 1, 3).reshape(P, P)
    d["a2_basis"], d["a2_vc"], d["a2_oc"] = (a["L2_attn_" + n].T for n in ("basis", "v_coeffs", "o_coeffs"))
    d["a2_wq"], d["a2_wk"] = a["L2_attn_shared_q_w"], a["L2_attn_shared_k_w"]
    d["a2_decay"] = np.broadcast_to(a["L2_attn_decay_logits"], (P, 4))
    d["a2_out_scale"] = np.broadcast_to(a["L2_attn_out_scale"], (P, 1))
    after = (np.arange(71)[:, None, None] + 71 * np.arange(2)[None, :, None]) - np.arange(SEQ)[None, None, :]
    d["a2_distance"] = np.maximum(after - 1, 0).astype(np.float32)
    d["a2_later"] = ((after > 0) & (after - 1 < SEQ)).astype(np.float32)
    d["hmask16"] = np.repeat(np.eye(8, dtype=np.float32), 16, axis=0)
    d["ident"] = np.eye(P, dtype=np.float32)
    for n, m in enumerate("qkv"):
        d["f2_w" + m] = a["L2_ffn_qkv_w"][n * P:(n + 1) * P].T
        d["f2_b" + m] = a["L2_ffn_qkv_b"][n * P:(n + 1) * P, None]
    d["f2_wo"], d["f2_bo"] = a["L2_ffn_wo_w"].T, a["L2_ffn_wo_b"][:, None]
    d["f2_pos_w"], d["f2_pos_b"] = a["L2_ffn_pos_w"][:, 0], a["L2_ffn_pos_b"][:, None]
    d["hmask64"] = np.repeat(np.eye(2, dtype=np.float32), 64, axis=0)
    d["ident"] = np.eye(P, dtype=np.float32)
    d["a3_wq"], d["a3_wk"], d["a3_wv"] = (a["L3_attn_" + n].T for n in ("Wq", "Wk", "Wv"))
    d["a3_wo"] = a["L3_attn_Wo"].T.reshape(4, P, P).transpose(1, 0, 2)
    d["ident"] = np.eye(P, dtype=np.float32)
    d["f3_wg"], d["f3_be"] = a["L3_ffn_Wg"], a["L3_ffn_be"]
    d["f3_bg"] = np.broadcast_to(a["L3_ffn_bg"], (BATCH, 16))
    d["f3_numbers"] = np.broadcast_to(np.arange(16, dtype=np.float32), (BATCH, 16))
    d["f3_we"] = a["L3_ffn_We"].transpose(1, 0, 2).reshape(P, 16 * P)
    return {k: c(v) for k, v in d.items()}


def kernel(**inputs):
    import numpy as _np
    import concourse.bacc as _bacc
    from concourse import mybir as _mybir
    from concourse.bass_utils import run_bass_kernel_spmd as _run

    arrays = lay_out(_np, {k: _np.asarray(v) for k, v in inputs.items()})
    nc = _bacc.Bacc("TRN2", target_bir_lowering=False, num_devices=1)
    dram = {k: nc.dram_tensor("in_" + k, list(v.shape), _mybir.dt.from_np(v.dtype), kind="ExternalInput").ap()
            for k, v in arrays.items()}
    out = nc.dram_tensor("out_h", [P, TOK], _mybir.dt.float32, kind="ExternalOutput").ap()
    build(nc, dram, {k: v.shape for k, v in arrays.items()}, out)
    r = _run(nc, [{"in_" + k: v for k, v in arrays.items()}], core_ids=[0])
    return _np.ascontiguousarray(r.results[0]["out_h"].reshape(P, BATCH, SEQ).transpose(1, 2, 0))
```

```python
import math
from contextlib import ExitStack

import concourse.bass as bass
from concourse import mybir

F32 = mybir.dt.float32
I32 = mybir.dt.int32
U32 = mybir.dt.uint32
I16 = mybir.dt.int16
ALU = mybir.AluOpType
ACT = mybir.ActivationFunctionType
AX = mybir.AxisListType

P = 128
BATCH = 32
PATCHES = 64
TEXT = 77
SEQ = PATCHES + TEXT
TOK = BATCH * SEQ
HALF = 71
PADSEQ = 2 * HALF
CHUNK = 512
TOKPAD = -(-TOK // CHUNK) * CHUNK
EPS = 1e-5
SLOTS = 2
GONE = -3.0e38


def made(n, slots=SLOTS):
    return n + (1 + slots)


def freed(n):
    return n + 1


class Core:
    def ready_after(self, steps):
        self.steps_set_up += steps
        return self.steps_set_up


def ds(start, size):
    return bass.ds(start, size)


def tokens_of_patches(nc, core, dram):
    with ExitStack() as ctx:
        sb = lambda name, shape, dt=F32: ctx.enter_context(nc.sbuf_tensor("tok_" + name, shape, dt))
        ps = lambda name, shape: ctx.enter_context(nc.psum_tensor("tok_" + name, shape, F32))
        sem = lambda name: core.keep(nc.semaphore("tok_" + name))
        GB = 8
        CH = BATCH // GB
        w = sb("w", [P, 2, 2, P])
        sw = sb("sw", [P, 2, 2, P])
        eo_row = sb("eo_row", [P, 2, P])
        eps_col = sb("eps_col", [P, 2, 3])
        bias = sb("bias", [P, 2, 2])
        b3 = sb("b3", [P, 1])
        w3 = sb("w3", [P, P])
        pe_tab = sb("pe", [P, PATCHES])
        x = [sb(f"x{s}", [P, 2, CHUNK]) for s in range(2)]
        t_row = sb("t_row", [P, 2, P])
        t_col = sb("t_col", [P, 2, 3])
        s_row = sb("s_row", [P, 2, P])
        s_col = sb("s_col", [P, 2, 3])
        noise = sb("noise", [P, 2, 2, P])
        bn = sb("bn", [P, 2])
        gate = [sb(f"gate{s}", [P, CHUNK]) for s in range(2)]
        inner = [sb(f"inner{s}", [P, CHUNK]) for s in range(2)]
        u = [sb(f"u{s}", [P, CHUNK]) for s in range(2)]
        v = [sb(f"v{s}", [P, CHUNK]) for s in range(2)]
        g_ps = [ps(f"g{s}", [P, CHUNK]) for s in range(2)]
        i_ps = [ps(f"i{s}", [P, CHUNK]) for s in range(2)]
        y_ps = [ps(f"y{s}", [P, CHUNK]) for s in range(2)]
        small_in = sem("small_in")
        x_in = [sem(f"x_in{s}") for s in range(2)]
        text_in = sem("text_in")
        root = sem("root")
        prep = sem("prep")
        prepared = sem("prepared")
        gate_ready = sem("gate_ready")
        proj = sem("proj")
        act_done = sem("act_done")
        dve = sem("dve")
        mixed = sem("mixed")
        y_ready = sem("y_ready")
        SMALL = 13

        def load_layer(eng, l):
            for to, name in ((eps_col, "eps"), (bias, "bias"), (w, "w"), (sw, "sw")):
                eng.dma_start(to[:, l], dram[f"{name}{l}"]).then_inc(small_in, 16)

        with nc.Block() as block:
            @block.sync
            def _(sp):
                for l in range(2):
                    sp.dma_start(eo_row[:, l], dram[f"eo{l}"].partition_broadcast(P)).then_inc(small_in, 16)
                load_layer(sp, 0)
                sp.dma_start(w3[:], dram["w3"]).then_inc(small_in, 16)
                sp.dma_start(b3[:], dram["b3"]).then_inc(small_in, 16)
                sp.dma_start(pe_tab[:], dram["pe"]).then_inc(small_in, 16)
                for c in range(CH):
                    if c == 2:
                        for name in core.weight_names:
                            sp.dma_start(core.w[name][:], dram[name]).then_inc(core.weights_in, 16)
                    if c >= 2:
                        sp.wait_ge(proj, c - 1)
                    sp.dma_start(x[c % 2][:], dram["x"][:, :, c * CHUNK:(c + 1) * CHUNK]).then_inc(x_in[c % 2], 16)

            @block.gpsimd
            def _(pool):
                pool.dma_start(core.h[:, 0:TOK].rearrange("p (b n) -> p b n", n=SEQ)[:, :, PATCHES:SEQ],
                               dram["txt"]).then_inc(text_in, 16)
                pool.wait_ge(text_in, 16)
                pool.wait_ge(core.weights_in, 16 * core.n_weights)

            @block.scalar
            def _(act):
                load_layer(act, 1)
                act.wait_ge(prep, 2)
                act.activation(s_row[:], t_row[:], ACT.Sqrt).then_inc(root, 1)
                act.activation(s_col[:], t_col[:], ACT.Sqrt).then_inc(root, 1)
                act.wait_ge(prepared, 1)
                for pair in range(CH // 2):
                    for s in range(2):
                        act.wait_ge(proj, 2 * pair + s + 1)
                        if pair:
                            act.wait_ge(y_ready, 4 * (pair - 1) + s + 1)
                        act.activation(gate[s][:], g_ps[s][:], ACT.Identity, bias=bn[:, 0:1]).then_inc(gate_ready, 1)
                        act.activation(inner[s][:], i_ps[s][:], ACT.Identity, bias=bn[:, 1:2]).then_inc(act_done, 1)
                    for s in range(2):
                        act.wait_ge(dve, 10 * pair + s + 1)
                        act.activation(u[s][:], v[s][:], ACT.Exp).then_inc(act_done, 1)

            @block.tensor
            def _(pe):
                pe.wait_ge(prepared, 1)
                def projections(pair):
                    for s in range(2):
                        pe.wait_ge(x_in[s], 16 * (pair + 1))
                        if pair:
                            pe.wait_ge(act_done, 4 * (pair - 1) + s + 1)
                        for l, out in ((0, g_ps[s]), (1, i_ps[s])):
                            for k in range(2):
                                mm = pe.matmul(out[:], noise[:, l, k], x[s][:, k], start=(k == 0), stop=(k == 1))
                        mm.then_inc(proj, 1)

                projections(0)
                for pair in range(CH // 2):
                    if pair + 1 < CH // 2:
                        projections(pair + 1)
                    for s in range(2):
                        if pair:
                            pe.wait_ge(y_ready, 4 * (pair - 1) + s + 3)
                        pe.wait_ge(mixed, 2 * pair + s + 1)
                        pe.matmul(y_ps[s][:], w3[:], gate[s][:], start=True, stop=True).then_inc(y_ready, 1)

            @block.vector
            def _(ve):
                ve.wait_ge(small_in, 16 * SMALL)
                ve.scalar_tensor_tensor(t_row[:], eo_row[:], -1.0, eo_row[:], ALU.mult, ALU.max).then_inc(prep, 1)
                ve.scalar_tensor_tensor(t_col[:], eps_col[:], -1.0, eps_col[:], ALU.mult, ALU.max).then_inc(prep, 1)
                ve.wait_ge(root, 2)
                ve.tensor_scalar(t_row[:], eo_row[:], 0.0, 2.0, ALU.is_ge, ALU.mult).then_inc(prep, 1)
                ve.tensor_scalar(t_col[:], eps_col[:], 0.0, 2.0, ALU.is_ge, ALU.mult).then_inc(prep, 1)
                ve.wait_ge(prep, 4)
                ve.scalar_tensor_tensor(s_row[:], t_row[:], -1.0, s_row[:], ALU.add, ALU.mult).then_inc(prep, 1)
                ve.scalar_tensor_tensor(s_col[:], t_col[:], -1.0, s_col[:], ALU.add, ALU.mult).then_inc(prep, 1)
                ve.wait_ge(prep, 6)
                for l in range(2):
                    for k in range(2):
                        ve.scalar_tensor_tensor(noise[:, l, k], s_row[:, l], s_col[:, l, k:k + 1], sw[:, l, k],
                                                ALU.mult, ALU.mult).then_inc(prep, 1)
                    ve.tensor_tensor(bn[:, l:l + 1], bias[:, l, 1:2], s_col[:, l, 2:3], ALU.mult).then_inc(prep, 1)
                ve.wait_ge(prep, 12)
                ve.tensor_tensor(noise[:], noise[:], w[:], ALU.add).then_inc(prep, 1)
                ve.tensor_tensor(bn[:], bn[:], bias[:, :, 0], ALU.add).then_inc(prep, 1)
                ve.wait_ge(prep, 14)
                ve.sem_inc(prepared, 1)
                for pair in range(CH // 2):
                    d0, p0 = 10 * pair, 14 + 4 * pair
                    for s in range(2):
                        ve.wait_ge(gate_ready, 2 * pair + s + 1)
                        ve.tensor_scalar(v[s][:], gate[s][:], 20.0, None, ALU.min).then_inc(dve, 1)
                    for s in range(2):
                        ve.wait_ge(act_done, 4 * pair + s + 3)
                        ve.scalar_tensor_tensor(v[s][:], u[s][:], 2.0, u[s][:], ALU.add, ALU.mult).then_inc(dve, 1)
                    for s in range(2):
                        ve.wait_ge(dve, d0 + s + 3)
                        ve.tensor_scalar(u[s][:], v[s][:], 2.0, None, ALU.add).then_inc(dve, 1)
                    for s in range(2):
                        ve.wait_ge(dve, d0 + s + 5)
                        ve.tensor_tensor(v[s][:], v[s][:], inner[s][:], ALU.mult).then_inc(dve, 1)
                        ve.reciprocal(u[s][:], u[s][:]).then_inc(dve, 1)
                        ve.wait_ge(dve, d0 + 2 * s + 7)
                        ve.tensor_tensor(gate[s][:], gate[s][:], v[s][:], ALU.mult).then_inc(prep, 1)
                        ve.wait_ge(dve, d0 + 2 * s + 8)
                        ve.wait_ge(prep, p0 + s + 1)
                        ve.tensor_tensor(gate[s][:], gate[s][:], u[s][:], ALU.mult).then_inc(mixed, 1)
                    for s in range(2):
                        c = 2 * pair + s
                        ve.wait_ge(y_ready, 4 * pair + s + 1)
                        ve.scalar_tensor_tensor(u[s][:].rearrange("p (b n) -> p b n", n=PATCHES),
                                                y_ps[s][:].rearrange("p (b n) -> p b n", n=PATCHES), b3[:, 0:1],
                                                pe_tab[:].unsqueeze(1).broadcast_to([P, GB, PATCHES]), ALU.add, ALU.add).then_inc(prep, 1)
                    for s in range(2):
                        c = 2 * pair + s
                        ve.wait_ge(prep, p0 + s + 3)
                        ve.tensor_copy(core.h[:, 0:TOK].rearrange("p (b n) -> p b n", n=SEQ)[:, c * GB:(c + 1) * GB, 0:PATCHES],
                                       u[s][:].rearrange("p (b n) -> p b n", n=PATCHES)).then_inc(y_ready, 1)


def layernorm(nc, core, tag, out_ap):
    N = 2 * SEQ
    PAIRS = 4
    UNITS = TOK // (N * PAIRS)
    ROWS = P // PAIRS
    with ExitStack() as ctx:
        sb = lambda name, shape: ctx.enter_context(nc.sbuf_tensor(f"{tag}_{name}", shape, F32))
        ps = lambda name, shape: ctx.enter_context(nc.psum_tensor(f"{tag}_{name}_ps", shape, F32))
        cent = [sb(f"cent{u}", [P, PAIRS, N]) for u in range(UNITS)]
        sq = [sb(f"sq{s}", [P, PAIRS, N]) for s in range(2)]
        std = [sb(f"std{u}", [P, N]) for u in range(UNITS)]
        mean_ps = [ps(f"mean{s}", [P, 512]) for s in range(2)]
        var_ps = [ps(f"var{s}", [P, 512]) for s in range(2)]
        rstd_ps = [ps(f"rstd{k}", [P, 512]) for k in range(PAIRS)]
        mean_made, cent_made, sq_act, sq_pool, var_made, std_made, rstd_made, spread_made, normed_made = core.norm_sems
        unit0 = UNITS * core.norms
        pair0 = PAIRS * unit0
        core.norms += 1

        with nc.Block() as block:
            @block.tensor
            def _(pe):
                def means(u):
                    for k in range(PAIRS):
                        n = PAIRS * u + k
                        if n >= 2:
                            pe.wait_ge(cent_made, pair0 + n - 1)
                        pe.matmul(mean_ps[k % 2][:, 0:N], core.mean_mat[:], core.h[:, n * N:(n + 1) * N],
                                  start=True, stop=True).then_inc(mean_made, 1)

                def variances(u):
                    pe.wait_ge(sq_act, 2 * (unit0 + u + 1))
                    pe.wait_ge(sq_pool, 2 * (unit0 + u + 1))
                    if u >= 2:
                        pe.wait_ge(std_made, unit0 + u - 1)
                    for k in range(PAIRS):
                        mm = pe.matmul(var_ps[u % 2][k * ROWS:(k + 1) * ROWS, 0:N], core.mean_mat[:, 0:ROWS], sq[u % 2][:, k],
                                       start=True, stop=True)
                    mm.then_inc(var_made, 1)

                def spread(u):
                    pe.wait_ge(rstd_made, unit0 + u + 1)
                    if u:
                        pe.wait_ge(normed_made, pair0 + PAIRS * u)
                    for k in range(PAIRS):
                        rows = slice(k * ROWS, (k + 1) * ROWS)
                        mm = pe.matmul(rstd_ps[k][:, 0:N], core.first_row[rows, :], std[u][rows, :], start=True, stop=True)
                    mm.then_inc(spread_made, 1)

                means(0)
                means(1)
                variances(0)
                for u in range(2, UNITS):
                    means(u)
                    spread(u - 2)
                    variances(u - 1)
                spread(UNITS - 2)
                variances(UNITS - 1)
                spread(UNITS - 1)

            def squares(u, eng, first, counted, square):
                for k in range(first, PAIRS, 2):
                    eng.wait_ge(cent_made, pair0 + PAIRS * u + k + 1)
                    if u >= 2:
                        eng.wait_ge(var_made, unit0 + u - 1)
                    square(sq[u % 2][:, k], cent[u][:, k]).then_inc(counted, 1)

            @block.gpsimd
            def _(pool):
                for u in range(UNITS):
                    squares(u, pool, 1, sq_pool, lambda out, x: pool.tensor_tensor(out, x, x, ALU.mult))

            @block.scalar
            def _(act):
                def root(u):
                    act.wait_ge(var_made, unit0 + u + 1)
                    act.activation(std[u][:], var_ps[u % 2][:, 0:N], ACT.Sqrt, bias=core.eps[:, 0:1]).then_inc(std_made, 1)

                for u in range(UNITS):
                    squares(u, act, 0, sq_act, lambda out, x: act.activation(out, x, ACT.Square))
                    if u:
                        root(u - 1)
                root(UNITS - 1)

            @block.vector
            def _(ve):
                def centre(u):
                    for k in range(PAIRS):
                        n = PAIRS * u + k
                        ve.wait_ge(mean_made, pair0 + n + 1)
                        ve.tensor_tensor(cent[u][:, k], core.h[:, n * N:(n + 1) * N], mean_ps[k % 2][:, 0:N],
                                         ALU.subtract).then_inc(cent_made, 1)

                def reciprocal(u):
                    ve.wait_ge(std_made, unit0 + u + 1)
                    ve.reciprocal(std[u][:], std[u][:]).then_inc(rstd_made, 1)

                def scale(u):
                    ve.wait_ge(spread_made, unit0 + u + 1)
                    for k in range(PAIRS):
                        ve.tensor_tensor(out_ap(PAIRS * u + k), cent[u][:, k].rearrange("p (b n) -> p b n", n=SEQ),
                                         rstd_ps[k][:, 0:N].rearrange("p (b n) -> p b n", n=SEQ), ALU.mult).then_inc(normed_made, 1)

                centre(0)
                centre(1)
                for u in range(2, UNITS):
                    reciprocal(u - 2)
                    centre(u)
                    scale(u - 2)
                for u in range(UNITS - 2, UNITS):
                    reciprocal(u)
                    scale(u)


def project_heads(nc, core, tag, conv, q_all, k_all, v_all):
    SCALE = float(P) ** -0.5
    W = core.w
    N = 2 * SEQ
    PAIRS = BATCH // 2
    S2 = range(SLOTS)
    with ExitStack() as ctx:
        sb = lambda name, shape: ctx.enter_context(nc.sbuf_tensor(f"{tag}p_{name}", shape, F32))
        ps = lambda name, shape: ctx.enter_context(nc.psum_tensor(f"{tag}p_{name}_ps", shape, F32))
        padded = core.normed[:, 0:BATCH * PADSEQ].rearrange("p (b n) -> p b n", n=PADSEQ)
        xs = [sb(f"xs{s}", [P, 2, PADSEQ]) for s in S2]
        bqs = sb("bqs", [P, 1])
        q_ps = [ps(f"q{s}", [P, 512]) for s in S2]
        k_ps = [ps(f"k{s}", [P, 512]) for s in S2]
        v_ps = [ps(f"v{s}", [P, 2, 2, P]) for s in S2]
        bqs_made, conv_step, x_made, qk_made, v_made, q_sb, k_sb, v_sb = core.project_sems
        pair0 = PAIRS * core.projections
        one0 = core.projections
        core.projections += 1
        if conv:
            xc = sb("xc", [P, BATCH, SEQ])
            source = xc[:]
        else:
            source = padded

        with nc.Block() as block:
            @block.gpsimd
            def _(pool):
                for s in S2:
                    pool.memset(xs[s][:], 0.0).then_inc(x_made, 1)
                pool.wait_ge(x_made, pair0 + SLOTS * one0 + SLOTS)
                with pool.Fori(0, PAIRS // SLOTS) as i:
                    for s in S2:
                        n = pool.snap(SLOTS * i + s)
                        if conv and s == 0:
                            pool.wait_ge(conv_step, pool.snap(4 * i + 4))
                        pool.wait_ge(v_made, freed(n + pair0))
                        pool.tensor_copy(xs[s][:, :, 0:SEQ], source[:, ds(2 * n, 2), 0:SEQ]).then_inc(x_made, 1)

            @block.tensor
            def _(pe):
                with pe.Fori(0, PAIRS // SLOTS) as i:
                    for s in S2:
                        n = pe.snap(SLOTS * i + s)
                        pe.wait_ge(x_made, n + (pair0 + SLOTS * (one0 + 1) + 1))
                        pe.wait_ge(q_sb, freed(n + pair0))
                        pe.wait_ge(k_sb, freed(n + pair0))
                        x = xs[s][:, :, 0:SEQ]
                        two = lambda t: t[:, 0:N].rearrange("p (b n) -> p b n", n=SEQ)
                        pe.matmul(two(q_ps[s]), W[tag + "_wq"][:], x, start=True, stop=True)
                        pe.matmul(two(k_ps[s]), W[tag + "_wk"][:], x, start=True, stop=True).then_inc(qk_made, 1)
                        pe.wait_ge(v_sb, freed(n + pair0))
                        for c in range(2):
                            for f in range(2):
                                mm = pe.matmul(v_ps[s][0:HALF, c, f], xs[s][:, c, f * HALF:(f + 1) * HALF], W[tag + "_wv"][:],
                                               start=True, stop=True)
                        mm.then_inc(v_made, 1)

            @block.scalar
            def _(act):
                act.activation(bqs[:], W[tag + "_bq"][:], ACT.Copy, scale=SCALE).then_inc(bqs_made, 1)
                act.wait_ge(bqs_made, one0 + 1)
                with act.Fori(0, PAIRS // SLOTS) as i:
                    for s in S2:
                        n = act.snap(SLOTS * i + s)
                        act.wait_ge(qk_made, n + (pair0 + 1))
                        act.activation(q_all[:, ds(n * N, N)], q_ps[s][:, 0:N], ACT.Identity, bias=bqs[:, 0:1], scale=SCALE).then_inc(q_sb, 1)

            @block.vector
            def _(ve):
                if pair0 == 0:
                    for m in (q_sb, k_sb, v_sb, v_made):
                        ve.sem_inc(m, SLOTS)
                def convolve(i):
                    cw = W[tag + "_pos_w"]
                    first, batches = ve.snap(4 * i), ds(ve.snap(2 * SLOTS * i), 2 * SLOTS)
                    x = padded[:, batches, 0:SEQ]
                    ve.tensor_scalar(xc[:, batches, :], x, cw[:, 1:2], W[tag + "_pos_b"][:, 0:1], ALU.mult, ALU.add).then_inc(conv_step, 1)
                    ve.wait_ge(conv_step, first + 1)
                    ve.scalar_tensor_tensor(xc[:, batches, 1:SEQ], padded[:, batches, 0:SEQ - 1], cw[:, 0:1],
                                            xc[:, batches, 1:SEQ], ALU.mult, ALU.add).then_inc(conv_step, 1)
                    ve.wait_ge(conv_step, first + 2)
                    ve.scalar_tensor_tensor(xc[:, batches, 0:SEQ - 1], padded[:, batches, 1:SEQ], cw[:, 2:3],
                                            xc[:, batches, 0:SEQ - 1], ALU.mult, ALU.add).then_inc(conv_step, 1)
                    ve.wait_ge(conv_step, first + 3)
                    ve.tensor_tensor(xc[:, batches, :], xc[:, batches, :], x, ALU.add).then_inc(conv_step, 1)

                def leave_products(i):
                    for s in S2:
                        n = ve.snap(SLOTS * i + s)
                        ve.wait_ge(qk_made, n + (pair0 + 1))
                        ve.tensor_scalar(k_all[:, ds(n * N, N)], k_ps[s][:, 0:N], W[tag + "_bk"][:, 0:1], None, ALU.add).then_inc(k_sb, 1)
                        ve.wait_ge(v_made, made(n + pair0))
                        ve.tensor_copy(v_all[:, ds(n * 4 * P, 4 * P)], v_ps[s][0:HALF].rearrange("p c f e -> p (c f e)")).then_inc(v_sb, 1)

                if conv:
                    convolve(0)
                    convolve(1)
                    with ve.Fori(0, PAIRS // SLOTS - 2) as i:
                        leave_products(i)
                        convolve(ve.snap(i + 2))
                    for i in range(PAIRS // SLOTS - 2, PAIRS // SLOTS):
                        leave_products(i)
                else:
                    with ve.Fori(0, PAIRS // SLOTS) as i:
                        leave_products(i)


def narrow_attention(nc, core, tag, projected, top_k, conv):
    HEADS, HD, G, TILES, TOP = 8, 16, 3, 3, 8
    ROWS = G * TILES * P
    GROUP = TILES * P
    W = core.w
    S2 = range(SLOTS)
    PAIRS = BATCH // SLOTS
    with ExitStack() as ctx:
        sb = lambda name, shape: ctx.enter_context(nc.sbuf_tensor(f"{tag}_{name}", shape, F32))
        ps = lambda name, shape: ctx.enter_context(nc.psum_tensor(f"{tag}_{name}_ps", shape, F32))
        sem = lambda name: core.keep(nc.semaphore(f"{tag}_{name}"))
        q_all = sb("q_all", [P, TOK])
        k_all = sb("k_all", [P, TOK])
        v_all = sb("v_all", [HALF, BATCH * 2 * P])
        project_heads(nc, core, tag, conv, q_all, k_all, v_all)

        qbd = [sb(f"qbd{s}", [P, ROWS]) for s in S2]
        vs = [sb(f"vs{s}", [HALF, 2, HEADS, 32]) for s in S2]
        prob = [[sb(f"prob{s}{g}", [P, TILES, PADSEQ]) for g in range(G)] for s in S2]
        negmax = [sb(f"negmax{s}", [P, G, TILES]) for s in S2]
        rsum = [sb(f"rsum{s}", [P, G, TILES]) for s in S2]
        rinv = [sb(f"rinv{s}", [P, G, TILES]) for s in S2]
        pt = [sb(f"pt{s}", [HALF, 2, ROWS]) for s in S2]
        if projected:
            oc = [sb(f"oc{s}", [P, SEQ]) for s in S2]
        if top_k:
            top = [sb(f"top{s}", [P, TILES, TOP]) for s in S2]
            next_top = [sb(f"next_top{s}", [P, TILES, TOP]) for s in S2]
            left = [sb(f"left{s}", [P, TILES, SEQ]) for s in S2]
        o_ps = [ps(f"o{s}", [P, 512]) for s in S2]
        s_ps = [ps(f"s{s}", [P, 512]) for s in S2]
        pt_ps = [[ps(f"pt{s}{f}", [P, 512]) for f in range(2)] for s in S2]
        qbd_made, v_spread, o_made, h_made = (sem(n) for n in ("qbd_made", "v_spread", "o_made", "h_made"))
        if projected:
            oc_made, y_made = sem("oc_made"), sem("y_made")
        s_made, max_made, exp_made, rsum_made, prob_made, pt_made, pt0_sb, pt1_sb = (
            sem(n) for n in ("s_made", "max_made", "exp_made", "rsum_made", "prob_made", "pt_made", "pt0_sb", "pt1_sb"))
        set_up, ready = core.set_up, core.ready_after(10)
        if top_k:
            passed, found, kept = sem("passed"), sem("found"), sem("kept")
        scores = lambda s: s_ps[s][:, 0:TILES * SEQ].rearrange("p (t k) -> p t k", k=SEQ)

        def step(i, g, s):
            return SLOTS * G * i + (SLOTS * g + s)

        def pairs(eng, body):
            body(0, None)
            with eng.Fori(1, PAIRS) as i:
                body(i, eng.snap(i - 1))
            body(None, PAIRS - 1)

        with nc.Block() as block:
            @block.gpsimd
            def _(pool):
                for s in S2:
                    pool.memset(qbd[s][:], 0.0).then_inc(set_up, 1)
                    pool.memset(vs[s][:], 0.0).then_inc(set_up, 1)
                    for g in range(G):
                        pool.memset(prob[s][g][:], 0.0).then_inc(set_up, 1)
                pool.wait_ge(set_up, ready)
                with pool.Fori(0, PAIRS) as i:
                    for s in S2:
                        b = pool.snap(SLOTS * i + s)
                        pool.wait_ge(s_made, pool.snap(SLOTS * G * i + (s + 1)))
                        pool.tensor_tensor(qbd[s][:, 0:HEADS * SEQ].rearrange("p (h q) -> p h q", h=HEADS),
                                           q_all[:, ds(b * SEQ, SEQ)].unsqueeze(1).broadcast_to([P, HEADS, SEQ]),
                                           W["hmask16"][:].unsqueeze(2).broadcast_to([P, HEADS, SEQ]),
                                           ALU.mult).then_inc(qbd_made, 1)
                    for g in range(G):
                        for s in S2:
                            j = pool.snap(step(i, g, s))
                            pool.wait_ge(rsum_made, j + 1)
                            pr = prob[s][g]
                            pool.tensor_tensor(pr[:, :, 0:SEQ], pr[:, :, 0:SEQ],
                                               rinv[s][:, g].unsqueeze(2).broadcast_to([P, TILES, SEQ]),
                                               ALU.mult).then_inc(prob_made, 1)

            @block.tensor
            def _(pe):
                def score(i, g, s):
                    j = pe.snap(step(i, g, s))
                    b = pe.snap(SLOTS * i + s)
                    if g == 0:
                        pe.wait_ge(qbd_made, b + 1)
                    pe.wait_ge(exp_made, freed(j))
                    for t in range(TILES):
                        r0 = g * GROUP + t * P
                        mm = pe.matmul(scores(s)[:, t], qbd[s][:, r0:r0 + P], k_all[:, ds(b * SEQ, SEQ)], start=True, stop=True)
                    mm.then_inc(s_made, 1)

                def transposes(i, g, s):
                    j = pe.snap(step(i, g, s))
                    pe.wait_ge(prob_made, j + 1)
                    for f, emptied in ((0, pt0_sb), (1, pt1_sb)):
                        pe.wait_ge(emptied, freed(j))
                        for t in range(TILES):
                            mm = pe.transpose(pt_ps[s][f][0:HALF, t * P:(t + 1) * P],
                                              prob[s][g][:, t, f * HALF:(f + 1) * HALF], W["ident"][:])
                        mm.then_inc(pt_made, 1)

                def values(i, s):
                    j = pe.snap(step(i, G - 1, s))
                    b = pe.snap(SLOTS * i + s)
                    pe.wait_ge(v_spread, b + 1)
                    pe.wait_ge(h_made, freed(b))
                    pe.wait_ge(pt0_sb, made(j))
                    pe.wait_ge(pt1_sb, made(j))
                    for par in range(2):
                        for f in range(2):
                            for r in range(4):
                                h = 2 * r + par
                                mm = pe.matmul(o_ps[s][32 * r:32 * (r + 1), 0:SEQ], vs[s][:, f, h],
                                               pt[s][:, f, h * SEQ:(h + 1) * SEQ],
                                               start=(par == 0 and f == 0), stop=(par == 1 and f == 1))
                    mm.then_inc(o_made, 1)

                def body(i, before):
                    if i is not None:
                        for s in S2:
                            score(i, 0, s)
                    if before is not None:
                        for s in S2:
                            transposes(before, G - 1, s)
                    if i is not None:
                        for s in S2:
                            score(i, 1, s)
                    if before is not None:
                        for s in S2:
                            values(before, s)
                        if projected:
                            for s in S2:
                                b = pe.snap(SLOTS * before + s)
                                pe.wait_ge(oc_made, b + 1)
                                pe.matmul(o_ps[s][:, PADSEQ:PADSEQ + SEQ], W[tag + "_wo"][:], oc[s][:],
                                          start=True, stop=True).then_inc(y_made, 1)
                    if i is not None:
                        for s in S2:
                            transposes(i, 0, s)
                            score(i, 2, s)
                        for s in S2:
                            transposes(i, 1, s)

                pe.wait_ge(set_up, ready)
                pairs(pe, body)

            @block.scalar
            def _(act):
                def exponentials(i, g, s):
                    j = act.snap(step(i, g, s))
                    act.wait_ge(max_made, j + 1)
                    for t in range(TILES):
                        a = act.activation(prob[s][g][:, t, 0:SEQ], scores(s)[:, t], ACT.Exp, bias=negmax[s][:, g, t:t + 1],
                                           accum_out=None if top_k else rsum[s][:, g, t:t + 1])
                    a.then_inc(exp_made, 1)

                def leave_halves(i, g, s):
                    j = act.snap(step(i, g, s))
                    act.wait_ge(pt_made, 2 * j + 1)
                    act.activation(pt[s][:, 0, g * GROUP:(g + 1) * GROUP], pt_ps[s][0][0:HALF, 0:GROUP], ACT.Copy).then_inc(pt0_sb, 1)
                    if top_k:
                        act.wait_ge(pt_made, 2 * j + 2)
                        act.activation(pt[s][:, 1, g * GROUP:(g + 1) * GROUP], pt_ps[s][1][0:HALF, 0:GROUP], ACT.Copy).then_inc(pt1_sb, 1)

                def body(i, before):
                    if i is not None:
                        for s in S2:
                            exponentials(i, 0, s)
                    if before is not None:
                        for s in S2:
                            leave_halves(before, G - 1, s)
                    if before is not None and projected:
                        for s in S2:
                            b = act.snap(SLOTS * before + s)
                            act.wait_ge(o_made, b + 1)
                            act.activation(oc[s][:], o_ps[s][:, 0:SEQ], ACT.Identity, bias=W[tag + "_bv"][:, 0:1]).then_inc(oc_made, 1)
                    if i is not None:
                        for s in S2:
                            exponentials(i, 1, s)
                    if i is not None:
                        for s in S2:
                            leave_halves(i, 0, s)
                            exponentials(i, 2, s)
                        for s in S2:
                            leave_halves(i, 1, s)

                act.wait_ge(set_up, ready)
                pairs(act, body)

            @block.vector
            def _(ve):
                def row_maxima(i, g):
                    if not top_k:
                        for s in S2:
                            j = ve.snap(step(i, g, s))
                            ve.wait_ge(s_made, made(j))
                            ve.tensor_reduce(negmax[s][:, g], scores(s), AX.X, ALU.max, negate=True).then_inc(max_made, 1)
                        return
                    j0 = ve.snap(step(i, g, 0))
                    for s in S2:
                        ve.wait_ge(s_made, ve.snap(j0 + (s + 1 + SLOTS)))
                        ve.sem_inc(passed, 1)
                        for t in range(TILES):
                            op = ve.max(top[s][:, t], scores(s)[:, t])
                        op.then_inc(found, 1)
                    for s in S2:
                        ve.wait_ge(found, ve.snap(4 * j0 + (s + 1)))
                        ve.sem_inc(passed, 1)
                        for t in range(TILES):
                            op = ve.match_replace(left[s][:, t], top[s][:, t], scores(s)[:, t], GONE)
                        op.then_inc(found, 1)
                        ve.tensor_scalar(negmax[s][:, g], top[s][:, :, 0], -1.0, None, ALU.mult).then_inc(max_made, 1)
                    for s in S2:
                        ve.wait_ge(found, ve.snap(4 * j0 + (SLOTS + s + 1)))
                        ve.sem_inc(passed, 1)
                        for t in range(TILES):
                            op = ve.max(next_top[s][:, t], left[s][:, t])
                        op.then_inc(found, 1)
                    for s in S2:
                        ve.wait_ge(found, ve.snap(4 * j0 + (2 * SLOTS + s + 1)))
                        ve.sem_inc(passed, 1)
                        for t in range(TILES):
                            op = ve.match_replace(left[s][:, t], next_top[s][:, t], left[s][:, t], GONE)
                        op.then_inc(found, 1)

                def row_sum(i, g, s):
                    j = ve.snap(step(i, g, s))
                    ve.wait_ge(exp_made, made(j))
                    if top_k:
                        ve.wait_ge(found, ve.snap(4 * step(i, g, 0) + (3 * SLOTS + s + 1)))
                        pr = prob[s][g]
                        for t in range(TILES):
                            op = ve.scalar_tensor_tensor(pr[:, t, 0:SEQ], left[s][:, t], GONE, pr[:, t, 0:SEQ],
                                                         ALU.is_equal, ALU.mult, accum_out=rsum[s][:, g, t:t + 1])
                        op.then_inc(kept, 1)
                        ve.wait_ge(kept, j + 1)
                    ve.reciprocal(rinv[s][:, g], rsum[s][:, g]).then_inc(rsum_made, 1)

                def leave_half_1(i, g, s):
                    if top_k:
                        return
                    j = ve.snap(step(i, g, s))
                    ve.wait_ge(pt_made, 2 * j + 2)
                    ve.tensor_copy(pt[s][:, 1, g * GROUP:(g + 1) * GROUP], pt_ps[s][1][0:HALF, 0:GROUP]).then_inc(pt1_sb, 1)

                def spread_values(i, before, s):
                    b = ve.snap(SLOTS * i + s)
                    if before is not None:
                        ve.wait_ge(o_made, ve.snap(SLOTS * before + (s + 1)))
                    for par in range(2):
                        op = ve.tensor_copy(vs[s][:].rearrange("p f (r two) e -> p f r two e", two=2)[:, :, :, par, par * HD:(par + 1) * HD],
                                            v_all[:, ds(b * 2 * P, 2 * P)].rearrange("p (f r two d) -> p f r two d", f=2, two=2, d=HD)[:, :, :, par])
                    op.then_inc(v_spread, 1)

                def add(before, s):
                    b = ve.snap(SLOTS * before + s)
                    ve.wait_ge(y_made if projected else o_made, b + 1)
                    h_b = core.h[:, ds(b * SEQ, SEQ)]
                    ve.scalar_tensor_tensor(h_b, o_ps[s][:, PADSEQ:PADSEQ + SEQ] if projected else o_ps[s][:, 0:SEQ],
                                            W[tag + ("_bo" if projected else "_bv")][:, 0:1], h_b,
                                            ALU.add, ALU.add).then_inc(h_made, 1)

                def body(i, before):
                    if i is not None:
                        row_maxima(i, 0)
                        for s in S2:
                            row_sum(i, 0, s)
                    if before is not None:
                        for s in S2:
                            leave_half_1(before, G - 1, s)
                    if i is not None:
                        row_maxima(i, 1)
                        for s in S2:
                            row_sum(i, 1, s)
                        for s in S2:
                            spread_values(i, before, s)
                        for s in S2:
                            leave_half_1(i, 0, s)
                        row_maxima(i, 2)
                        for s in S2:
                            row_sum(i, 2, s)
                        for s in S2:
                            leave_half_1(i, 1, s)
                    if before is not None:
                        for s in S2:
                            add(before, s)

                for m in (h_made, exp_made, s_made, pt0_sb, pt1_sb):
                    ve.sem_inc(m, SLOTS)
                ve.wait_ge(set_up, ready)
                pairs(ve, body)


def routed_experts(nc, core, dram):
    EXPERTS, TOP_K, FF, ROUTED = 8, 2, 512, 1024
    FC = FF // P
    CHUNKS = ROUTED // CHUNK
    S2 = range(SLOTS)
    AHEAD = SLOTS + 1
    with ExitStack() as ctx:
        sb = lambda name, shape, dt=F32: ctx.enter_context(nc.sbuf_tensor(f"m_{name}", shape, dt))
        ps = lambda name, shape: ctx.enter_context(nc.psum_tensor(f"m_{name}_ps", shape, F32))
        sem = lambda name: core.keep(nc.semaphore(f"m_{name}"))
        ids_i = sb("ids_i", [P, TOP_K, ROUTED], I32)
        ids = sb("ids", [P, TOP_K, ROUTED])
        slot_w = sb("slot_w", [P, TOP_K, ROUTED])
        picked = sb("picked", [P, TOP_K, ROUTED])
        share = sb("share", [P, EXPERTS, ROUTED])
        w1 = [sb(f"w1{s}", [P, FF]) for s in S2]
        w2 = [sb(f"w2{s}", [P, FC, P]) for s in S2]
        hid = [sb(f"hid{s}", [P, FC, CHUNK]) for s in S2]
        part = [sb(f"part{s}", [P, CHUNK]) for s in S2]
        up_ps = [ps(f"up{f}", [P, CHUNK]) for f in range(FC)]
        down_ps = [ps(f"down{s}", [P, CHUNK]) for s in S2]
        ids_in, ids_made, share_step = (sem(n) for n in ("ids_in", "ids_made", "share_step"))
        w_in = [sem(f"w_in{s}") for s in S2]
        up_made, gelu_made, down_made, part_made, h_made = (
            sem(n) for n in ("up_made", "gelu_made", "down_made", "part_made", "h_made"))

        with nc.Block() as block:
            @block.sync
            def _(sp):
                sp.dma_start(ids_i[:], dram["expert_ids"].partition_broadcast(P)).then_inc(ids_in, 16)
                sp.dma_start(slot_w[:], dram["expert_rows"].partition_broadcast(P)).then_inc(ids_in, 16)
                with sp.Fori(0, EXPERTS // SLOTS) as i:
                    for s in S2:
                        e = sp.snap(SLOTS * i + s)
                        sp.wait_ge(down_made, CHUNKS * e + (AHEAD - 2))
                        sp.dma_start(w1[s][:], dram["m_w1"][ds(e, 1)].rearrange("e p f -> p (e f)")).then_inc(w_in[s], 16)
                        sp.dma_start(w2[s][:], dram["m_w2"][ds(e, 1)].rearrange("e p c o -> p (e c) o")).then_inc(w_in[s], 16)

            @block.tensor
            def _(pe):
                def up(i, s, c):
                    t = pe.snap(SLOTS * CHUNKS * i + (CHUNKS * s + c))
                    if c == 0:
                        pe.wait_ge(w_in[s], 32 * i + 32)
                    for f in range(FC):
                        pe.wait_ge(gelu_made, FC * t + (f + 1))
                        pe.matmul(up_ps[f][:], w1[s][:, f * P:(f + 1) * P], core.normed[:, c * CHUNK:(c + 1) * CHUNK],
                                  start=True, stop=True).then_inc(up_made, 1)

                def down(i, s, c):
                    t = pe.snap(SLOTS * CHUNKS * i + (CHUNKS * s + c))
                    pe.wait_ge(gelu_made, FC * t + 2 * FC)
                    pe.wait_ge(part_made, freed(t))
                    for f in range(FC):
                        mm = pe.matmul(down_ps[c][:], w2[s][:, f], hid[c][:, f], start=(f == 0), stop=(f == FC - 1))
                    mm.then_inc(down_made, 1)

                steps = [(s, c) for s in S2 for c in range(CHUNKS)]
                def body(i, before):
                    up(i, *steps[0])
                    if before is not None:
                        down(before, *steps[-1])
                    for n in range(1, len(steps)):
                        up(i, *steps[n])
                        down(i, *steps[n - 1])

                body(0, None)
                with pe.Fori(1, EXPERTS // SLOTS) as i:
                    body(i, pe.snap(i - 1))
                down(EXPERTS // SLOTS - 1, *steps[-1])

            @block.scalar
            def _(act):
                with act.Fori(0, EXPERTS // SLOTS) as i:
                    for n in range(SLOTS * CHUNKS):
                        t = act.snap(SLOTS * CHUNKS * i + n)
                        act.wait_ge(down_made, made(t, AHEAD) - SLOTS)
                        for f in range(FC):
                            act.wait_ge(up_made, FC * t + (f + 1))
                            act.activation(hid[n % CHUNKS][:, f], up_ps[f][:], ACT.Gelu).then_inc(gelu_made, 1)

            @block.vector
            def _(ve):
                ve.sem_inc(gelu_made, FC)
                ve.sem_inc(down_made, AHEAD)
                ve.sem_inc(part_made, SLOTS)
                ve.sem_inc(h_made, SLOTS)
                ve.wait_ge(ids_in, 32)
                ve.tensor_copy(ids[:], ids_i[:]).then_inc(ids_made, 1)
                ve.wait_ge(ids_made, 1)
                for e in range(EXPERTS):
                    if e:
                        ve.wait_ge(share_step, 2 * e)
                    ve.scalar_tensor_tensor(picked[:], ids[:], float(e), slot_w[:], ALU.is_equal, ALU.mult).then_inc(share_step, 1)
                    ve.wait_ge(share_step, 2 * e + 1)
                    ve.tensor_tensor(share[:, e], picked[:, 0], picked[:, 1], ALU.add).then_inc(share_step, 1)
                ve.wait_ge(share_step, 2 * EXPERTS)
                with ve.Fori(0, EXPERTS // SLOTS) as i:
                    for s in S2:
                        for c in range(CHUNKS):
                            t = ve.snap(SLOTS * CHUNKS * i + (CHUNKS * s + c))
                            ve.wait_ge(down_made, made(t, AHEAD))
                            ve.wait_ge(h_made, freed(t))
                            ve.tensor_tensor(part[c][:], down_ps[c][:],
                                             share[:, ds(SLOTS * i + s, 1), c * CHUNK:(c + 1) * CHUNK].rearrange("p e n -> p (e n)"),
                                             ALU.mult).then_inc(part_made, 1)
                            ve.wait_ge(part_made, made(t))
                            h_c = core.h[:, c * CHUNK:(c + 1) * CHUNK]
                            ve.tensor_tensor(h_c, h_c, part[c][:], ALU.add).then_inc(h_made, 1)


def head_mixing(nc, core):
    HEADS, HD = 8, 16
    SCALE = float(HD) ** -0.5
    TILES = TOKPAD // P
    W = core.w
    SLOTS = 4
    S2 = range(SLOTS)
    with ExitStack() as ctx:
        sb = lambda name, shape: ctx.enter_context(nc.sbuf_tensor(f"a1_{name}", shape, F32))
        ps = lambda name, shape: ctx.enter_context(nc.psum_tensor(f"a1_{name}_ps", shape, F32))
        sem = lambda name: core.keep(nc.semaphore(f"a1_{name}"))
        xs = [sb(f"xs{s}", [P, P]) for s in S2]
        qkv = [sb(f"qkv{s}", [P, 3, P]) for s in S2]
        prod = [sb(f"prod{s}", [P, HEADS, HEADS, HD]) for s in S2]
        prod2 = [sb(f"prod2{s}", [P, HEADS, HD, HEADS]) for s in S2]
        score = [sb(f"score{s}", [P, HEADS, HEADS]) for s in S2]
        shifted = [sb(f"shifted{s}", [P, HEADS, HEADS]) for s in S2]
        weight = [sb(f"weight{s}", [P, HEADS, HEADS]) for s in S2]
        top = [sb(f"top{s}", [P, HEADS]) for s in S2]
        total = [sb(f"total{s}", [P, HEADS]) for s in S2]
        inv = [sb(f"inv{s}", [P, HEADS]) for s in S2]
        mixed = [sb(f"mixed{s}", [P, HEADS, HD]) for s in S2]
        scaled = [sb(f"scaled{s}", [P, P]) for s in S2]
        qkv_ps = [ps(f"qkv{s}", [P, 512]) for s in S2]
        turn_ps = [ps(f"turn{s}", [P, 512]) for s in S2]
        names = ["x_made", "qkv_made", "qkv_sb", "prod_made", "score_made", "top_made", "shifted_made", "weight_made",
                 "total_made", "inv_made", "prod2_made", "mixed_made", "scaled_made", "turn_made", "turned_made"]
        (x_made, qkv_made, qkv_sb, prod_made, score_made, top_made, shifted_made, weight_made, total_made, inv_made,
         prod2_made, mixed_made, scaled_made, turn_made, turned_made) = (sem(n) for n in names)

        def groups(eng, body):
            body(0, None)
            with eng.Fori(1, TILES // SLOTS) as i:
                body(i, eng.snap(i - 1))
            body(None, TILES // SLOTS - 1)

        with nc.Block() as block:
            @block.gpsimd
            def _(pool):
                def fetch(i, s):
                    t = pool.snap(SLOTS * i + s)
                    pool.wait_ge(qkv_made, freed(t))
                    pool.tensor_copy(xs[s][:], core.normed[:, ds(t * P, P)]).then_inc(x_made, 1)

                def products(i, s):
                    t = pool.snap(SLOTS * i + s)
                    pool.wait_ge(qkv_sb, made(t, SLOTS))
                    pool.wait_ge(score_made, freed(t))
                    q = qkv[s][:, 0].rearrange("p (h d) -> p h d", d=HD)
                    k = qkv[s][:, 1].rearrange("p (g d) -> p g d", d=HD)
                    pool.tensor_tensor(prod[s][:], q.unsqueeze(2).broadcast_to([P, HEADS, HEADS, HD]),
                                       k.unsqueeze(1).broadcast_to([P, HEADS, HEADS, HD]), ALU.mult).then_inc(prod_made, 1)

                def body(i, before):
                    for s in S2:
                        if i is not None:
                            fetch(i, s)
                    for s in S2:
                        if before is not None:
                            t = pool.snap(SLOTS * before + s)
                            pool.wait_ge(mixed_made, t + 1)
                            pool.wait_ge(inv_made, t + 1)
                            pool.wait_ge(turn_made, freed(t))
                            pool.tensor_tensor(scaled[s][:].rearrange("p (h d) -> p h d", d=HD), mixed[s][:],
                                               inv[s][:].unsqueeze(2).broadcast_to([P, HEADS, HD]), ALU.mult).then_inc(scaled_made, 1)
                        if i is not None:
                            products(i, s)

                groups(pool, body)

            @block.tensor
            def _(pe):
                def body(i, before):
                    for s in S2:
                        if i is not None:
                            t = pe.snap(SLOTS * i + s)
                            pe.wait_ge(x_made, t + 1)
                            pe.wait_ge(qkv_sb, freed(t))
                            pe.matmul(qkv_ps[s][:, 0:3 * P], xs[s][:], W["a1_wqkv"][:], start=True, stop=True).then_inc(qkv_made, 1)
                    for s in S2:
                        if before is not None:
                            t = pe.snap(SLOTS * before + s)
                            pe.wait_ge(scaled_made, made(t, SLOTS))
                            pe.wait_ge(turned_made, freed(t))
                            pe.transpose(turn_ps[s][:, 0:P], scaled[s][:], W["ident"][:]).then_inc(turn_made, 1)

                groups(pe, body)

            @block.scalar
            def _(act):
                def body(i, before):
                    for s in S2:
                        if i is not None:
                            t = act.snap(SLOTS * i + s)
                            act.wait_ge(qkv_made, made(t, SLOTS))
                            act.wait_ge(prod2_made, freed(t))
                            act.activation(qkv[s][:], qkv_ps[s][:, 0:3 * P].rearrange("p (c e) -> p c e", e=P), ACT.Copy).then_inc(qkv_sb, 1)
                    for s in S2:
                        if before is not None:
                            t = act.snap(SLOTS * before + s)
                            act.wait_ge(turn_made, made(t, SLOTS))
                            act.activation(core.normed[:, ds(t * P, P)], turn_ps[s][:, 0:P], ACT.Copy).then_inc(turned_made, 1)
                    for s in S2:
                        if i is not None:
                            t = act.snap(SLOTS * i + s)
                            act.wait_ge(shifted_made, t + 1)
                            act.activation(weight[s][:], shifted[s][:], ACT.Exp, scale=SCALE).then_inc(weight_made, 1)

                groups(act, body)

            @block.vector
            def _(ve):
                for m in (turned_made, qkv_made, qkv_sb, score_made, prod2_made, scaled_made, turn_made):
                    ve.sem_inc(m, SLOTS)
                with ve.Fori(0, TILES // SLOTS) as i:
                    for s in S2:
                        t = ve.snap(SLOTS * i + s)
                        ve.wait_ge(prod_made, t + 1)
                        ve.tensor_reduce(score[s][:], prod[s][:], AX.X, ALU.add).then_inc(score_made, 1)
                        ve.wait_ge(score_made, made(t, SLOTS))
                        ve.tensor_reduce(top[s][:], score[s][:], AX.X, ALU.max).then_inc(top_made, 1)
                        ve.wait_ge(top_made, t + 1)
                        ve.tensor_tensor(shifted[s][:], score[s][:], top[s][:].unsqueeze(2).broadcast_to([P, HEADS, HEADS]),
                                         ALU.subtract).then_inc(shifted_made, 1)
                    for s in S2:
                        t = ve.snap(SLOTS * i + s)
                        ve.wait_ge(weight_made, t + 1)
                        v = qkv[s][:, 2].rearrange("p (g d) -> p d g", d=HD)
                        ve.tensor_tensor(prod2[s][:], weight[s][:].unsqueeze(2).broadcast_to([P, HEADS, HD, HEADS]),
                                         v.unsqueeze(1).broadcast_to([P, HEADS, HD, HEADS]), ALU.mult).then_inc(prod2_made, 1)
                        ve.tensor_reduce(total[s][:], weight[s][:], AX.X, ALU.add).then_inc(total_made, 1)
                        ve.wait_ge(prod2_made, made(t, SLOTS))
                        ve.wait_ge(scaled_made, freed(t))
                        ve.tensor_reduce(mixed[s][:], prod2[s][:], AX.X, ALU.add).then_inc(mixed_made, 1)
                        ve.wait_ge(total_made, t + 1)
                        ve.reciprocal(inv[s][:], total[s][:]).then_inc(inv_made, 1)


def window_projection(nc, core):
    HEADS, HD, WINDOW = 8, 16, 64
    SHIFT = WINDOW // 2
    WINDOWS = -(-SEQ // WINDOW)
    HALF_BATCHES = BATCH // 2
    W = core.w
    S2 = range(SLOTS)
    kept = lambda w, h: max(0, min(HEADS, SEQ - (WINDOW * w + HEADS * h)))
    with ExitStack() as ctx:
        sb = lambda name, shape: ctx.enter_context(nc.sbuf_tensor(f"wp_{name}", shape, F32))
        ps = lambda name, shape: ctx.enter_context(nc.psum_tensor(f"wp_{name}_ps", shape, F32))
        sem = lambda name: core.keep(nc.semaphore(f"wp_{name}"))
        rolled = sb("rolled", [P, BATCH, WINDOWS * WINDOW])
        w_head = [sb(f"w_head{s}", [P, HEADS, P]) for s in S2]
        y_ps = [[ps(f"y{s}{q}", [P, 512]) for q in range(2)] for s in S2]
        padded_made, rolled_made, w_made, y_made, h_made = (
            sem(n) for n in ("padded_made", "rolled_made", "w_made", "y_made", "h_made"))
        flat = core.normed[:, 0:TOK].rearrange("p (b n) -> p b n", n=SEQ)
        res = core.h[:, 0:TOK].rearrange("p (b n) -> p b n", n=SEQ)
        with nc.Block() as block:
            @block.gpsimd
            def _(pool):
                pool.memset(rolled[:, :, SEQ:], 0.0).then_inc(padded_made, 1)
                pool.tensor_copy(rolled[:, :, SEQ - SHIFT:SEQ], flat[:, :, 0:SHIFT]).then_inc(padded_made, 1)

            @block.scalar
            def _(act):
                act.activation(rolled[:, :, 0:SEQ - SHIFT], flat[:, :, SHIFT:SEQ], ACT.Copy).then_inc(rolled_made, 1)

            @block.tensor
            def _(pe):
                pe.wait_ge(padded_made, 2)
                pe.wait_ge(rolled_made, 1)
                tok = rolled[:].rearrange("p b (w a e) -> p b w a e", a=HEADS, e=HEADS)
                for h in range(HEADS):
                    s = h % SLOTS
                    wins = sum(kept(w, h) > 0 for w in range(WINDOWS))
                    pe.wait_ge(w_made, h + 1)
                    if h >= SLOTS:
                        pe.wait_ge(h_made, h - 1)
                    for q in range(2):
                        y = y_ps[s][q][:, 0:HALF_BATCHES * wins * HEADS].rearrange("p (b w a) -> p b w a", w=wins, a=HEADS)
                        for e in range(HEADS):
                            mm = pe.matmul(y, w_head[s][:, e], tok[:, q * HALF_BATCHES:(q + 1) * HALF_BATCHES, 0:wins, :, e],
                                           start=(e == 0), stop=(e == HEADS - 1))
                    mm.then_inc(y_made, 1)

            @block.vector
            def _(ve):
                def head_weights(h):
                    if h >= SLOTS:
                        ve.wait_ge(y_made, h - 1)
                    ve.tensor_scalar(w_head[h % SLOTS][:], W["wp_w"][:], W["hmask16"][:, h:h + 1], None, ALU.mult).then_inc(w_made, 1)

                head_weights(0)
                for h in range(HEADS):
                    s = h % SLOTS
                    wins = sum(kept(w, h) > 0 for w in range(WINDOWS))
                    if h + 1 < HEADS:
                        head_weights(h + 1)
                    ve.wait_ge(y_made, h + 1)
                    for q in range(2):
                        bs = slice(q * HALF_BATCHES, (q + 1) * HALF_BATCHES)
                        y = y_ps[s][q][:, 0:HALF_BATCHES * wins * HEADS].rearrange("p (b w a) -> p b w a", w=wins, a=HEADS)
                        for w in range(wins):
                            first = (WINDOW * w + HEADS * h + SHIFT) % SEQ
                            n = kept(w, h)
                            cut = min(n, SEQ - first)
                            for a0, a1, at in ((0, cut, first), (cut, n, 0)):
                                if a1 > a0:
                                    r = res[:, bs, at:at + a1 - a0]
                                    op = ve.scalar_tensor_tensor(r, y[:, :, w, a0:a1], W["wp_b"][:, 0:1], r, ALU.add, ALU.add)
                    op.then_inc(h_made, 1)


def trig_ffn(nc, core):
    NF, QUAD, LUT = 64, 4, 1024
    R = NF // QUAD
    W = core.w
    STEP = 2.0 * math.pi / LUT
    CHUNKS = TOKPAD // CHUNK
    WIDE = QUAD * CHUNK
    S2 = range(SLOTS)
    with ExitStack() as ctx:
        sb = lambda name, shape, dt=F32: ctx.enter_context(nc.sbuf_tensor(f"f1_{name}", shape, dt))
        ps = lambda name, shape: ctx.enter_context(nc.psum_tensor(f"f1_{name}_ps", shape, F32))
        sem = lambda name: core.keep(nc.semaphore(f"f1_{name}"))
        scale = sb("scale", [P, NF])
        shift = sb("shift", [P, NF])
        absw = sb("absw", [P, NF])
        cols = sb("cols", [P, NF, 2, 32])
        minus_pi = sb("minus_pi", [P, 1])
        angle = [sb(f"angle{s}", [P, QUAD, CHUNK], I32) for s in S2]
        sin_at = [sb(f"sin_at{s}", [P, QUAD, CHUNK], I16) for s in S2]
        cos_at = [sb(f"cos_at{s}", [P, QUAD, CHUNK], I16) for s in S2]
        cos_raw = [sb(f"cos_raw{s}", [P, QUAD, CHUNK], I16) for s in S2]
        sin_v = [sb(f"sin_v{s}", [P, QUAD, CHUNK]) for s in S2]
        cos_v = [sb(f"cos_v{s}", [P, QUAD, CHUNK]) for s in S2]
        x_fixed = sb("x_fixed", [P, CHUNK])
        sums = sb("sums", [P, CHUNK])
        e = sb("e", [P, CHUNK])
        sum_ps = ps("sum", [P, CHUNK])
        y_ps = ps("y", [P, CHUNK])
        set_up, x_fixed_made, angle_made, last_angle_made, sin_at_made, cos_raw_made, cos_at_made, sin_made, cos_made, used = (
            sem(n) for n in ("set_up", "x_fixed_made", "angle_made", "last_angle_made", "sin_at_made", "cos_raw_made", "cos_at_made", "sin_made", "cos_made", "used"))
        sums_sb, y_made, e_made = (sem(n) for n in ("sums_sb", "y_made", "e_made"))

        with nc.Block() as block:
            @block.tensor
            def _(pe):
                def product(before):
                    pe.wait_ge(sums_sb, before + 1)
                    pe.matmul(y_ps[:], W["f1_proj"][:], sums[:], start=True, stop=True).then_inc(y_made, 1)

                def quads(c, before):
                    for r in range(R):
                        s = r % SLOTS
                        q = pe.snap(R * c + r)
                        for cs, value_made, values in ((1, sin_made, sin_v), (0, cos_made, cos_v)):
                            pe.wait_ge(value_made, made(q))
                            if r == 0 and cs == 1 and before is not None:
                                pe.wait_ge(sums_sb, before + 1)
                            for j in range(QUAD):
                                mm = pe.matmul(sum_ps[32 * j:32 * (j + 1), :], cols[:, QUAD * r + j, cs], values[s][:, j],
                                               start=(r == 0 and cs == 1), stop=(r == R - 1 and cs == 0))
                        mm.then_inc(used, 1)
                        if r == 1 and before is not None:
                            product(before)

                pe.wait_ge(set_up, 9)
                quads(0, None)
                with pe.Fori(1, CHUNKS) as c:
                    quads(c, pe.snap(c - 1))
                product(CHUNKS - 1)

            @block.scalar
            def _(act):
                def leave_sums(before):
                    act.wait_ge(used, made(R * before + (R - 1)))
                    act.activation(sums[:], sum_ps[:], ACT.Copy).then_inc(sums_sb, 1)

                def sines(c, r):
                    s = r % SLOTS
                    q = act.snap(R * c + r)
                    act.wait_ge(used, freed(q))
                    act.wait_ge(sin_at_made, q + 1)
                    act.activation(sin_v[s][:], sin_at[s][:], ACT.Sin, bias=minus_pi[:, 0:1], scale=STEP).then_inc(sin_made, 1)
                    act.wait_ge(cos_at_made, q + 1)
                    act.activation(cos_v[s][:], cos_at[s][:], ACT.Sin, bias=minus_pi[:, 0:1], scale=STEP).then_inc(cos_made, 1)

                def silu(before):
                    act.wait_ge(y_made, before + 1)
                    act.activation(e[:], y_ps[:], ACT.Silu, scale=-1.0).then_inc(e_made, 1)

                act.wait_ge(set_up, 9)
                for r in range(R):
                    sines(0, r)
                with act.Fori(1, CHUNKS) as c:
                    before = act.snap(c - 1)
                    for r in range(R):
                        sines(c, r)
                        if r == 0:
                            leave_sums(before)
                        if r == 5:
                            silu(before)
                leave_sums(CHUNKS - 1)
                silu(CHUNKS - 1)

            @block.gpsimd
            def _(pool):
                pool.wait_ge(set_up, 9)
                with pool.Fori(0, CHUNKS) as c:
                    pool.wait_ge(last_angle_made, pool.snap(R * c + 1))
                    pool.tensor_copy(x_fixed[:], core.normed[:, ds(c * CHUNK, CHUNK)]).then_inc(x_fixed_made, 1)
                    pool.wait_ge(x_fixed_made, pool.snap((R + 1) * c + 1))
                    for r in range(R):
                        n = QUAD * r + QUAD - 1
                        q = pool.snap(R * c + r)
                        pool.wait_ge(cos_raw_made, freed(q))
                        pool.sem_inc(x_fixed_made, 1)
                        pool.tensor_scalar(angle[r % SLOTS][:, QUAD - 1], x_fixed[:],
                                           scale[:, n:n + 1], shift[:, n:n + 1], ALU.mult, ALU.add).then_inc(last_angle_made, 1)

            @block.vector
            def _(ve):
                ve.scalar_tensor_tensor(absw[:], W["f1_w"][:], -1.0, W["f1_w"][:], ALU.mult, ALU.max).then_inc(set_up, 1)
                ve.wait_ge(set_up, 1)
                ve.tensor_scalar(absw[:], absw[:], 1.0, STEP, ALU.add, ALU.mult).then_inc(set_up, 1)
                ve.wait_ge(set_up, 2)
                ve.reciprocal(scale[:], absw[:]).then_inc(set_up, 1)
                ve.tensor_scalar(shift[:], W["f1_b"][:], 1.0 / STEP, None, ALU.mult).then_inc(set_up, 1)
                ve.memset(cols[:], 0.0).then_inc(set_up, 1)
                ve.memset(minus_pi[:], -math.pi).then_inc(set_up, 1)
                ve.wait_ge(set_up, 6)
                for r in range(R):
                    for cs, name in ((0, "f1_attn_cos"), (1, "f1_attn_sin")):
                        op = ve.tensor_copy(cols[:, QUAD * r:QUAD * (r + 1), cs, R * cs + r],
                                            W[name][:, QUAD * r:QUAD * (r + 1)])
                op.then_inc(set_up, 1)
                ve.sem_inc(last_angle_made, 1)
                for m in (used, sin_made, cos_made, cos_raw_made):
                    ve.sem_inc(m, SLOTS)
                ve.wait_ge(set_up, 7)
                ve.sem_inc(set_up, 2)

                def indices(c, r):
                    x = core.normed[:, ds(c * CHUNK, CHUNK)]
                    s = r % SLOTS
                    q = ve.snap(R * c + r)
                    ve.wait_ge(sin_made, freed(q))
                    for j in range(QUAD - 1):
                        n = QUAD * r + j
                        op = ve.tensor_scalar(angle[s][:, j], x, scale[:, n:n + 1], shift[:, n:n + 1], ALU.mult, ALU.add)
                    op.then_inc(angle_made, 1)
                    ve.wait_ge(angle_made, q + 1)
                    ve.wait_ge(last_angle_made, q + 2)
                    low = angle[s][:].bitcast(I16).rearrange("p j (t w) -> p j t w", w=2)[:, :, :, 0]
                    ve.tensor_scalar(sin_at[s][:], low, LUT - 1, None, ALU.bitwise_and).then_inc(sin_at_made, 1)
                    ve.wait_ge(sin_at_made, q + 1)
                    ve.tensor_scalar(cos_raw[s][:], sin_at[s][:], float(LUT // 4), None, ALU.add).then_inc(cos_raw_made, 1)
                    ve.wait_ge(cos_raw_made, made(q))
                    ve.wait_ge(cos_made, freed(q))
                    ve.tensor_scalar(cos_at[s][:], cos_raw[s][:], LUT - 1, None, ALU.bitwise_and).then_inc(cos_at_made, 1)

                def add(before):
                    ve.wait_ge(e_made, before + 1)
                    h_c = core.h[:, ds(before * CHUNK, CHUNK)]
                    ve.tensor_tensor(h_c, h_c, e[:], ALU.add)

                for r in range(R):
                    indices(0, r)
                with ve.Fori(1, CHUNKS) as c:
                    before = ve.snap(c - 1)
                    for r in range(R):
                        indices(c, r)
                        if r == 7:
                            add(before)
                add(CHUNKS - 1)


def unit_heads(nc, core, qk_all, v_all, v_w):
    W = core.w
    N = 2 * SEQ
    UNITS = BATCH // 4
    S2 = range(SLOTS)
    with ExitStack() as ctx:
        sb = lambda name, shape: ctx.enter_context(nc.sbuf_tensor(f"a2p_{name}", shape, F32))
        ps = lambda name, shape: ctx.enter_context(nc.psum_tensor(f"a2p_{name}_ps", shape, F32))
        sem = lambda name: core.keep(nc.semaphore(f"a2p_{name}"))
        padded = core.normed[:, 0:BATCH * PADSEQ].rearrange("p (b n) -> p b n", n=PADSEQ)
        ones = sb("ones", [P, 32])
        xs = [sb(f"xs{s}", [P, 2, PADSEQ]) for s in S2]
        sq = [sb(f"sq{s}", [P, 2, N]) for s in S2]
        inv = sb("inv", [P, N])
        raw_ps = [[ps(f"raw{s}{m}", [P, 512]) for m in range(2)] for s in S2]
        n_ps = ps("n", [P, 512])
        v_ps = ps("v", [P, 2, 2, P])
        inv_ps = [ps(f"inv{m}", [P, 512]) for m in range(2)]
        x_made, raw_made, q_sb, k_sb, sq_made, v_made, v_sb, spread_made, unit_made = (
            sem(n) for n in ("x_made", "raw_made", "q_sb", "k_sb", "sq_made", "v_made", "v_sb", "spread_made", "unit_made"))
        n_made, root_made, floored, inv_made = (sem(n) for n in ("n_made", "root_made", "floored", "inv_made"))

        def units(eng, body):
            body(0, None)
            with eng.Fori(1, UNITS) as u:
                body(u, eng.snap(u - 1))
            body(None, UNITS - 1)

        with nc.Block() as block:
            @block.gpsimd
            def _(pool):
                for s in S2:
                    pool.memset(xs[s][:], 0.0).then_inc(x_made, 1)
                pool.wait_ge(x_made, SLOTS)
                with pool.Fori(0, UNITS) as u:
                    for s in S2:
                        n = pool.snap(SLOTS * u + s)
                        pool.wait_ge(v_made, freed(n))
                        pool.tensor_copy(xs[s][:, :, 0:SEQ], padded[:, ds(2 * n, 2), 0:SEQ]).then_inc(x_made, 1)
                    for s in S2:
                        n = pool.snap(SLOTS * u + s)
                        pool.wait_ge(q_sb, made(n))
                        pool.wait_ge(k_sb, made(n))
                        pool.wait_ge(n_made, pool.snap(u + 1))
                        for m in range(2):
                            x = qk_all[:, m, ds(n * N, N)]
                            op = pool.tensor_tensor(sq[s][:, m], x, x, ALU.mult)
                        op.then_inc(sq_made, 1)

            @block.tensor
            def _(pe):
                def project(u):
                    for s in S2:
                        n = pe.snap(SLOTS * u + s)
                        pe.wait_ge(x_made, made(n))
                        pe.wait_ge(q_sb, freed(n))
                        pe.wait_ge(k_sb, freed(n))
                        for m, w in enumerate(("a2_wq", "a2_wk")):
                            mm = pe.matmul(raw_ps[s][m][:, 0:N].rearrange("p (b n) -> p b n", n=SEQ), W[w][:],
                                           xs[s][:, :, 0:SEQ], start=True, stop=True)
                        mm.then_inc(raw_made, 1)
                        pe.wait_ge(v_sb, n + 1)
                        for c in range(2):
                            for f in range(2):
                                mm = pe.matmul(v_ps[0:HALF, c, f], xs[s][:, c, f * HALF:(f + 1) * HALF], v_w[:], start=True, stop=True)
                        mm.then_inc(v_made, 1)

                def spread(before):
                    pe.wait_ge(inv_made, before + 1)
                    for s in S2:
                        n = pe.snap(SLOTS * before + s)
                        pe.wait_ge(unit_made, n + 1)
                        for m in range(2):
                            k = 2 * s + m
                            rows = slice(32 * k, 32 * (k + 1))
                            mm = pe.matmul(inv_ps[m][:, 0:N], core.first_row[rows, :], inv[rows, :], start=True, stop=True)
                        mm.then_inc(spread_made, 1)

                def lengths(u):
                    pe.wait_ge(sq_made, pe.snap(SLOTS * u + SLOTS))
                    pe.wait_ge(root_made, pe.snap(u + 1))
                    for s in S2:
                        for m in range(2):
                            k = 2 * s + m
                            mm = pe.matmul(n_ps[32 * k:32 * (k + 1), 0:N], ones[:], sq[s][:, m], start=True, stop=True)
                    mm.then_inc(n_made, 1)

                def body(u, before):
                    if u is not None:
                        project(u)
                    if before is not None:
                        spread(before)
                    if u is not None:
                        lengths(u)

                pe.wait_ge(x_made, SLOTS)
                units(pe, body)

            @block.scalar
            def _(act):
                with act.Fori(0, UNITS) as u:
                    for s in S2:
                        n = act.snap(SLOTS * u + s)
                        act.wait_ge(raw_made, n + 1)
                        act.activation(qk_all[:, 0, ds(n * N, N)], raw_ps[s][0][:, 0:N], ACT.Copy).then_inc(q_sb, 1)
                    act.wait_ge(n_made, act.snap(u + 2))
                    act.wait_ge(spread_made, act.snap(SLOTS * u + 1))
                    act.activation(inv[:], n_ps[:, 0:N], ACT.Sqrt).then_inc(root_made, 1)

            @block.vector
            def _(ve):
                def body(u, before):
                    if u is not None:
                        for s in S2:
                            n = ve.snap(SLOTS * u + s)
                            ve.wait_ge(raw_made, n + 1)
                            ve.tensor_copy(qk_all[:, 1, ds(n * N, N)], raw_ps[s][1][:, 0:N]).then_inc(k_sb, 1)
                            ve.wait_ge(v_made, made(n))
                            ve.tensor_copy(v_all[:, ds(n * 4 * P, 4 * P)], v_ps[0:HALF].rearrange("p c f e -> p (c f e)")).then_inc(v_sb, 1)
                    if before is not None:
                        for s in S2:
                            n = ve.snap(SLOTS * before + s)
                            ve.wait_ge(spread_made, n + 2)
                            for m in range(2):
                                x = qk_all[:, m, ds(n * N, N)]
                                op = ve.tensor_tensor(x, x, inv_ps[m][:, 0:N], ALU.mult)
                            op.then_inc(unit_made, 1)
                    if u is not None:
                        ve.wait_ge(root_made, ve.snap(u + 2))
                        ve.tensor_scalar(inv[:], inv[:], 1e-12, None, ALU.max).then_inc(floored, 1)
                        ve.wait_ge(floored, ve.snap(u + 1))
                        ve.reciprocal(inv[:], inv[:]).then_inc(inv_made, 1)

                ve.memset(ones[:], 1.0)
                for c in (q_sb, k_sb, v_made):
                    ve.sem_inc(c, SLOTS)
                for c in (v_sb, unit_made, n_made, root_made, spread_made):
                    ve.sem_inc(c, 1)
                units(ve, body)


def decay_retrieval(nc, core):
    HEADS, HD = 4, 32
    PAIRS = BATCH // SLOTS
    W = core.w
    S2 = range(SLOTS)
    with ExitStack() as ctx:
        sb = lambda name, shape: ctx.enter_context(nc.sbuf_tensor(f"a2_{name}", shape, F32))
        ps = lambda name, shape: ctx.enter_context(nc.psum_tensor(f"a2_{name}_ps", shape, F32))
        sem = lambda name: core.keep(nc.semaphore(f"a2_{name}"))
        qk_all = sb("qk_all", [P, 2, TOK])
        v_all = sb("v_all", [HALF, BATCH * 2 * P])
        v_w = sb("v_w", [P, P])
        o_w = sb("o_w", [P, P])
        log_decay = sb("log_decay", [P, HEADS])
        decay = sb("decay", [HALF, HEADS, 2, SEQ])
        decay_made, w_ps_made = sem("decay_made"), sem("w_ps_made")

        with ExitStack() as early:
            w_ps = early.enter_context(nc.psum_tensor("a2_w_ps", [P, 2, P], F32))
            with nc.Block() as block:
                @block.tensor
                def _(pe):
                    pe.matmul(w_ps[:, 0], W["a2_basis"][:], W["a2_vc"][:], start=True, stop=True)
                    pe.matmul(w_ps[:, 1], W["a2_oc"][:], W["a2_basis"][:], start=True, stop=True).then_inc(w_ps_made, 1)

                @block.scalar
                def _(act):
                    act.activation(log_decay[:], W["a2_decay"][:], ACT.Exp, scale=-1.0).then_inc(decay_made, 1)
                    act.wait_ge(decay_made, 3)
                    act.activation(log_decay[:], log_decay[:], ACT.Ln).then_inc(decay_made, 1)
                    act.wait_ge(decay_made, 4)
                    for h in range(HEADS):
                        a = act.activation(decay[:, h], W["a2_distance"][:], ACT.Exp, scale=log_decay[0:HALF, h:h + 1])
                    a.then_inc(decay_made, 1)

                @block.vector
                def _(ve):
                    ve.wait_ge(w_ps_made, 1)
                    ve.tensor_copy(v_w[:], w_ps[:, 0])
                    ve.tensor_scalar(o_w[:], w_ps[:, 1], W["a2_out_scale"][:, 0:1], None, ALU.mult)
                    ve.wait_ge(decay_made, 1)
                    ve.tensor_scalar(log_decay[:], log_decay[:], 1.0, None, ALU.add).then_inc(decay_made, 1)
                    ve.wait_ge(decay_made, 2)
                    ve.reciprocal(log_decay[:], log_decay[:]).then_inc(decay_made, 1)
                    ve.wait_ge(decay_made, 5)
                    ve.tensor_tensor(decay[:], decay[:], W["a2_later"][:].unsqueeze(1).broadcast_to([HALF, HEADS, 2, SEQ]),
                                     ALU.mult).then_inc(decay_made, 1)
                    ve.wait_ge(decay_made, 6)

        unit_heads(nc, core, qk_all, v_all, v_w)

        qkx = [sb(f"qkx{s}", [P, 2, PADSEQ]) for s in S2]
        vx = [sb(f"vx{s}", [HALF, 2, P]) for s in S2]
        weight = [sb(f"weight{s}", [HALF, HEADS, 2, SEQ]) for s in S2]
        got = [sb(f"got{s}", [P, SEQ]) for s in S2]
        s_ps = ps("s", [P, HEADS, 512])
        o_ps = [ps(f"o{s}", [P, 512]) for s in S2]
        qk_fixed, v_fixed, s_made, weight_made, got_made, got_sb, y_made, h_made = (
            sem(n) for n in ("qk_fixed", "v_fixed", "s_made", "weight_made", "got_made", "got_sb", "y_made", "h_made"))

        def pairs(eng, body):
            body(0, None)
            with eng.Fori(1, PAIRS) as i:
                body(i, eng.snap(i - 1))
            body(None, PAIRS - 1)

        with nc.Block() as block:
            @block.gpsimd
            def _(pool):
                for s in S2:
                    pool.memset(qkx[s][:], 0.0).then_inc(qk_fixed, 1)
                pool.wait_ge(qk_fixed, SLOTS)
                with pool.Fori(0, PAIRS) as i:
                    for s in S2:
                        b = pool.snap(SLOTS * i + s)
                        pool.wait_ge(s_made, pool.snap(2 * b + 2))
                        pool.tensor_copy(qkx[s][:, :, 0:SEQ], qk_all[:, :, ds(b * SEQ, SEQ)]).then_inc(qk_fixed, 1)
                        pool.wait_ge(got_made, freed(b))
                        pool.tensor_copy(vx[s][:].rearrange("p f e -> p (f e)"), v_all[:, ds(b * 2 * P, 2 * P)]).then_inc(v_fixed, 1)

            @block.tensor
            def _(pe):
                def score(i, s):
                    b = pe.snap(SLOTS * i + s)
                    pe.wait_ge(qk_fixed, made(b))
                    for two in range(2):
                        pe.wait_ge(weight_made, pe.snap(2 * b + (two + 1)))
                        for f in range(2):
                            for h in (2 * two, 2 * two + 1):
                                rows = slice(h * HD, (h + 1) * HD)
                                mm = pe.matmul(s_ps[0:HALF, h, f * SEQ:(f + 1) * SEQ], qkx[s][rows, 1, f * HALF:(f + 1) * HALF],
                                               qkx[s][rows, 0, 0:SEQ], start=True, stop=True)
                        mm.then_inc(s_made, 1)

                def retrieve(i, s):
                    b = pe.snap(SLOTS * i + s)
                    pe.wait_ge(weight_made, pe.snap(2 * b + 4))
                    pe.wait_ge(v_fixed, b + 1)
                    pe.wait_ge(h_made, freed(b))
                    for f in range(2):
                        for h in range(HEADS):
                            rows = slice(h * HD, (h + 1) * HD)
                            mm = pe.matmul(o_ps[s][rows, 0:SEQ], vx[s][:, f, rows], weight[s][:, h, f], start=(f == 0), stop=(f == 1))
                    mm.then_inc(got_made, 1)

                def product(i, s):
                    b = pe.snap(SLOTS * i + s)
                    pe.wait_ge(got_sb, b + 1)
                    pe.matmul(o_ps[s][:, PADSEQ:PADSEQ + SEQ], o_w[:], got[s][:], start=True, stop=True).then_inc(y_made, 1)

                def body(i, before):
                    if i is not None:
                        score(i, 0)
                    if before is not None:
                        product(before, 0)
                        retrieve(before, 1)
                    if i is not None:
                        score(i, 1)
                    if before is not None:
                        product(before, 1)
                    if i is not None:
                        retrieve(i, 0)

                pairs(pe, body)

            @block.scalar
            def _(act):
                with act.Fori(0, PAIRS) as i:
                    for s in S2:
                        b = act.snap(SLOTS * i + s)
                        act.wait_ge(got_made, made(b))
                        act.activation(got[s][:], o_ps[s][:, 0:SEQ], ACT.Copy).then_inc(got_sb, 1)

            @block.vector
            def _(ve):
                def weigh(i, s):
                    b = ve.snap(SLOTS * i + s)
                    ve.wait_ge(got_made, freed(b))
                    for two in range(2):
                        heads = slice(2 * two, 2 * two + 2)
                        ve.wait_ge(s_made, ve.snap(2 * b + (two + 5)))
                        ve.tensor_tensor(weight[s][:, heads].rearrange("p h f q -> p h (f q)"), s_ps[0:HALF, heads, 0:2 * SEQ],
                                         decay[:, heads].rearrange("p h f q -> p h (f q)"), ALU.mult).then_inc(weight_made, 1)

                def add(i, s):
                    b = ve.snap(SLOTS * i + s)
                    ve.wait_ge(y_made, b + 1)
                    h_b = core.h[:, ds(b * SEQ, SEQ)]
                    ve.tensor_tensor(h_b, h_b, o_ps[s][:, PADSEQ:PADSEQ + SEQ], ALU.add).then_inc(h_made, 1)

                def body(i, before):
                    for s in S2:
                        if i is not None:
                            weigh(i, s)
                        if before is not None:
                            add(before, s)

                ve.sem_inc(weight_made, 2)
                ve.sem_inc(s_made, 2 * SLOTS)
                for c in (h_made, got_made):
                    ve.sem_inc(c, SLOTS)
                pairs(ve, body)





def wide_attention(nc, core):
    HD, G, TILES, R, QW = 64, 4, 3, 96, 144
    ROWS = TILES * R
    PAIRS = BATCH // SLOTS
    INNER = G * P
    SCALE = float(HD) ** -0.5
    W = core.w
    S2 = range(SLOTS)
    with ExitStack() as ctx:
        sb = lambda name, shape: ctx.enter_context(nc.sbuf_tensor(f"a3_{name}", shape, F32))
        ps = lambda name, shape: ctx.enter_context(nc.psum_tensor(f"a3_{name}_ps", shape, F32))
        sem = lambda name: core.keep(nc.semaphore(f"a3_{name}"))
        xs = [sb(f"xs{s}", [P, PADSEQ]) for s in S2]
        qs = [sb(f"qs{s}", [P, SEQ]) for s in S2]
        kt = [sb(f"kt{s}", [P, SEQ]) for s in S2]
        qbd = [sb(f"qbd{s}", [P, ROWS]) for s in S2]
        vs = [sb(f"vs{s}", [HALF, 2, INNER]) for s in S2]
        prob = [[sb(f"prob{s}{par}", [R, TILES, PADSEQ]) for par in range(2)] for s in S2]
        negmax = [[sb(f"negmax{s}{par}", [R, TILES]) for par in range(2)] for s in S2]
        rsum = [[sb(f"rsum{s}{par}", [R, TILES]) for par in range(2)] for s in S2]
        rinv = [[sb(f"rinv{s}{par}", [R, TILES]) for par in range(2)] for s in S2]
        pt = [sb(f"pt{s}", [HALF, 2, ROWS]) for s in S2]
        oc = [sb(f"oc{s}", [P, G, SEQ]) for s in S2]
        qk_ps = [ps(f"qk{s}", [P, 512]) for s in S2]
        vo_ps = [ps(f"vo{s}", [P, 512]) for s in S2]
        s_ps = [ps(f"s{s}", [P, 512]) for s in S2]
        pt_ps = [ps(f"pt{f}", [P, 512]) for f in range(2)]
        first, second = (slice(n * PADSEQ, n * PADSEQ + SEQ) for n in range(2))
        x_made, half_made, v_made, v0_sb, v1_sb, y_made, h_made = (
            sem(n) for n in ("x_made", "half_made", "v_made", "v0_sb", "v1_sb", "y_made", "h_made"))
        qk_made, q_sb, k_sb, qbd_made, s_made, max_made, exp_made, rsum_made, prob_made, pt_made, pt0_sb, pt1_sb, o_made, oc_made = (
            sem(n) for n in ("qk_made", "q_sb", "k_sb", "qbd_made", "s_made", "max_made", "exp_made", "rsum_made",
                             "prob_made", "pt_made", "pt0_sb", "pt1_sb", "o_made", "oc_made"))
        set_up, ready = core.set_up, core.ready_after(8)
        scores = lambda s: s_ps[s][0:R, 0:TILES * SEQ].rearrange("p (t k) -> p t k", k=SEQ)

        def step(i, g, s):
            return SLOTS * G * i + (SLOTS * g + s)

        def pairs(eng, body):
            body(0, None)
            with eng.Fori(1, PAIRS) as i:
                body(i, eng.snap(i - 1))
            body(None, PAIRS - 1)

        with nc.Block() as block:
            @block.gpsimd
            def _(pool):
                def spread_queries(i, g):
                    for s in S2:
                        j = pool.snap(step(i, g, s))
                        pool.wait_ge(q_sb, j + 1)
                        pool.wait_ge(s_made, freed(j))
                        pool.tensor_tensor(qbd[s][:].rearrange("p (h q) -> p h q", q=QW)[:, :, 0:SEQ],
                                           qs[s][:].unsqueeze(1).broadcast_to([P, 2, SEQ]),
                                           W["hmask64"][:].unsqueeze(2).broadcast_to([P, 2, SEQ]),
                                           ALU.mult).then_inc(qbd_made, 1)

                for s in S2:
                    pool.memset(qbd[s][:], 0.0).then_inc(set_up, 1)
                    for par in range(2):
                        pool.memset(prob[s][par][:], 0.0).then_inc(set_up, 1)
                    pool.memset(xs[s][:], 0.0).then_inc(set_up, 1)
                pool.wait_ge(set_up, ready)
                with pool.Fori(0, PAIRS) as i:
                    for s in S2:
                        b = pool.snap(SLOTS * i + s)
                        pool.wait_ge(qk_made, pool.snap(SLOTS * G * i + (s + 1)))
                        pool.tensor_copy(xs[s][:, 0:SEQ], core.normed[:, ds(b * PADSEQ, SEQ)]).then_inc(x_made, 1)
                    spread_queries(i, 0)
                    for s in S2:
                        b = pool.snap(SLOTS * i + s)
                        h_b = core.h[:, ds(b * SEQ, SEQ)]
                        pool.tensor_tensor(h_b, h_b, core.normed[:, ds(b * PADSEQ, SEQ)], ALU.add).then_inc(half_made, 1)
                    for g in range(G):
                        if g + 1 < G:
                            spread_queries(i, g + 1)
                        for s in S2:
                            j = pool.snap(step(i, g, s))
                            pr = prob[s][g % 2]
                            pool.wait_ge(rsum_made, j + 1)
                            pool.tensor_tensor(pr[:, :, 0:SEQ], pr[:, :, 0:SEQ],
                                               rinv[s][g % 2][:].unsqueeze(2).broadcast_to([R, TILES, SEQ]),
                                               ALU.mult).then_inc(prob_made, 1)

            @block.tensor
            def _(pe):
                def projections(i, g, s):
                    j = pe.snap(step(i, g, s))
                    if g == 0:
                        pe.wait_ge(x_made, pe.snap(SLOTS * i + (s + 1)))
                    pe.wait_ge(k_sb, freed(j))
                    c = slice(g * P, (g + 1) * P)
                    pe.matmul(qk_ps[s][:, first], W["a3_wq"][:, c], xs[s][:, 0:SEQ], start=True, stop=True)
                    pe.matmul(qk_ps[s][:, second], W["a3_wk"][:, c], xs[s][:, 0:SEQ], start=True, stop=True).then_inc(qk_made, 1)

                def score(i, g, s):
                    j = pe.snap(step(i, g, s))
                    pe.wait_ge(k_sb, made(j))
                    pe.wait_ge(qbd_made, j + 1)
                    pe.wait_ge(exp_made, freed(j))
                    for t in range(TILES):
                        mm = pe.matmul(scores(s)[:, t], qbd[s][:, t * R:(t + 1) * R], kt[s][:], start=True, stop=True)
                    mm.then_inc(s_made, 1)

                def transposes(i, g, s):
                    j = pe.snap(step(i, g, s))
                    pe.wait_ge(prob_made, j + 1)
                    for f, emptied in ((0, pt0_sb), (1, pt1_sb)):
                        pe.wait_ge(emptied, j + 1)
                        for t in range(TILES):
                            mm = pe.transpose(pt_ps[f][0:HALF, t * R:(t + 1) * R],
                                              prob[s][g % 2][:, t, f * HALF:(f + 1) * HALF], W["ident"][0:R, 0:R])
                        mm.then_inc(pt_made, 1)

                def output(i, g, s):
                    j = pe.snap(step(i, g, s))
                    if g == 0 and s == 0:
                        pe.wait_ge(v0_sb, pe.snap(SLOTS * i + (SLOTS + 1)))
                        pe.wait_ge(v1_sb, pe.snap(SLOTS * i + (SLOTS + 1)))
                    pe.wait_ge(pt0_sb, j + 2)
                    pe.wait_ge(pt1_sb, j + 2)
                    pe.wait_ge(oc_made, freed(j))
                    for f in range(2):
                        for h in range(2):
                            d0 = g * P + h * HD
                            mm = pe.matmul(vo_ps[s][h * HD:(h + 1) * HD, first], vs[s][:, f, d0:d0 + HD],
                                           pt[s][:, f, h * QW:h * QW + SEQ], start=(f == 0), stop=(f == 1))
                    mm.then_inc(o_made, 1)

                def values(i, s):
                    b = pe.snap(SLOTS * i + s)
                    if s == 0:
                        pe.wait_ge(h_made, pe.snap(SLOTS * i + SLOTS))
                    pe.wait_ge(v0_sb, b + 1)
                    pe.wait_ge(v1_sb, b + 1)
                    for f in range(2):
                        mm = pe.matmul(vo_ps[f][0:HALF], xs[s][:, f * HALF:(f + 1) * HALF], W["a3_wv"][:],
                                       start=True, stop=True)
                    mm.then_inc(v_made, 1)

                def product(i, s):
                    j = pe.snap(step(i, G - 1, s))
                    pe.wait_ge(oc_made, made(j))
                    for g in range(G):
                        mm = pe.matmul(vo_ps[s][:, second], W["a3_wo"][:, g], oc[s][:, g], start=(g == 0), stop=(g == G - 1))
                    mm.then_inc(y_made, 1)

                def body(i, before):
                    for s in S2:
                        if i is not None:
                            projections(i, 0, s)
                        if before is not None:
                            transposes(before, G - 1, s)
                    for s in S2:
                        if before is not None:
                            output(before, G - 1, s)
                    for s in S2:
                        if i is not None:
                            score(i, 0, s)
                    for s in S2:
                        if i is not None:
                            projections(i, 1, s)
                        if before is not None:
                            product(before, s)
                    if i is None:
                        return
                    values(i, 0)
                    score(i, 1, 0)
                    values(i, 1)
                    score(i, 1, 1)
                    for g in range(1, G):
                        for s in S2:
                            if g + 1 < G:
                                projections(i, g + 1, s)
                            transposes(i, g - 1, s)
                        for s in S2:
                            output(i, g - 1, s)
                        if g + 1 < G:
                            for s in S2:
                                score(i, g + 1, s)

                pe.wait_ge(set_up, ready)
                pairs(pe, body)

            @block.scalar
            def _(act):
                def leave_qk(i, g, s):
                    j = act.snap(step(i, g, s))
                    act.wait_ge(qk_made, made(j))
                    act.wait_ge(s_made, freed(j))
                    act.activation(qs[s][:], qk_ps[s][:, first], ACT.Copy, scale=SCALE).then_inc(q_sb, 1)
                    act.activation(kt[s][:], qk_ps[s][:, second], ACT.Copy).then_inc(k_sb, 1)

                def exponentials(i, g, s):
                    j = act.snap(step(i, g, s))
                    act.wait_ge(max_made, j + 1)
                    act.wait_ge(pt_made, 2 * j + 2)
                    for t in range(TILES):
                        a = act.activation(prob[s][g % 2][:, t, 0:SEQ], scores(s)[:, t], ACT.Exp, bias=negmax[s][g % 2][:, t:t + 1],
                                           accum_out=rsum[s][g % 2][:, t:t + 1])
                    a.then_inc(exp_made, 1)

                def leave_half_0(i, g, s):
                    j = act.snap(step(i, g, s))
                    act.wait_ge(pt_made, 2 * j + (1 + 4 * SLOTS))
                    act.wait_ge(o_made, freed(j))
                    act.activation(pt[s][:, 0], pt_ps[0][0:HALF, 0:ROWS], ACT.Copy).then_inc(pt0_sb, 1)

                def body(i, before):
                    for s in S2:
                        if i is not None:
                            leave_qk(i, 0, s)
                        if before is not None:
                            leave_half_0(before, G - 1, s)
                    if i is None:
                        return
                    for s in S2:
                        exponentials(i, 0, s)
                    for s in S2:
                        leave_qk(i, 1, s)
                    for s in S2:
                        b = act.snap(SLOTS * i + s)
                        act.wait_ge(v_made, b + 1)
                        act.activation(vs[s][:, 0], vo_ps[0][0:HALF], ACT.Copy).then_inc(v0_sb, 1)
                        exponentials(i, 1, s)
                    for g in range(1, G):
                        for s in S2:
                            if g > 1:
                                exponentials(i, g, s)
                            leave_half_0(i, g - 1, s)
                            if g + 1 < G:
                                leave_qk(i, g + 1, s)

                act.wait_ge(set_up, ready)
                pairs(act, body)

            @block.vector
            def _(ve):
                def row_max(i, g, s):
                    j = ve.snap(step(i, g, s))
                    ve.wait_ge(s_made, made(j))
                    ve.tensor_reduce(negmax[s][g % 2][:], scores(s), AX.X, ALU.max, negate=True).then_inc(max_made, 1)

                def row_sum(i, g, s):
                    j = ve.snap(step(i, g, s))
                    ve.wait_ge(exp_made, made(j))
                    ve.reciprocal(rinv[s][g % 2][:], rsum[s][g % 2][:]).then_inc(rsum_made, 1)

                def leave_half_1(i, g, s):
                    j = ve.snap(step(i, g, s))
                    ve.wait_ge(pt_made, 2 * j + (2 + 4 * SLOTS))
                    ve.wait_ge(o_made, freed(j))
                    ve.tensor_copy(pt[s][:, 1], pt_ps[1][0:HALF, 0:ROWS]).then_inc(pt1_sb, 1)

                def leave_output(i, g, s):
                    j = ve.snap(step(i, g, s))
                    ve.wait_ge(o_made, made(j))
                    ve.tensor_copy(oc[s][:, g], vo_ps[s][:, first]).then_inc(oc_made, 1)

                def body(i, before):
                    if before is not None:
                        for s in S2:
                            leave_half_1(before, G - 1, s)
                        for s in S2:
                            leave_output(before, G - 1, s)
                    if i is not None:
                        for s in S2:
                            row_max(i, 0, s)
                        for s in S2:
                            row_sum(i, 0, s)
                    if before is not None:
                        for s in S2:
                            b = ve.snap(SLOTS * before + s)
                            h_b = core.h[:, ds(b * SEQ, SEQ)]
                            ve.wait_ge(half_made, b + 1)
                            ve.wait_ge(y_made, b + 1)
                            ve.tensor_tensor(h_b, h_b, vo_ps[s][:, second], ALU.add).then_inc(h_made, 1)
                    if i is None:
                        return
                    for s in S2:
                        b = ve.snap(SLOTS * i + s)
                        ve.wait_ge(v_made, b + 1)
                        ve.tensor_copy(vs[s][:, 1], vo_ps[1][0:HALF]).then_inc(v1_sb, 1)
                        row_max(i, 1, s)
                    for g in range(1, G):
                        leave_half_1(i, g - 1, 0)
                        for s in S2:
                            row_sum(i, g, s)
                        leave_half_1(i, g - 1, 1)
                        for s in S2:
                            leave_output(i, g - 1, s)
                        if g + 1 < G:
                            for s in S2:
                                row_max(i, g + 1, s)

                ve.sem_inc(exp_made, SLOTS)
                ve.sem_inc(pt_made, 4 * SLOTS)
                for c in (pt0_sb, pt1_sb, v0_sb, v1_sb):
                    ve.sem_inc(c, 1)
                for c in (qk_made, h_made, k_sb, s_made, oc_made, o_made):
                    ve.sem_inc(c, SLOTS)
                ve.wait_ge(set_up, ready)
                pairs(ve, body)


def gated_expert(nc, core):
    EXPERTS = 16
    W = core.w
    S2 = range(SLOTS)
    with ExitStack() as ctx:
        sb = lambda name, shape, dt=F32: ctx.enter_context(nc.sbuf_tensor(f"f3_{name}", shape, dt))
        ps = lambda name, shape: ctx.enter_context(nc.psum_tensor(f"f3_{name}_ps", shape, F32))
        sem = lambda name: core.keep(nc.semaphore(f"f3_{name}"))
        mean = sb("mean", [P, BATCH])
        ones = sb("ones", [BATCH, P])
        logit = sb("logit", [BATCH, EXPERTS])
        ranked = sb("ranked", [BATCH, 8])
        which = sb("which", [BATCH, 8], U32)
        neg_top = sb("neg_top", [BATCH, 1])
        term = sb("term", [BATCH, EXPERTS])
        total = sb("total", [BATCH, 1])
        gate = sb("gate", [BATCH, 1])
        which_f = sb("which_f", [BATCH, 1])
        chosen = sb("chosen", [BATCH, EXPERTS])
        gate_diag = sb("gate_diag", [BATCH, BATCH])
        chosen_t = sb("chosen_t", [EXPERTS, BATCH])
        which_row = sb("which_row", [1, BATCH], I32)
        gates = sb("gates", [P, BATCH])
        biases = sb("biases", [P, BATCH])
        w_sel = [sb(f"w_sel{s}", [P, P]) for s in S2]
        small_ps = ps("small", [P, 512])
        y_ps = [ps(f"y{s}", [P, 512]) for s in S2]
        v, pe_, a_ = (sem(n) for n in ("route", "route_pe", "route_act"))
        w_made, y_made, h_made = (sem(n) for n in ("w_made", "y_made", "h_made"))
        res = core.h[:, 0:TOK].rearrange("p (b n) -> p b n", n=SEQ)

        with nc.Block() as block:
            @block.tensor
            def _(pe):
                pe.wait_ge(v, 3)
                pe.matmul(small_ps[0:BATCH, 0:EXPERTS], mean[:], W["f3_wg"][:], start=True, stop=True).then_inc(pe_, 1)
                pe.wait_ge(v, 11)
                pe.transpose(small_ps[0:EXPERTS, 32:32 + BATCH], chosen[:], W["ident"][0:BATCH, 0:BATCH])
                pe.transpose(small_ps[0:1, 64:64 + BATCH], which_f[:], W["ident"][0:BATCH, 0:BATCH])
                pe.matmul(small_ps[:, 96:96 + BATCH], ones[:], gate_diag[:], start=True, stop=True).then_inc(pe_, 1)
                pe.wait_ge(v, 14)
                pe.matmul(small_ps[:, 128:128 + BATCH], W["f3_be"][:], chosen_t[:], start=True, stop=True).then_inc(pe_, 1)
                with pe.Fori(0, BATCH // SLOTS) as i:
                    for s in S2:
                        b = pe.snap(SLOTS * i + s)
                        pe.wait_ge(w_made, b + 1)
                        pe.wait_ge(h_made, freed(b))
                        pe.matmul(y_ps[s][:, 0:SEQ], w_sel[s][:], core.normed[:, ds(b * SEQ, SEQ)],
                                  start=True, stop=True).then_inc(y_made, 1)

            @block.scalar
            def _(act):
                act.wait_ge(v, 7)
                act.activation(term[:], logit[:], ACT.Exp, bias=neg_top[:, 0:1], accum_out=total[:, 0:1]).then_inc(a_, 1)

            @block.gpsimd
            def _(pool):
                pool.wait_ge(v, 13)
                with pool.Fori(0, BATCH // SLOTS) as i:
                    for s in S2:
                        b = pool.snap(SLOTS * i + s)
                        e = pool.value_load(which_row[0:1, ds(b, 1)], min_val=0, max_val=EXPERTS - 1)
                        pool.wait_ge(y_made, freed(b))
                        pool.tensor_tensor(w_sel[s][:], W["f3_we"][:, ds(e * P, P)],
                                           gates[:, ds(b, 1)].broadcast_to([P, P]), ALU.mult).then_inc(w_made, 1)

            @block.vector
            def _(ve):
                ve.sem_inc(y_made, SLOTS)
                ve.sem_inc(h_made, SLOTS)
                ve.memset(ones[:], 1.0).then_inc(v, 1)
                ve.tensor_reduce(mean[:], core.normed[:, 0:TOK].rearrange("p (b n) -> p b n", n=SEQ), AX.X, ALU.add).then_inc(v, 1)
                ve.wait_ge(v, 2)
                ve.tensor_scalar(mean[:], mean[:], 1.0 / SEQ, None, ALU.mult).then_inc(v, 1)
                ve.wait_ge(pe_, 1)
                ve.tensor_tensor(logit[:], small_ps[0:BATCH, 0:EXPERTS], W["f3_bg"][:], ALU.add).then_inc(v, 1)
                ve.wait_ge(v, 4)
                ve.max(ranked[:], logit[:]).then_inc(v, 1)
                ve.wait_ge(v, 5)
                ve.max_index(which[:], ranked[:], logit[:]).then_inc(v, 1)
                ve.tensor_scalar(neg_top[:], ranked[:, 0:1], -1.0, None, ALU.mult).then_inc(v, 1)
                ve.wait_ge(v, 6)
                ve.tensor_copy(which_f[:], which[:, 0:1]).then_inc(v, 1)
                ve.wait_ge(a_, 1)
                ve.reciprocal(gate[:], total[:]).then_inc(v, 1)
                ve.wait_ge(v, 9)
                ve.tensor_scalar(chosen[:], W["f3_numbers"][:], which_f[:, 0:1], gate[:, 0:1], ALU.is_equal, ALU.mult).then_inc(v, 1)
                ve.tensor_scalar(gate_diag[:], W["ident"][0:BATCH, 0:BATCH], gate[:, 0:1], None, ALU.mult).then_inc(v, 1)
                ve.wait_ge(pe_, 2)
                ve.tensor_copy(gates[:], small_ps[:, 96:96 + BATCH]).then_inc(v, 1)
                ve.tensor_copy(which_row[:], small_ps[0:1, 64:64 + BATCH]).then_inc(v, 1)
                ve.tensor_copy(chosen_t[:], small_ps[0:EXPERTS, 32:32 + BATCH]).then_inc(v, 1)
                ve.wait_ge(pe_, 3)
                ve.tensor_copy(biases[:], small_ps[:, 128:128 + BATCH]).then_inc(v, 1)
                ve.wait_ge(v, 15)
                ve.tensor_tensor(res, res, biases[:].unsqueeze(2).broadcast_to([P, BATCH, SEQ]), ALU.add).then_inc(v, 1)
                ve.wait_ge(v, 16)
                with ve.Fori(0, BATCH // SLOTS) as i:
                    for s in S2:
                        b = ve.snap(SLOTS * i + s)
                        ve.wait_ge(y_made, made(b))
                        h_b = core.h[:, ds(b * SEQ, SEQ)]
                        ve.tensor_tensor(h_b, h_b, y_ps[s][:, 0:SEQ], ALU.add).then_inc(h_made, 1)


def store_output(nc, core, out):
    with nc.semaphore("stored") as stored, nc.Block() as block:
        @block.sync
        def _(sp):
            for q in range(4):
                sp.dma_start(out[:, q * TOK // 4:(q + 1) * TOK // 4], core.h[:, q * TOK // 4:(q + 1) * TOK // 4]).then_inc(stored, 16)
            sp.wait_ge(stored, 64)


def build(nc, dram, shapes, out, stop=8):
    with ExitStack() as ctx:
        core = Core()
        core.keep = ctx.enter_context
        core.norms = 0
        core.norm_sems = [core.keep(nc.semaphore("ln_" + n)) for n in
                          ("mean_made", "cent_made", "sq_act", "sq_pool", "var_made", "std_made", "rstd_made", "spread_made", "normed_made")]
        core.h = ctx.enter_context(nc.sbuf_tensor("h", [P, TOKPAD], F32))
        core.normed = ctx.enter_context(nc.sbuf_tensor("normed", [P, TOKPAD], F32))
        core.mean_mat = ctx.enter_context(nc.sbuf_tensor("mean_mat", [P, P], F32))
        core.first_row = ctx.enter_context(nc.sbuf_tensor("first_row", [P, P], F32))
        core.eps = ctx.enter_context(nc.sbuf_tensor("eps", [P, 1], F32))
        core.weights_in = ctx.enter_context(nc.semaphore("weights_in"))
        core.weight_names = [n for n in shapes if n not in BLOCK_OWN]
        core.n_weights = len(core.weight_names)
        core.w = {n: ctx.enter_context(nc.sbuf_tensor("w_" + n, list(shapes[n]), F32)) for n in core.weight_names}
        core.projections = 0
        core.project_sems = [core.keep(nc.semaphore("proj_" + n)) for n in
                             ("bqs_made", "conv_step", "x_made", "qk_made", "v_made", "q_sb", "k_sb", "v_sb")]
        core.set_up, core.steps_set_up = core.keep(nc.semaphore("set_up")), 0
        cleared = core.keep(nc.semaphore("cleared"))
        with nc.Block() as block:
            @block.vector
            def _(ve):
                ve.memset(core.mean_mat[:], 1.0 / P)
                ve.memset(core.eps[:], EPS)
                ve.memset(core.first_row[:], 0.0).then_inc(cleared, 1)
                ve.wait_ge(cleared, 1)
                for k in range(4):
                    ve.memset(core.first_row[32 * k:32 * k + 1, :], 1.0)
                ve.memset(core.h[:, TOK:TOKPAD], 0.0)
                ve.memset(core.normed[:], 0.0)
        padded = core.normed[:, 0:BATCH * PADSEQ].rearrange("p (b n) -> p b n", n=PADSEQ)
        padded_out = lambda n: padded[:, ds(2 * n, 2), 0:SEQ]
        flat = core.normed[:, 0:TOK].rearrange("p (b n) -> p b n", n=SEQ)
        flat_out = lambda n: flat[:, ds(2 * n, 2), :]
        tokens_of_patches(nc, core, dram)
        layernorm(nc, core, "a0_ln", padded_out)
        narrow_attention(nc, core, "a0", projected=False, top_k=False, conv=False)
        layernorm(nc, core, "m_ln", flat_out)
        routed_experts(nc, core, dram)
        layernorm(nc, core, "a1_ln", flat_out)
        head_mixing(nc, core)
        window_projection(nc, core)
        layernorm(nc, core, "f1_ln", flat_out)
        trig_ffn(nc, core)
        layernorm(nc, core, "a2_ln", padded_out)
        decay_retrieval(nc, core)
        layernorm(nc, core, "f2_ln", padded_out)
        narrow_attention(nc, core, "f2", projected=True, top_k=True, conv=True)
        layernorm(nc, core, "a3_ln", padded_out)
        wide_attention(nc, core)
        layernorm(nc, core, "f3_ln", flat_out)
        gated_expert(nc, core)
        store_output(nc, core, out)


BLOCK_OWN = {"x", "txt", "w0", "w1", "sw0", "sw1", "eo0", "eo1", "eps0", "eps1", "bias0", "bias1", "w3", "b3", "pe",
             "expert_rows", "expert_ids", "m_w1", "m_w2"}


def lay_out(np, a):
    c = np.ascontiguousarray
    blocks = lambda m: m.reshape(m.shape[0] // P, P, -1).transpose(1, 0, 2)
    col = lambda v: v.reshape(-1, P).T
    x = a["x"].reshape(BATCH, 8, 16, 8, 16).transpose(0, 1, 3, 2, 4).reshape(BATCH * PATCHES, 256)
    pos = np.arange(PATCHES, dtype=np.float32)[:, None]
    div = np.exp(np.arange(0, P, 2, dtype=np.float32) * np.float32(-np.log(10000.0) / P))
    ang = (pos * div).astype(np.float32)
    pe = np.stack([np.sin(ang), np.cos(ang)], axis=-1).reshape(PATCHES, P).astype(np.float32)
    d = {"x": blocks(x.T), "txt": a["txt"].transpose(2, 0, 1), "pe": pe.T}
    for l, name in enumerate(("W1", "W2")):
        t = f"L0_tok_{name}"
        d[f"w{l}"] = blocks(a[t + "_w"].T)
        d[f"sw{l}"] = blocks(a[t + "_sw"].T)
        d[f"eo{l}"] = a[f"L0_tok_eps_out{l + 1}"]
        d[f"eps{l}"] = np.concatenate([col(a[f"L0_tok_eps_in{l + 1}"]), col(a[f"L0_tok_eps_out{l + 1}"])], axis=1)
        d[f"bias{l}"] = np.stack([a[t + "_b"], a[t + "_sb"]], axis=1)
    d["w3"] = a["L0_tok_W3_w"].T
    d["b3"] = a["L0_tok_W3_b"][:, None]
    d["hmask16"] = np.repeat(np.eye(8, dtype=np.float32), 16, axis=0)
    d["ident"] = np.eye(P, dtype=np.float32)
    d["a0_wq"], d["a0_wk"], d["a0_wv"] = a["L0_attn_Wq"].T, a["L0_attn_Wk"].T, a["L0_attn_Wk"].T
    d["a0_bq"], d["a0_bk"], d["a0_bv"] = (a["L0_attn_" + n][:, None] for n in ("bq", "bk", "bk"))
    d["expert_ids"], d["expert_rows"] = a["L0_ffn_expert_indices"].T, a["L0_ffn_expert_weights"].T
    d["m_w1"] = a["L0_ffn_w1"]
    d["m_w2"] = a["L0_ffn_w2"].reshape(8, 4, P, P).transpose(0, 2, 1, 3)
    d["ident"] = np.eye(P, dtype=np.float32)
    d["hmask16"] = np.repeat(np.eye(8, dtype=np.float32), 16, axis=0)
    d["a1_wqkv"], d["wp_b"] = a["L1_attn_w_qkv"].T, a["L1_attn_b_proj"][:, None]
    d["wp_w"] = np.tile(a["L1_attn_w_proj"].reshape(P, 8, 16).transpose(2, 1, 0), (8, 1, 1))
    d["f1_w"], d["f1_b"] = a["L1_ffn_W"].T, a["L1_ffn_B_param"].T
    d["f1_attn_cos"], d["f1_attn_sin"] = a["L1_ffn_attn_cos"].T, a["L1_ffn_attn_sin"].T
    proj = np.stack([a["L1_ffn_proj_cos_w"].T, a["L1_ffn_proj_sin_w"].T])
    d["f1_proj"] = proj.reshape(2, 16, 4, P).transpose(2, 0, 1, 3).reshape(P, P)
    d["a2_basis"], d["a2_vc"], d["a2_oc"] = (a["L2_attn_" + n].T for n in ("basis", "v_coeffs", "o_coeffs"))
    d["a2_wq"], d["a2_wk"] = a["L2_attn_shared_q_w"], a["L2_attn_shared_k_w"]
    d["a2_decay"] = np.broadcast_to(a["L2_attn_decay_logits"], (P, 4))
    d["a2_out_scale"] = np.broadcast_to(a["L2_attn_out_scale"], (P, 1))
    after = (np.arange(71)[:, None, None] + 71 * np.arange(2)[None, :, None]) - np.arange(SEQ)[None, None, :]
    d["a2_distance"] = np.maximum(after - 1, 0).astype(np.float32)
    d["a2_later"] = ((after > 0) & (after - 1 < SEQ)).astype(np.float32)
    d["hmask16"] = np.repeat(np.eye(8, dtype=np.float32), 16, axis=0)
    d["ident"] = np.eye(P, dtype=np.float32)
    for n, m in enumerate("qkv"):
        d["f2_w" + m] = a["L2_ffn_qkv_w"][n * P:(n + 1) * P].T
        d["f2_b" + m] = a["L2_ffn_qkv_b"][n * P:(n + 1) * P, None]
    d["f2_wo"], d["f2_bo"] = a["L2_ffn_wo_w"].T, a["L2_ffn_wo_b"][:, None]
    d["f2_pos_w"], d["f2_pos_b"] = a["L2_ffn_pos_w"][:, 0], a["L2_ffn_pos_b"][:, None]
    d["hmask64"] = np.repeat(np.eye(2, dtype=np.float32), 64, axis=0)
    d["ident"] = np.eye(P, dtype=np.float32)
    d["a3_wq"], d["a3_wk"], d["a3_wv"] = (a["L3_attn_" + n].T for n in ("Wq", "Wk", "Wv"))
    d["a3_wo"] = a["L3_attn_Wo"].T.reshape(4, P, P).transpose(1, 0, 2)
    d["ident"] = np.eye(P, dtype=np.float32)
    d["f3_wg"], d["f3_be"] = a["L3_ffn_Wg"], a["L3_ffn_be"]
    d["f3_bg"] = np.broadcast_to(a["L3_ffn_bg"], (BATCH, 16))
    d["f3_numbers"] = np.broadcast_to(np.arange(16, dtype=np.float32), (BATCH, 16))
    d["f3_we"] = a["L3_ffn_We"].transpose(1, 0, 2).reshape(P, 16 * P)
    return {k: c(v) for k, v in d.items()}


def kernel(**inputs):
    import numpy as _np
    import concourse.bacc as _bacc
    from concourse import mybir as _mybir
    from concourse.bass_utils import run_bass_kernel_spmd as _run

    arrays = lay_out(_np, {k: _np.asarray(v) for k, v in inputs.items()})
    nc = _bacc.Bacc("TRN2", target_bir_lowering=False, num_devices=1)
    dram = {k: nc.dram_tensor("in_" + k, list(v.shape), _mybir.dt.from_np(v.dtype), kind="ExternalInput").ap()
            for k, v in arrays.items()}
    out = nc.dram_tensor("out_h", [P, TOK], _mybir.dt.float32, kind="ExternalOutput").ap()
    build(nc, dram, {k: v.shape for k, v in arrays.items()}, out)
    r = _run(nc, [{"in_" + k: v for k, v in arrays.items()}], core_ids=[0])
    return _np.ascontiguousarray(r.results[0]["out_h"].reshape(P, BATCH, SEQ).transpose(1, 2, 0))
```
